# Optimizing a Trainium2 kernel written in Bass

```python
import numpy as np
import jax
import jax.numpy as jnp

def _softmax(x, axis=-1):
    return jax.nn.softmax(x, axis=axis)

def _gelu(x):
    return jax.nn.gelu(x, approximate=True)

def _silu(x):
    return jax.nn.silu(x)

def _sigmoid(x):
    return jax.nn.sigmoid(x)

def _layernorm(x, axis=-1, eps=1e-05):
    m = jnp.mean(x, axis=axis, keepdims=True)
    v = jnp.var(x, axis=axis, keepdims=True)
    return (x - m) / jnp.sqrt(v + eps)

def _scatter_add(tgt, idx, src, axis=0):
    return tgt.at[idx].add(src)

def _segment_sum(src, seg, n):
    return jax.ops.segment_sum(src, seg, n)
kernel_name = 'mk_gnn_resnorm_d2_gnn_r8_c6dadf'

def setup_inputs(seed: int=0):
    np.random.seed(seed)
    _w = jnp.asarray

    def _rec_inputs():
        import jax
        import jax.numpy as jnp
        _gk = jax.random.key(seed)
        x = -0.000202 + 1 * jax.random.normal(jax.random.fold_in(_gk, 1), (6250, 128), jnp.float32)
        src = jax.random.randint(jax.random.fold_in(_gk, 2), (200000,), 0, 6250, jnp.int32)
        dst = jnp.minimum((6250 * jax.random.uniform(jax.random.fold_in(_gk, 3), (200000,)) ** 2.0).astype(jnp.int32), 49999)
        _o = jnp.argsort(dst, stable=True)
        src = src[_o]
        dst = dst[_o]
        edge_weight = jax.random.uniform(jax.random.fold_in(_gk, 12), (200000,), jnp.float32, 0.0, 0.999998)
        return (x, src, dst, edge_weight)
    x, src, dst, edge_weight = _rec_inputs()

    def _L0_gnn_setup():
        import jax, jax.numpy as jnp
        import numpy as np
        N = 6250
        E = 75000
        F = 128
        H = 8
        C = 16
        D = H * C
        NEF = 4
        LN_EPS = 1e-05
        LRELU_SLOPE = 0.2

        def _layer_norm(h, g, b):
            mu = jnp.mean(h, axis=-1, keepdims=True)
            var = jnp.var(h, axis=-1, keepdims=True)
            return (h - mu) * jax.lax.rsqrt(var + LN_EPS) * g + b

        def _edge_features(x, src, dst):
            xi, xj = (x[src], x[dst])
            return jnp.stack([jnp.sum(xi * xj, -1), jnp.sum((xi - xj) ** 2, -1), jnp.sum(xi * xi, -1), jnp.sum(xj * xj, -1)], axis=-1)

        def _gat_conv(x, src, dst, edge_attr, lin_w, att_src, att_dst, att_edge, lin_edge_w, bias):
            xs = (x @ lin_w.T).reshape(N, H, C)
            a_src = jnp.sum(xs * att_src, -1)
            a_dst = jnp.sum(xs * att_dst, -1)
            e = (edge_attr @ lin_edge_w.T).reshape(-1, H, C)
            a_edge = jnp.sum(e * att_edge, -1)
            alpha = a_src[src] + a_dst[dst] + a_edge
            alpha = jnp.where(alpha > 0, alpha, LRELU_SLOPE * alpha)
            m = jax.ops.segment_max(alpha, dst, num_segments=N)
            alpha = jnp.exp(alpha - m[dst])
            denom = jax.ops.segment_sum(alpha, dst, num_segments=N)
            alpha = alpha / (denom[dst] + 1e-16)
            msg = xs[src] * alpha[..., None]
            out = jax.ops.segment_sum(msg, dst, num_segments=N)
            return out.reshape(N, D) + bias
        key = jax.random.key(seed)
        ks = jax.random.split(key, 32)

        def nrm(k, shp, s=0.05):
            return jax.random.normal(k, shp, dtype=jnp.float32) * s
        return {'x': jax.random.normal(ks[0], (N, F), dtype=jnp.float32), 'edge_index': jax.random.randint(ks[1], (2, E), 0, N), 'enc_w1': nrm(ks[2], (C, NEF)), 'enc_b1': jnp.zeros((C,), jnp.float32), 'enc_w2': nrm(ks[3], (H, C)), 'enc_b2': jnp.zeros((H,), jnp.float32), 'in_w': nrm(ks[4], (D, F)), 'in_b': jnp.zeros((D,), jnp.float32), 'lin_w1': nrm(ks[5], (D, F)), 'att_src1': nrm(ks[6], (H, C)), 'att_dst1': nrm(ks[7], (H, C)), 'att_edge1': nrm(ks[8], (H, C)), 'lin_edge_w1': nrm(ks[9], (D, H)), 'bias1': jnp.zeros((D,), jnp.float32), 'lin_w2': nrm(ks[10], (D, D)), 'att_src2': nrm(ks[11], (H, C)), 'att_dst2': nrm(ks[12], (H, C)), 'att_edge2': nrm(ks[13], (H, C)), 'lin_edge_w2': nrm(ks[14], (D, H)), 'bias2': jnp.zeros((D,), jnp.float32), 'g1': jnp.ones((D,), jnp.float32), 'bn1': jnp.zeros((D,), jnp.float32), 'g2': jnp.ones((D,), jnp.float32), 'bn2': jnp.zeros((D,), jnp.float32), 'jk_w': nrm(ks[15], (D, 3 * D)), 'jk_b': jnp.zeros((D,), jnp.float32)}
    _L0_gnn_all = _L0_gnn_setup()
    _L0_gnn_in = {k: v for k, v in _L0_gnn_all.items() if k in ('enc_w1', 'enc_b1', 'enc_w2', 'enc_b2', 'in_w', 'in_b', 'lin_w1', 'att_src1', 'att_dst1', 'att_edge1', 'lin_edge_w1', 'bias1', 'lin_w2', 'att_src2', 'att_dst2', 'att_edge2', 'lin_edge_w2', 'bias2', 'g1', 'bn1', 'g2', 'bn2', 'jk_w', 'jk_b')}
    del _L0_gnn_all

    def _L1_gnn_setup():
        import jax, jax.numpy as jnp
        import numpy as np
        N, E, H = (6250, 100000, 128)
        LN_EPS = 1e-05

        def layer_norm(x, gamma, beta):
            mu = jnp.mean(x, axis=-1, keepdims=True)
            var = jnp.mean((x - mu) ** 2, axis=-1, keepdims=True)
            return (x - mu) * jax.lax.rsqrt(var + LN_EPS) * gamma + beta
        key = jax.random.key(seed)
        ks = jax.random.split(key, 8)
        sc = 1.0 / np.sqrt(2 * H)
        return {'x': jax.random.normal(ks[0], (N, H), dtype=jnp.float32), 'edge_index': jax.random.randint(ks[1], (2, E), 0, N, dtype=jnp.int64), 'edge_weights': jax.random.uniform(ks[2], (E,), dtype=jnp.float32), 'msg_w': jax.random.normal(ks[3], (2 * H, H), dtype=jnp.float32) * sc, 'msg_b': jnp.zeros((H,), jnp.float32), 'msg_g': jnp.ones((H,), jnp.float32), 'msg_beta': jnp.zeros((H,), jnp.float32), 'upd_w': jax.random.normal(ks[4], (2 * H, H), dtype=jnp.float32) * sc, 'upd_b': jnp.zeros((H,), jnp.float32), 'upd_g': jnp.ones((H,), jnp.float32), 'upd_beta': jnp.zeros((H,), jnp.float32), 'gate_w': jax.random.normal(ks[5], (H, 1), dtype=jnp.float32) / np.sqrt(H), 'gate_b': jnp.zeros((1,), jnp.float32)}
    _L1_gnn_all = _L1_gnn_setup()
    _L1_gnn_in = {k: v for k, v in _L1_gnn_all.items() if k in ('msg_w', 'msg_b', 'msg_g', 'msg_beta', 'upd_w', 'upd_b', 'upd_g', 'upd_beta', 'gate_w', 'gate_b')}
    del _L1_gnn_all
    return {'x': x, 'src': src, 'dst': dst, 'edge_weight': edge_weight, 'L0_gnn_enc_w1': _L0_gnn_in['enc_w1'], 'L0_gnn_enc_b1': _L0_gnn_in['enc_b1'], 'L0_gnn_enc_w2': _L0_gnn_in['enc_w2'], 'L0_gnn_enc_b2': _L0_gnn_in['enc_b2'], 'L0_gnn_in_w': _L0_gnn_in['in_w'], 'L0_gnn_in_b': _L0_gnn_in['in_b'], 'L0_gnn_lin_w1': _L0_gnn_in['lin_w1'], 'L0_gnn_att_src1': _L0_gnn_in['att_src1'], 'L0_gnn_att_dst1': _L0_gnn_in['att_dst1'], 'L0_gnn_att_edge1': _L0_gnn_in['att_edge1'], 'L0_gnn_lin_edge_w1': _L0_gnn_in['lin_edge_w1'], 'L0_gnn_bias1': _L0_gnn_in['bias1'], 'L0_gnn_lin_w2': _L0_gnn_in['lin_w2'], 'L0_gnn_att_src2': _L0_gnn_in['att_src2'], 'L0_gnn_att_dst2': _L0_gnn_in['att_dst2'], 'L0_gnn_att_edge2': _L0_gnn_in['att_edge2'], 'L0_gnn_lin_edge_w2': _L0_gnn_in['lin_edge_w2'], 'L0_gnn_bias2': _L0_gnn_in['bias2'], 'L0_gnn_g1': _L0_gnn_in['g1'], 'L0_gnn_bn1': _L0_gnn_in['bn1'], 'L0_gnn_g2': _L0_gnn_in['g2'], 'L0_gnn_bn2': _L0_gnn_in['bn2'], 'L0_gnn_jk_w': _L0_gnn_in['jk_w'], 'L0_gnn_jk_b': _L0_gnn_in['jk_b'], 'L1_gnn_msg_w': _L1_gnn_in['msg_w'], 'L1_gnn_msg_b': _L1_gnn_in['msg_b'], 'L1_gnn_msg_g': _L1_gnn_in['msg_g'], 'L1_gnn_msg_beta': _L1_gnn_in['msg_beta'], 'L1_gnn_upd_w': _L1_gnn_in['upd_w'], 'L1_gnn_upd_b': _L1_gnn_in['upd_b'], 'L1_gnn_upd_g': _L1_gnn_in['upd_g'], 'L1_gnn_upd_beta': _L1_gnn_in['upd_beta'], 'L1_gnn_gate_w': _L1_gnn_in['gate_w'], 'L1_gnn_gate_b': _L1_gnn_in['gate_b']}

def reference(x, src, dst, edge_weight, L0_gnn_enc_w1, L0_gnn_enc_b1, L0_gnn_enc_w2, L0_gnn_enc_b2, L0_gnn_in_w, L0_gnn_in_b, L0_gnn_lin_w1, L0_gnn_att_src1, L0_gnn_att_dst1, L0_gnn_att_edge1, L0_gnn_lin_edge_w1, L0_gnn_bias1, L0_gnn_lin_w2, L0_gnn_att_src2, L0_gnn_att_dst2, L0_gnn_att_edge2, L0_gnn_lin_edge_w2, L0_gnn_bias2, L0_gnn_g1, L0_gnn_bn1, L0_gnn_g2, L0_gnn_bn2, L0_gnn_jk_w, L0_gnn_jk_b, L1_gnn_msg_w, L1_gnn_msg_b, L1_gnn_msg_g, L1_gnn_msg_beta, L1_gnn_upd_w, L1_gnn_upd_b, L1_gnn_upd_g, L1_gnn_upd_beta, L1_gnn_gate_w, L1_gnn_gate_b):
    import jax
    import jax.numpy as jnp

    def _L0_gnn_ref(x, edge_index, enc_w1, enc_b1, enc_w2, enc_b2, in_w, in_b, lin_w1, att_src1, att_dst1, att_edge1, lin_edge_w1, bias1, lin_w2, att_src2, att_dst2, att_edge2, lin_edge_w2, bias2, g1, bn1, g2, bn2, jk_w, jk_b):
        import jax, jax.numpy as jnp
        import numpy as np
        N = 6250
        E = 75000
        F = 128
        H = 8
        C = 16
        D = H * C
        NEF = 4
        LN_EPS = 1e-05
        LRELU_SLOPE = 0.2

        def _layer_norm(h, g, b):
            mu = jnp.mean(h, axis=-1, keepdims=True)
            var = jnp.var(h, axis=-1, keepdims=True)
            return (h - mu) * jax.lax.rsqrt(var + LN_EPS) * g + b

        def _edge_features(x, src, dst):
            xi, xj = (x[src], x[dst])
            return jnp.stack([jnp.sum(xi * xj, -1), jnp.sum((xi - xj) ** 2, -1), jnp.sum(xi * xi, -1), jnp.sum(xj * xj, -1)], axis=-1)

        def _gat_conv(x, src, dst, edge_attr, lin_w, att_src, att_dst, att_edge, lin_edge_w, bias):
            xs = (x @ lin_w.T).reshape(N, H, C)
            a_src = jnp.sum(xs * att_src, -1)
            a_dst = jnp.sum(xs * att_dst, -1)
            e = (edge_attr @ lin_edge_w.T).reshape(-1, H, C)
            a_edge = jnp.sum(e * att_edge, -1)
            alpha = a_src[src] + a_dst[dst] + a_edge
            alpha = jnp.where(alpha > 0, alpha, LRELU_SLOPE * alpha)
            m = jax.ops.segment_max(alpha, dst, num_segments=N)
            alpha = jnp.exp(alpha - m[dst])
            denom = jax.ops.segment_sum(alpha, dst, num_segments=N)
            alpha = alpha / (denom[dst] + 1e-16)
            msg = xs[src] * alpha[..., None]
            out = jax.ops.segment_sum(msg, dst, num_segments=N)
            return out.reshape(N, D) + bias
        src, dst = (edge_index[0], edge_index[1])
        ef = _edge_features(x, src, dst)
        ea = jax.nn.relu(ef @ enc_w1.T + enc_b1) @ enc_w2.T + enc_b2
        loop = jnp.arange(N)
        src_f = jnp.concatenate([src, loop])
        dst_f = jnp.concatenate([dst, loop])
        ea_f = jnp.concatenate([ea, jnp.broadcast_to(jnp.mean(ea, 0), (N, H))])
        h0 = x @ in_w.T + in_b
        h1 = jax.nn.elu(_gat_conv(x, src_f, dst_f, ea_f, lin_w1, att_src1, att_dst1, att_edge1, lin_edge_w1, bias1))
        h1 = _layer_norm(h1 + h0, g1, bn1)
        h2 = jax.nn.elu(_gat_conv(h1, src_f, dst_f, ea_f, lin_w2, att_src2, att_dst2, att_edge2, lin_edge_w2, bias2))
        h2 = _layer_norm(h2 + h1, g2, bn2)
        h = jnp.concatenate([h0, h1, h2], axis=-1)
        return h @ jk_w.T + jk_b

    def _L1_gnn_ref(x, edge_index, edge_weights, msg_w, msg_b, msg_g, msg_beta, upd_w, upd_b, upd_g, upd_beta, gate_w, gate_b):
        import jax, jax.numpy as jnp
        import numpy as np
        N, E, H = (6250, 100000, 128)
        LN_EPS = 1e-05

        def layer_norm(x, gamma, beta):
            mu = jnp.mean(x, axis=-1, keepdims=True)
            var = jnp.mean((x - mu) ** 2, axis=-1, keepdims=True)
            return (x - mu) * jax.lax.rsqrt(var + LN_EPS) * gamma + beta
        num_nodes = x.shape[0]
        src, dst = (edge_index[0], edge_index[1])
        em = jnp.concatenate([x[src], x[dst]], axis=-1)
        em = jax.nn.relu(layer_norm(em @ msg_w + msg_b, msg_g, msg_beta))
        em = em * edge_weights[:, None]
        msgs = jax.ops.segment_sum(em, dst, num_segments=num_nodes)
        counts = jax.ops.segment_sum(jnp.ones((src.shape[0], 1), x.dtype), dst, num_segments=num_nodes)
        valid = (counts > 0).astype(x.dtype)
        messages = msgs / (counts + 1e-08) * valid
        gate = jax.nn.sigmoid(x @ gate_w + gate_b)
        combined = jnp.concatenate([x, messages], axis=-1)
        h_new = jax.nn.relu(layer_norm(combined @ upd_w + upd_b, upd_g, upd_beta))
        return gate * h_new + (1.0 - gate) * x
    edge_index = jnp.stack([src, dst])
    x = _layernorm(x + _L0_gnn_ref(x, edge_index, L0_gnn_enc_w1, L0_gnn_enc_b1, L0_gnn_enc_w2, L0_gnn_enc_b2, L0_gnn_in_w, L0_gnn_in_b, L0_gnn_lin_w1, L0_gnn_att_src1, L0_gnn_att_dst1, L0_gnn_att_edge1, L0_gnn_lin_edge_w1, L0_gnn_bias1, L0_gnn_lin_w2, L0_gnn_att_src2, L0_gnn_att_dst2, L0_gnn_att_edge2, L0_gnn_lin_edge_w2, L0_gnn_bias2, L0_gnn_g1, L0_gnn_bn1, L0_gnn_g2, L0_gnn_bn2, L0_gnn_jk_w, L0_gnn_jk_b), axis=-1)
    x = _layernorm(x + _L1_gnn_ref(x, edge_index, edge_weight, L1_gnn_msg_w, L1_gnn_msg_b, L1_gnn_msg_g, L1_gnn_msg_beta, L1_gnn_upd_w, L1_gnn_upd_b, L1_gnn_upd_g, L1_gnn_upd_beta, L1_gnn_gate_w, L1_gnn_gate_b), axis=-1)
    return x

_drawn_inputs = setup_inputs


def setup_inputs(seed=0):
    import zlib

    import numpy as np

    out = dict(_drawn_inputs(seed))
    spreads = {'L0_gnn_enc_b1': (0.0, 2.0),
     'L0_gnn_enc_b2': (0.0, 2.0),
     'L0_gnn_in_b': (0.0, 0.1),
     'L0_gnn_bias1': (0.0, 0.1),
     'L0_gnn_bias2': (0.0, 0.1),
     'L0_gnn_g1': (1.0, 0.2),
     'L0_gnn_bn1': (0.0, 0.1),
     'L0_gnn_g2': (1.0, 0.2),
     'L0_gnn_bn2': (0.0, 0.1),
     'L0_gnn_jk_b': (0.0, 0.1),
     'L1_gnn_msg_b': (0.0, 0.8),
     'L1_gnn_msg_g': (1.0, 0.6),
     'L1_gnn_msg_beta': (0.0, 0.8),
     'L1_gnn_upd_b': (0.0, 0.571),
     'L1_gnn_upd_g': (1.0, 0.2),
     'L1_gnn_upd_beta': (0.0, 0.303)}
    factors = {'edge_weight': 15.923,
     'L0_gnn_enc_w1': 8.0,
     'L0_gnn_enc_w2': 8.0,
     'L0_gnn_att_src1': 3.255,
     'L0_gnn_att_dst1': 45.157,
     'L0_gnn_att_edge1': 8.0,
     'L0_gnn_lin_edge_w1': 8.0,
     'L0_gnn_att_src2': 8.0,
     'L0_gnn_att_dst2': 64.0,
     'L0_gnn_att_edge2': 8.0,
     'L0_gnn_lin_edge_w2': 8.0}
    for name, (base, spread) in spreads.items():
        noise = np.random.default_rng([zlib.crc32(name.encode()), seed]).standard_normal(out[name].shape)
        drawn = base * np.exp(spread * noise) if base else spread * noise
        out[name] = jnp.asarray(drawn.astype(out[name].dtype))
    for name, factor in factors.items():
        out[name] = (out[name] * factor).astype(out[name].dtype)
    return out
```

```python
import concourse.bass as bass
from concourse import mybir
from contextlib import ExitStack, contextmanager

P = 128
N, E, F = 6250, 200000, 128
H, C = 8, 16
HID = 16
NB = -(-N // P)
NPAD = NB * P
LAST = N - (NB - 1) * P
TILES = -(-E // P)
G = 4
U = 2
CH = P // H
SLOTS = -(-(TILES + NB - 1) // (CH * 1)) * CH
while SLOTS % (G * U):
    SLOTS += CH
KC = SLOTS // CH
TC = KC * P
SC = -(-SLOTS // P)
EROWS = SLOTS - (NB - 1)
BIG = 1e30
EPS = 1e-5
SLOPE = 0.2
ROW1 = F + F + H + 1
ROW2 = F + H
DCOL1 = F + H + 1
AW = F + H + H + 1
RF_ = max(NB * ROW1, SLOTS * H)
REGION = -(-RF_ // 64) * 64

fp32, bf16, i32, i16 = mybir.dt.float32, mybir.dt.bfloat16, mybir.dt.int32, mybir.dt.int16
ALU = mybir.AluOpType
ACT = mybir.ActivationFunctionType
AX = mybir.AxisListType
ET = mybir.EngineType
ENGINES = [ET.Pool, ET.Activation, ET.PE, ET.DVE, ET.SP]


class Relay:

    def __init__(self, sem, by=1):
        self.sem, self.by, self.n = sem, by, 0

    def after(self, *engines):
        for e in engines:
            if self.n:
                e.wait_ge(self.sem, self.n)

    def done(self, instruction):
        instruction.then_inc(self.sem, self.by)
        self.n += self.by

    def step(self, engine, emit):
        self.after(engine)
        self.done(emit())


class Build:

    def __init__(self, nc, ctx):
        self.nc, self.ctx, self.sems, self.used = nc, ctx, ctx, []
        self.pool, self.act, self.pe, self.dve, self.sp = nc.gpsimd, nc.scalar, nc.tensor, nc.vector, nc.sync
        self.tick = {e: self.sem("tick_" + n) for n, e in
                     (("pool", self.pool), ("act", self.act), ("pe", self.pe), ("dve", self.dve), ("sp", self.sp))}

        self.arrived = [self.sem(f"rows_arrived{u}") for u in range(U)]
        self.arrived_before = [0] * U

    def sb(self, name, shape, dt=fp32):
        return self.ctx.enter_context(self.nc.sbuf_tensor(name, shape, dt))

    def dram(self, name, shape, dt=fp32):
        return self.nc.dram_tensor(name, shape, dt, kind="Internal").ap()

    @contextmanager
    def phase(self):
        self.used = []
        with ExitStack() as self.sems:
            yield
            self.barrier()
            for s in self.used:
                self.pool.sem_clear(s)
        self.barrier()

    def sem(self, name):
        s = self.sems.enter_context(self.nc.semaphore(name))
        self.used.append(s)
        return s

    def relay(self, name):
        return Relay(self.sem(name))

    def dmas(self, name):
        return Relay(self.sem(name), 16)

    def loop_wait(self, engine, sem, value):
        engine.wait_ge(sem, value)
        engine.sem_inc(self.tick[engine], 1)

    def barrier(self):
        self.nc.all_engine_barrier()


def table(region, width, at=0):
    return region[:, at:at + NB * width].rearrange("p (b w) -> p b w", w=width)


def rows(dram):
    return dram.rearrange("(b p) w -> p b w", p=P)


def load_weights(K, D):
    nc, pool, pe, dve, sp, act = K.nc, K.pool, K.pe, K.dve, K.sp, K.act
    K.ident = K.sb("ident", [P, P])
    K.iota = K.sb("iota", [P, P])
    K.ones = K.sb("ones", [P, P])
    K.W1 = K.sb("W_node1", [P, F + 2 * H + F])
    K.W2 = K.sb("W_node2", [P, F + 2 * H])
    K.JK = K.sb("W_jk", [P, 3, F])
    K.WM = K.sb("W_msg_upd", [P, 4, F])
    names = ["L0_gnn_bias1", "L0_gnn_g1", "L0_gnn_bn1", "L0_gnn_in_b", "L0_gnn_bias2", "L0_gnn_g2", "L0_gnn_bn2",
             "L0_gnn_jk_b", "L1_gnn_msg_b", "L1_gnn_msg_g", "L1_gnn_msg_beta", "L1_gnn_upd_b", "L1_gnn_upd_g",
             "L1_gnn_upd_beta", "gate_w_row"]
    K.vecs = K.sb("vectors", [P, len(names), F])
    K.vec = {n: K.vecs[:, k, :] for k, n in enumerate(names)}
    K.gate_b = K.sb("gate_b", [P, 1])
    K.Wbd = K.sb("enc_w1_diag", [4 * CH, 2, P])
    K.b1rep = K.sb("enc_b1_rep", [P, 1])
    K.Vbd = K.sb("edge_alpha_diag", [P, 2, 2, P])
    K.Vrep = K.sb("edge_alpha_rep", [P, 2, H])
    K.ccol = K.sb("edge_alpha_const_col", [P, 2])
    K.crow = K.sb("edge_alpha_const_row", [P, 2, H])
    R = K.RA
    att = R[:, 0:6 * H].rearrange("p (m h) -> p m h", h=H)
    lin = R[:, 64:64 + 2 * F].rearrange("p (m f) -> p m f", f=F)
    edge = R[:, 320:320 + 2 * H].rearrange("p (m f) -> p m f", f=H)
    encw2 = R[0:H, 340:340 + HID]
    encb2 = R[0:H, 360:361]
    We = R[0:H, 368:368 + 2 * H].rearrange("p (m f) -> p m f", f=H)
    WeR = R[0:H, 400:400 + 2 * P].rearrange("p (m f) -> p m f", f=P)
    b2R = R[0:H, 660:660 + P]
    V = R[0:HID, 800:800 + 2 * H].rearrange("p (m f) -> p m f", f=H)

    made, loads, folded = K.relay("const_made"), K.dmas("weights_in"), K.relay("folded")
    made.done(pool.memset(K.ident[:, :], 0.0))
    made.done(pool.memset(K.ones[:, :], 1.0))
    made.done(pool.iota(K.iota[:, :], [[1, P]], base=0, channel_multiplier=0, allow_small_or_imprecise_dtypes=True))
    made.step(pool, lambda: pool.affine_select(out=K.ident[:, :], in_=K.ident[:, :], compare_op=ALU.not_equal,
                                               fill=1.0, base=0, pattern=[[-1, P]], channel_multiplier=1))
    zeroed = K.relay("diagonals_zeroed")
    zeroed.done(dve.memset(att, 0.0))
    zeroed.done(dve.memset(K.Wbd[:, :, :], 0.0))
    zeroed.done(dve.memset(K.Vbd[:, :, :, :], 0.0))
    zeroed.after(sp, act)

    queue = [sp, act]

    def load(dst, src):
        queue.reverse()
        loads.done(queue[0].dma_start(dst, src))

    for l in (1, 2):
        lw = f"L0_gnn_lin_w{l}"
        load((K.W1 if l == 1 else K.W2)[:, 0:F], D[lw + "_T"])
        load(lin[:, l - 1, :], D[lw])
        load(edge[:, l - 1, :], D[f"L0_gnn_lin_edge_w{l}"])
        for k, what in enumerate(("src", "dst", "edge")):
            for h in range(H):
                load(att[C * h:C * h + C, 3 * (l - 1) + k, h:h + 1],
                     D[f"L0_gnn_att_{what}{l}"][h:h + 1, :].rearrange("a c -> c a"))
    load(K.W1[:, F + 2 * H:], D["L0_gnn_in_w_T"])
    load(K.JK[:, :, :], D["L0_gnn_jk_w_T"].rearrange("(s f) o -> f s o", s=3))
    load(K.WM[:, 0:2, :], D["L1_gnn_msg_w"].rearrange("(s f) o -> f s o", s=2))
    load(K.WM[:, 2:4, :], D["L1_gnn_upd_w"].rearrange("(s f) o -> f s o", s=2))
    for n in names:
        load(K.vec[n], D[n].rearrange("(a f) -> a f", a=1).broadcast_to([P, F]))
    load(K.gate_b[:, :], D["L1_gnn_gate_b"].rearrange("(a f) -> a f", a=1).broadcast_to([P, 1]))
    load(encw2, D["L0_gnn_enc_w2"])
    load(encb2, D["L0_gnn_enc_b2"].rearrange("(a f) -> a f", f=1))
    for c in range(CH):
        q, d = divmod(c, CH // 2)
        load(K.Wbd[4 * c:4 * c + 4, q, HID * d:HID * d + HID], D["L0_gnn_enc_w1_T"])
    for d in range(CH // 2):
        load(K.b1rep[HID * d:HID * d + HID, :], D["L0_gnn_enc_b1"].rearrange("(a f) -> a f", f=1))
    loads.after(pe, dve)

    made.after(pe, dve)
    ps = K.ps
    for l in (0, 1):
        W = (K.W1, K.W2)[l]
        folded.step(pe, lambda: pe.matmul(ps[:, 0, 0:H], lin[:, l, :], att[:, 3 * l, :], start=True, stop=True))
        folded.step(pe, lambda: pe.matmul(ps[:, 1, 0:H], lin[:, l, :], att[:, 3 * l + 1, :], start=True, stop=True))
        folded.step(pe, lambda: pe.matmul(ps[0:H, 2, 0:H], edge[:, l, :], att[:, 3 * l + 2, :], start=True, stop=True))
        folded.step(dve, lambda: dve.tensor_copy(W[:, F:F + 2 * H].rearrange("p (m h) -> p m h", h=H), ps[:, 0:2, 0:H]))
        folded.step(dve, lambda: dve.tensor_copy(We[:, l, :], ps[0:H, 2, 0:H]))
        folded.step(dve, lambda: dve.tensor_copy(
            WeR[:, l, :].rearrange("p (c h) -> p c h", h=H), We[:, l, :].unsqueeze(1).broadcast_to([H, CH, H])))
        folded.step(dve, lambda: dve.tensor_copy(b2R, encb2.broadcast_to([H, P])))
        folded.step(pe, lambda: pe.matmul(ps[0:HID, 3, 0:H], encw2, We[:, l, :], start=True, stop=True))
        folded.step(pe, lambda: pe.matmul(ps[:, 4, 0:1], WeR[:, l, :], encb2, start=True, stop=True))
        folded.step(pe, lambda: pe.matmul(ps[:, 5, 0:H], b2R, We[:, l, :], start=True, stop=True))
        folded.step(dve, lambda: dve.tensor_copy(V[:, l, :], ps[0:HID, 3, 0:H]))
        folded.step(dve, lambda: dve.tensor_copy(K.ccol[:, l:l + 1], ps[:, 4, 0:1]))
        folded.step(dve, lambda: dve.tensor_copy(K.crow[:, l, :], ps[:, 5, 0:H]))
    folded.after(sp, act)
    for l in (0, 1):
        for c in range(CH):
            q, d = divmod(c, CH // 2)
            load(K.Vbd[HID * d:HID * d + HID, l, q, H * c:H * c + H], V[:, l, :])
        for d in range(CH // 2):
            load(K.Vrep[HID * d:HID * d + HID, l, :], V[:, l, :])
    loads.after(sp)
    K.barrier()


def place_edges(K, D):
    nc, pool, pe, dve, sp, act = K.nc, K.pool, K.pe, K.dve, K.sp, K.act
    K.SRC = K.sb("slot_src", [P, SLOTS], i32)
    K.DL = K.sb("slot_local_dst", [P, SLOTS])
    K.KEY = K.sb("slot_key", [P, SLOTS])
    K.WT = K.sb("slot_weight", [P, SLOTS])
    K.BLK = K.sb("slot_block", [1, SLOTS], i16)
    edge_rows = K.dram("edge_rows", [EROWS, 3, P], i32)
    blk_dram = K.dram("slot_block_dram", [SC * P], i16)

    pad = K.RL[0:EROWS - TILES + 1, 0:3 * P].bitcast(i32).rearrange("p (a e) -> p a e", a=3)
    NR = 125
    RW = E // NR
    dst_nat = K.RL[0:NR, 512:512 + RW].bitcast(i32)
    hit = K.RL[0:NR, 512 + RW:512 + 2 * RW]
    below = K.RL[0:NR, 4000:4000 + NB - 1]
    start_i = K.RL[:, 4100:4100 + NB - 1].bitcast(i32)
    thresh = K.RL[:, 4200:4200 + NB - 1]
    sidx = K.RL[:, 4300:4300 + SC]
    blk = K.RL[:, 4320:4320 + SC]
    blk_i = K.RL[:, 4340:4340 + SC].bitcast(i16)[:, 0:SC]
    tile_f = K.RL[:, 4360:4360 + SC]
    tile_i = K.RL[:, 4380:4380 + SC].bitcast(i32)
    blk128 = K.RL[:, 4400:4400 + SC]
    junk = K.RL[:, 4500:4500 + NB - 1]
    erow = K.RF[:, 0:SC * 3 * P].rearrange("p (c a e) -> p c a e", a=3, e=P)
    erow_flat = K.RF[:, 0:SC * 3 * P].rearrange("p (c w) -> p c w", w=3 * P).bitcast(i32)
    SW = SC * P
    srcf = K.RA[:, 0:SW].rearrange("p (c e) -> p c e", e=P)
    dstf = K.RA[:, SW:2 * SW].rearrange("p (c e) -> p c e", e=P)
    local = K.RA[:, 2 * SW:3 * SW].rearrange("p (c e) -> p c e", e=P)
    valid = K.RA[:, 3 * SW:4 * SW].rearrange("p (c e) -> p c e", e=P)

    m, d, g = K.relay("place_steps"), K.dmas("place_dmas"), Relay(K.arrived[0], 16)
    filled = K.relay("pad_filled")
    filled.done(pool.memset(pad[:, 0, :], 0))
    filled.done(pool.memset(pad[:, 1, :], -1))
    filled.done(pool.memset(pad[:, 2, :], 0))
    full = (TILES - 1) * P
    for a, name in enumerate(("src", "dst", "edge_weight")):
        flat = D[name] if name != "edge_weight" else D[name].bitcast(i32)
        d.done(sp.dma_start(edge_rows[0:TILES - 1, a, :], flat[0:full].rearrange("(t e) -> t e", e=P)))
        d.done(act.dma_start(edge_rows[TILES - 1:TILES, a, 0:E - full], flat[full:E].rearrange("(t e) -> t e", t=1)))
    d.done(sp.dma_start(dst_nat, D["dst"].rearrange("(r e) -> r e", r=NR)))
    filled.after(sp, act)
    if E - full < P:
        d.done(act.dma_start(edge_rows[TILES - 1:TILES, :, E - full:P], pad[0:1, :, E - full:P]))
    d.done(act.dma_start(edge_rows[TILES:EROWS, :, :], pad[1:EROWS - TILES + 1, :, :]))
    filled.done(pool.iota(sidx, [[P, SC]], base=0, channel_multiplier=1, allow_small_or_imprecise_dtypes=True))
    d.after(dve)
    for b in range(1, NB):
        m.step(dve, lambda: dve.tensor_scalar(hit, dst_nat, float(P * b), 0.0, ALU.is_lt, ALU.add,
                                              accum_out=below[:, b - 1:b]))
    m.step(pe, lambda: pe.matmul(K.ps[:, 0, 0:NB - 1], K.ones[0:NR, :], below, start=True, stop=True))
    m.step(dve, lambda: dve.tensor_copy(start_i, K.ps[:, 0, 0:NB - 1]))
    m.step(dve, lambda: dve.tensor_scalar(start_i, start_i, 7, None, ALU.arith_shift_right))
    m.step(dve, lambda: dve.tensor_copy(thresh, start_i))
    m.step(dve, lambda: dve.tensor_tensor(thresh, thresh, K.iota[:, 1:NB], ALU.add))
    filled.after(dve)
    for c in range(SC):
        m.step(dve, lambda: dve.tensor_scalar(junk, thresh, sidx[:, c:c + 1], 0.0, ALU.is_le, ALU.add,
                                              accum_out=blk[:, c:c + 1]))
    m.step(dve, lambda: dve.tensor_tensor(tile_f, sidx, blk, ALU.subtract))
    m.step(dve, lambda: dve.tensor_scalar(tile_f, tile_f, float(EROWS - 1), None, ALU.min))
    m.step(dve, lambda: dve.tensor_copy(tile_i, tile_f))
    m.step(dve, lambda: dve.tensor_copy(blk_i, blk))
    m.step(dve, lambda: dve.tensor_scalar(blk128, blk, float(P), None, ALU.mult))
    m.after(pool, sp)
    with nc.allow_non_contiguous_dma("block of each slot, once"):
        d.done(sp.dma_start(blk_dram.rearrange("(c p) -> p c", p=P), blk_i))
    d.after(pool, sp)
    d.done(sp.dma_start(K.BLK[:, :], blk_dram[0:SLOTS].rearrange("(a s) -> a s", a=1)))
    for c in range(SC):
        g.done(pool.indirect_dma_start(out=erow_flat[:, c, :], out_offset=None,
                                       in_=edge_rows.rearrange("t a e -> t (a e)"),
                                       in_offset=bass.IndirectOffsetOnAxis(ap=tile_i[:, c:c + 1], axis=0)))
    g.after(dve, act, pe)
    K.arrived_before[0] += g.n
    m.step(act, lambda: act.activation(srcf, erow[:, :, 0, :].bitcast(i32), ACT.Copy))
    m.step(dve, lambda: dve.tensor_copy(dstf, erow[:, :, 1, :].bitcast(i32)))
    m.step(dve, lambda: dve.tensor_tensor(local, dstf, blk128.unsqueeze(2).broadcast_to([P, SC, P]), ALU.subtract))
    m.step(dve, lambda: dve.tensor_scalar(valid, local, 0.0, None, ALU.is_ge))
    m.step(dve, lambda: dve.scalar_tensor_tensor(valid, local, float(P), valid, ALU.is_lt, ALU.mult))
    m.step(dve, lambda: dve.scalar_tensor_tensor(local, local, 1.0, valid, ALU.add, ALU.mult))
    m.step(dve, lambda: dve.tensor_scalar(local, local, -1.0, None, ALU.add))
    m.step(dve, lambda: dve.scalar_tensor_tensor(dstf, dstf, 1.0, valid, ALU.add, ALU.mult))
    m.step(dve, lambda: dve.tensor_scalar(dstf, dstf, -1.0, None, ALU.add))
    n = 0
    for out, source in ((K.SRC, srcf), (K.DL, local), (K.KEY, dstf), (K.WT, erow[:, :, 2, :])):
        for c0 in range(0, SC, 4):
            cs = range(c0, min(c0 + 4, SC))
            w = min(SLOTS, (cs[-1] + 1) * P) - c0 * P
            m.after(pe)
            for c in cs:
                last = pe.transpose(K.ps[:, n % 8, (c - c0) * P:(c - c0 + 1) * P], source[:, c, :], K.ident[:, :])
            m.done(last)
            m.step(dve, lambda: dve.tensor_copy(out[:, c0 * P:c0 * P + w], K.ps[:, n % 8, 0:w]))
            n += 1
    d.after(sp)
    K.barrier()


def project(K, name, sources, width, evacuate):
    pe, act, dve = K.pe, K.act, K.dve
    transposed, copied = K.relay(name + "_transposed"), K.relay(name + "_copied")
    multiplied, evacuated = K.relay(name + "_multiplied"), K.relay(name + "_evacuated")
    units = [(b, k) for b in range(NB) for k in range(len(sources))]

    def transpose(q):
        b, k = units[q]
        if q >= 2:
            pe.wait_ge(copied.sem, q - 1)
        transposed.done(pe.transpose(K.ps[:, q % 2, 0:P], sources[k][0][:, b, :], K.ident[:, :]))
        act.wait_ge(transposed.sem, q + 1)
        if q >= 2:
            act.wait_ge(multiplied.sem, q - 1)
        copied.done(act.activation(K.xT[:, q % 2, :], K.ps[:, q % 2, 0:P], ACT.Copy))

    transpose(0)
    for q, (b, k) in enumerate(units):
        if q + 1 < len(units):
            transpose(q + 1)
        pe.wait_ge(copied.sem, q + 1)
        if k == 0 and b >= 2:
            pe.wait_ge(evacuated.sem, b - 1)
        multiplied.done(pe.matmul(K.ps[:, 2 + b % 2, 0:width], K.xT[:, q % 2, :], sources[k][1],
                                  start=k == 0, stop=k == len(sources) - 1))
        if k == len(sources) - 1:
            dve.wait_ge(multiplied.sem, q + 1)
            evacuated.done(evacuate(b, K.ps[:, 2 + b % 2, 0:width]))


def nodes_in(K, D):
    dve, sp, act, pool = K.dve, K.sp, K.act, K.pool
    K.rows1, K.h0, K.h1 = K.dram("rows1", [NPAD, ROW1]), K.dram("h0", [NPAD, F]), K.dram("h1", [NPAD, F])
    K.rows2, K.h2 = K.dram("rows2", [NPAD, ROW2]), K.dram("h2", [NPAD, F])
    K.a_node = K.sb("a_src_a_dst", [P, NB, 2 * H])
    K.by_dst = table(K.RL, DCOL1)
    stage, h0 = table(K.RA, ROW1), table(K.RF, F)
    square = table(K.RF, F)
    s, d = K.relay("nodes_in_steps"), K.dmas("nodes_in_dmas")
    s.done(pool.memset(K.by_dst[:, NB - 1, :], 0.0))
    s.after(sp)
    load_x(K, D, K.by_dst[:, :, 0:F], d)
    d.after(K.pe, dve)

    def evacuate(b, ps):
        dve.tensor_copy(stage[:, b, F:2 * F + H], ps[:, 0:F + H])
        dve.tensor_copy(K.a_node[:, b, :], ps[:, F:F + 2 * H])
        return dve.tensor_tensor(h0[:, b, :], ps[:, F + 2 * H:], K.vec["L0_gnn_in_b"], ALU.add)

    project(K, "in", [(K.by_dst[:, :, 0:F], K.W1[:, :])], F + 2 * H + F, evacuate)
    K.barrier()
    d.done(sp.dma_start(rows(K.h0), h0))
    s.step(dve, lambda: dve.tensor_copy(stage[:, :, 0:F], K.by_dst[:, :, 0:F]))
    s.step(dve, lambda: dve.tensor_copy(K.by_dst[:, :, F:F + H], K.a_node[:, :, H:2 * H]))
    d.after(dve)
    s.step(dve, lambda: dve.tensor_tensor(square, K.by_dst[:, :, 0:F], K.by_dst[:, :, 0:F], ALU.mult))
    s.step(dve, lambda: dve.tensor_reduce(stage[:, :, ROW1 - 1], square, AX.X, ALU.add))
    s.step(dve, lambda: dve.tensor_copy(K.by_dst[:, :, DCOL1 - 1], stage[:, :, ROW1 - 1]))
    s.after(sp)
    d.done(sp.dma_start(rows(K.rows1), stage))
    d.after(sp)
    K.barrier()


def load_x(K, D, out, relay):
    cut = (NB - 1) * P
    relay.done(K.sp.dma_start(out[:, 0:NB - 1, :], D["x"][0:cut, :].rearrange("(b p) w -> p b w", p=P)))
    relay.done(K.sp.dma_start(out[0:LAST, NB - 1, :], D["x"][cut:N, :]))


class Gather:

    def __init__(self, K, name, source, width, buffer):
        self.K, self.source, self.buffer = K, source, buffer
        self.index = K.slot_index
        self.picked = [K.sem(f"{name}_indices_picked{u}") for u in range(U)]
        self.arrived, self.before = K.arrived, list(K.arrived_before)
        for u in range(U):
            K.arrived_before[u] += SLOTS // (G * U) * G * 16

    def wait(self, engine, i, u):
        self.K.loop_wait(engine, self.arrived[u], i * (16 * G) + 16 * G + self.before[u])

    def emit(self, i, u, slot):
        K, pool = self.K, self.K.pool
        pool.tensor_copy(self.index[:, u, :], K.SRC[:, bass.ds(slot, G)]).then_inc(self.picked[u], 1)
        K.loop_wait(pool, self.picked[u], i + 1)
        for j in range(G):
            pool.indirect_dma_start(out=self.buffer[:, u, j, :], out_offset=None, in_=self.source,
                                    in_offset=bass.IndirectOffsetOnAxis(ap=self.index[:, u, j:j + 1], axis=0)
                                    ).then_inc(self.arrived[u], 16)


def slot_blocks(K, engine, kind, slot):
    _, values = K.nc.values_load_multi_w_load_instructions(
        K.BLK[0:1, bass.ds(slot, G)], engines=[kind], min_val=0, max_val=NB - 1,
        skip_runtime_bounds_check_because="counts of the 48 block starts that a slot has passed")
    return values


def logits_pass(K, layer):
    nc, pool, act, pe, dve, sp = K.nc, K.pool, K.act, K.pe, K.dve, K.sp
    first = layer == 1
    row, dcol = (ROW1, DCOL1) if first else (ROW2, H)
    source = K.rows1 if first else K.rows2
    xs0, as0 = (F, 2 * F) if first else (0, F)
    at = NB * DCOL1
    def take(n, shape, **kw):
        nonlocal at
        v = K.RL[:, at:at + n].rearrange(shape, **kw)
        at += n
        return v
    rowbuf = take(U * G * row, "p (u g w) -> p u g w", u=U, g=G)
    onehot = take(U * G * P, "p (u g e) -> p u g e", u=U, g=G)
    onehotT = take(U * G * P, "p (u g e) -> p u g e", u=U, g=G)
    junk = take(U * G * P, "p (u g e) -> p u g e", u=U, g=G)
    dots = take(U * G, "p (u g) -> p u g", u=U)
    assert at <= REGION
    asum = K.RA[:, 0:SLOTS * H].rearrange("p (s h) -> p s h", h=H)
    feat = K.RF[:, 0:SLOTS * 4].rearrange("p (s f) -> p s f", f=4)
    psT = [K.ps[:, u, :].rearrange("p (g e) -> p g e", g=G) for u in range(U)]
    psX = [K.ps[:, 2 + 2 * u:4 + 2 * u, :].rearrange("p k (a w) -> p (k a) w", a=2) for u in range(U)]
    n = f"logits{layer}"
    gather = Gather(K, n, source, row, rowbuf)
    onehot_made = [K.sem(f"{n}_onehot_made{u}") for u in range(U)]
    transposed = [K.sem(f"{n}_transposed{u}") for u in range(U)]
    transpose_out = [K.sem(f"{n}_transpose_out{u}") for u in range(U)]
    selected = [K.sem(f"{n}_selected{u}") for u in range(U)]
    dotted = [K.sem(f"{n}_dotted{u}") for u in range(U)]
    consumed = [K.sem(f"{n}_consumed{u}") for u in range(U)]
    spilled = [K.sem(f"{n}_spilled{u}") for u in range(U)]
    for u in range(U):
        for sem in (transposed[u], transpose_out[u], selected[u], consumed[u]):
            dve.sem_inc(sem, 1)
        sp.dma_start(K.credit[u:u + 1, :], K.ident[0:1, 0:P]).then_inc(spilled[u], 16)
    K.barrier()
    with nc.Fori(0, SLOTS // (G * U), engines=ENGINES) as i:
        for u in range(U):
            slot = i * (G * U) + u * G
            K.loop_wait(pool, consumed[u], i + 1)
            K.loop_wait(pool, spilled[u], i * 16 + 16)
            gather.emit(i, u, slot)
            K.loop_wait(dve, transposed[u], i + 1)
            dve.tensor_tensor(onehot[:, u, :, :], K.iota[:, :].unsqueeze(1).broadcast_to([P, G, P]),
                              K.DL[:, bass.ds(slot, G)].unsqueeze(2).broadcast_to([P, G, P]),
                              ALU.is_equal).then_inc(onehot_made[u], 1)
            K.loop_wait(pe, onehot_made[u], i + 1)
            K.loop_wait(pe, transpose_out[u], i + 1)
            for j in range(G):
                last = pe.transpose(psT[u][:, j, :], onehot[:, u, j, :], K.ident[:, :])
            last.then_inc(transposed[u], 1)
            K.loop_wait(act, transposed[u], i + 2)
            K.loop_wait(act, selected[u], i + 1)
            act.activation(onehotT[:, u, :, :], psT[u], ACT.Copy).then_inc(transpose_out[u], 1)
            blocks = slot_blocks(K, pe, ET.PE, slot)
            K.loop_wait(pe, transpose_out[u], i + 2)
            K.loop_wait(pe, consumed[u], i + 1)
            for j in range(G):
                last = pe.matmul(psX[u][:, j, 0:dcol], onehotT[:, u, j, :],
                                 K.by_dst[:, bass.ds(blocks[j], 1), 0:dcol].rearrange("p b w -> p (b w)"),
                                 start=True, stop=True)
            last.then_inc(selected[u], 1)
            gather.wait(sp, i, u)
            sp.dma_start(K.spill[bass.ds(i * U + u, 1), :, :].rearrange("a p (g w) -> (a p) g w", g=G),
                         rowbuf[:, u, :, xs0:xs0 + F]).then_inc(spilled[u], 16)
        for u in range(U):
            slot = i * (G * U) + u * G
            K.loop_wait(dve, selected[u], i + 2)
            gather.wait(dve, i, u)
            if first:
                for j in range(G):
                    last = dve.tensor_tensor_reduce(out=junk[:, u, j, :], in0=rowbuf[:, u, j, 0:F],
                                                    in1=psX[u][:, j, 0:F], scale=1.0, scalar=0.0,
                                                    op0=ALU.mult, op1=ALU.add, accum_out=dots[:, u, j:j + 1])
                last.then_inc(dotted[u], 1)
                dve.tensor_copy(feat[:, bass.ds(slot, G), 2:3], rowbuf[:, u, :, ROW1 - 1:ROW1])
                dve.tensor_copy(feat[:, bass.ds(slot, G), 3:4], psX[u][:, :, DCOL1 - 1:DCOL1])
                K.loop_wait(dve, dotted[u], i + 1)
                dve.tensor_copy(feat[:, bass.ds(slot, G), 0:1], dots[:, u, :].unsqueeze(2))
            dve.tensor_tensor(asum[:, bass.ds(slot, G), :], rowbuf[:, u, :, as0:as0 + H],
                              psX[u][:, :, dcol - H - 1:dcol - 1] if first else psX[u][:, :, 0:H],
                              ALU.add).then_inc(consumed[u], 1)
    for u in range(U):
        sp.wait_ge(spilled[u], 16 + 16 * (SLOTS // (G * U)))
    K.barrier()


def chunked(region, width):
    return region[:, 0:SLOTS * width].rearrange("p (c k w) -> p k c w", k=KC, w=width)


def edge_features(K):
    dve = K.dve
    feat = K.RF[:, 0:SLOTS * 4].rearrange("p (s f) -> p s f", f=4)
    valid = K.RF[:, SLOTS * 4:SLOTS * 5]
    s = K.relay("features")
    s.step(dve, lambda: dve.tensor_scalar(valid, K.DL[:, :], 0.0, None, ALU.is_ge))
    s.step(dve, lambda: dve.tensor_tensor(feat[:, :, 1], feat[:, :, 2], feat[:, :, 3], ALU.add))
    s.step(dve, lambda: dve.scalar_tensor_tensor(feat[:, :, 1], feat[:, :, 0], -2.0, feat[:, :, 1], ALU.mult, ALU.add))
    s.step(dve, lambda: dve.tensor_tensor(feat, feat, valid.unsqueeze(2).broadcast_to([P, SLOTS, 4]), ALU.mult))
    K.barrier()


def logits(K, layer):
    act, pe, dve, sp, pool = K.act, K.pe, K.dve, K.sp, K.pool
    L = K.RL
    first = layer == 1
    feat, asum = chunked(K.RF, 4), chunked(K.RA, H)
    at = SLOTS * 4
    def take(n):
        nonlocal at
        at += n
        return K.RF[:, at - n:at]
    W = 4 * P
    featT, hidden, raw, edge2 = take(2 * W), take(4 * W), take(2 * W), take(2 * W)
    sum_packed = take(8 * P).rearrange("p (z k w) -> p z k w", z=2, w=P)
    feat_packed = K.xT[:, :, :].rearrange("p u (k w) -> p (u k) w", w=4 * CH)
    assert at <= REGION
    n = f"softmax_in{layer}_"
    packed = K.relay(n + "packed")
    ftr, fcp, hid_mm, hid_out = (K.relay(n + x) for x in ("features_transposed", "features_out", "hidden_product", "hidden_out"))
    lg_mm, e2_mm, biased, done, e2_out = (K.relay(n + x) for x in ("logit_product", "edge2_product", "biased", "done", "edge2_out"))
    io = [K.dmas(n + f"edge2_dma{z}") for z in range(2)]
    for z, k0 in enumerate(range(0, KC, 4)):
        ks = range(k0, min(k0 + 4, KC))
        w = len(ks) * P
        half = (z % 2) * W
        if z >= 2:
            pool.wait_ge(lg_mm.sem, z - 1)
        split = lambda t, w: t.rearrange("p k (c w) -> p k c w", w=w)
        if first:
            if z >= 1:
                pool.wait_ge(ftr.sem, z)
            pool.tensor_copy(split(feat_packed[:, 0:len(ks), :], 4), feat[:, k0:k0 + len(ks), :, :])
        packed.done(pool.tensor_copy(split(sum_packed[:, z % 2, 0:len(ks), :], H), asum[:, k0:k0 + len(ks), :, :]))
        pe.wait_ge(packed.sem, z + 1)
        if first:
            if z >= 1:
                pe.wait_ge(fcp.sem, z)
            for k in ks:
                last = pe.transpose(K.ps[0:4 * CH, 0, (k - k0) * P:(k - k0 + 1) * P], feat_packed[:, k - k0, :], K.ident[:, :])
            ftr.done(last)
            act.wait_ge(ftr.sem, z + 1)
            if z >= 2:
                act.wait_ge(hid_mm.sem, 2 * (z - 1))
            fcp.done(act.activation(featT[0:4 * CH, half:half + w], K.ps[0:4 * CH, 0, 0:w], ACT.Copy))
            for q in (0, 1):
                pe.wait_ge(fcp.sem, z + 1)
                if z >= 1:
                    pe.wait_ge(hid_out.sem, 2 * (z - 1) + q + 1)
                hid_mm.done(pe.matmul(K.ps[:, 1 + q, 0:w], K.Wbd[:, q, :], featT[0:4 * CH, half:half + w], start=True, stop=True))
                act.wait_ge(hid_mm.sem, 2 * z + q + 1)
                if z >= 2:
                    act.wait_ge(e2_mm.sem, z - 1)
                hid_out.done(act.activation(hidden[:, 2 * half + q * W:2 * half + q * W + w], K.ps[:, 1 + q, 0:w], ACT.Relu,
                                            bias=K.b1rep[:, 0:1], accum_out=K.hidden_sums[:, q, z:z + 1]))
            pe.wait_ge(hid_out.sem, 2 * z + 2)
        if z >= 2:
            pe.wait_ge(biased.sem, z - 1)
        bank = 3 + z % 2
        if first:
            for q in (0, 1):
                pe.matmul(K.ps[:, bank, 0:w], K.Vbd[:, 0, q, :], hidden[:, 2 * half + q * W:2 * half + q * W + w],
                          start=q == 0, stop=False, skip_group_check=True)
        for k in ks:
            last = pe.matmul(K.ps[:, bank, (k - k0) * P:(k - k0 + 1) * P], sum_packed[:, z % 2, k - k0, :], K.ident[:, :],
                             start=not first, stop=True, skip_group_check=True)
        lg_mm.done(last)
        if first:
            if z >= 2:
                pe.wait_ge(e2_out.sem, z - 1)
            for q in (0, 1):
                last = pe.matmul(K.ps[:, 5 + z % 2, 0:w], K.Vbd[:, 1, q, :], hidden[:, 2 * half + q * W:2 * half + q * W + w],
                                 start=q == 0, stop=q == 1)
            e2_mm.done(last)
        dve.wait_ge(lg_mm.sem, z + 1)
        if first:
            biased.done(dve.tensor_scalar(raw[:, half:half + w], K.ps[:, bank, 0:w], K.ccol[:, 0:1], None, ALU.add))
            act.wait_ge(e2_mm.sem, z + 1)
            if z >= 2:
                io[z % 2].after(act)
            e2_out.done(act.activation(edge2[:, half:half + w], K.ps[:, 5 + z % 2, 0:w], ACT.Identity, bias=K.ccol[:, 1:2]))
            sp.wait_ge(e2_out.sem, z + 1)
            io[z % 2].done(sp.dma_start(K.edge2[:, k0 * P:k0 * P + w], edge2[:, half:half + w]))
        else:
            if z >= 2:
                sp.wait_ge(biased.sem, z - 1)
            io[z % 2].done(sp.dma_start(edge2[:, half:half + w], K.edge2[:, k0 * P:k0 * P + w]))
            io[z % 2].after(dve)
            biased.done(dve.tensor_tensor(raw[:, half:half + w], K.ps[:, bank, 0:w], edge2[:, half:half + w], ALU.add))
        dve.wait_ge(biased.sem, z + 1)
        done.done(dve.scalar_tensor_tensor(L[:, k0 * P:k0 * P + w], raw[:, half:half + w], SLOPE, raw[:, half:half + w],
                                           ALU.mult, ALU.max))
    for r in io:
        r.after(sp)
    K.barrier()


def breaks(K, layer):
    act, pe, dve = K.act, K.pe, K.dve
    n = f"breaks{layer}_"
    tr, cp, s = K.relay(n + "transposed"), K.relay(n + "copied"), K.relay(n + "steps")
    keys = K.RF[:, 0:TC]
    pen = K.penalty
    rep = K.RA[:, 8192:8192 + 2 * 4 * P].rearrange("p (z c h) -> p z c h", z=8, h=H)
    kview = chunked(K.KEY, 1)
    for k in range(KC):
        if k >= 8:
            dve.wait_ge(tr.sem, k - 7)
        s.done(dve.tensor_copy(rep[:, k % 8, :, :], kview[:, k, :, :].broadcast_to([P, CH, H])))
        pe.wait_ge(s.sem, k + 1)
        if k >= 8:
            pe.wait_ge(cp.sem, k - 7)
        tr.done(pe.transpose(K.ps[:, k % 8, 0:P], rep[:, k % 8, :, :].rearrange("p c h -> p (c h)"), K.ident[:, :]))
        act.wait_ge(tr.sem, k + 1)
        cp.done(act.activation(keys[:, k * P:(k + 1) * P], K.ps[:, k % 8, 0:P], ACT.Copy))
    K.barrier()
    s.step(dve, lambda: dve.memset(pen[:, 0:1], 0.0))
    s.step(dve, lambda: dve.tensor_tensor(pen[:, 1:TC], keys[:, 1:TC], keys[:, 0:TC - 1], ALU.not_equal))
    s.step(dve, lambda: dve.tensor_scalar(pen[:, 1:TC], pen[:, 1:TC], -BIG, None, ALU.mult))
    cols, R = K.cols, K.rowbuf
    s.step(dve, lambda: dve.tensor_reduce(cols[:, 0:1], pen, AX.X, ALU.min))
    s.step(dve, lambda: dve.tensor_scalar(cols[:, 0:1], cols[:, 0:1], 0.0, None, ALU.is_ge))
    s.step(dve, lambda: dve.tensor_copy(cols[:, 1:2], keys[:, 0:1]))
    s.step(dve, lambda: dve.tensor_copy(cols[:, 2:3], keys[:, TC - 1:TC]))
    rows_of(K, s, [(0, 0, False), (1, 1, False), (2, 2, False)])
    whole, first, last = (R[0:1, k, :, :] for k in range(3))
    goes = R[0:1, 3, :, :]
    s.step(dve, lambda: dve.memset(R[0:1, 3:7, :, :], 0.0))
    s.step(dve, lambda: dve.tensor_tensor(goes[:, :, 1:CH], first[:, :, 1:CH], last[:, :, 0:CH - 1], ALU.is_equal))
    M = K.rowbuf2
    s.step(dve, lambda: dve.tensor_tensor(M[0:1, 0, :, :], whole, goes, ALU.mult))
    s.step(dve, lambda: dve.tensor_copy(M[0:1, 1, :, :], goes))
    s.step(dve, lambda: dve.memset(M[0:1, 2:4, :, :], 0.0))
    s.step(dve, lambda: dve.tensor_copy(M[0:1, 3, :, 1:CH], goes[:, :, CH - 1:0:-1]))
    s.step(dve, lambda: dve.tensor_tensor(M[0:1, 2, :, 1:CH], M[0:1, 3, :, 1:CH], whole[:, :, CH - 2::-1], ALU.mult))
    s.step(dve, lambda: dve.tensor_scalar(M[0:1, :, :, :], M[0:1, :, :, :], BIG, -BIG, ALU.mult, ALU.add))
    s.step(dve, lambda: dve.tensor_copy(R[0:1, 4, :, :], goes))
    columns_of(K, s, [(4, 3, False)])
    K.barrier()


def rows_of(K, s, moves):
    for col, row, mirrored in moves:
        s.step(K.pe, lambda: K.pe.matmul(K.ps[0:1, 0, 0:P], K.cols[:, col:col + 1], K.ident[:, :], start=True, stop=True))
        source = K.ps[0:1, 0, 0:P].rearrange("a (c h) -> a h c", h=H)
        s.step(K.dve, lambda: K.dve.tensor_copy(K.rowbuf[0:1, row, :, :], source[:, :, ::-1] if mirrored else source))


def columns_of(K, s, moves):
    flat = K.rowflat
    for row, col, mirrored in moves:
        source = K.rowbuf[0:1, row, :, :]
        s.step(K.dve, lambda: K.dve.tensor_copy(flat[0:1, :].rearrange("a (c h) -> a h c", h=H),
                                                source[:, :, ::-1] if mirrored else source))
        s.step(K.pe, lambda: K.pe.matmul(K.ps[:, 1, 0:1], flat[0:1, :], K.ones[0:1, 0:1], start=True, stop=True))
        s.step(K.dve, lambda: K.dve.tensor_copy(K.cols[:, col:col + 1], K.ps[:, 1, 0:1]))


def segment_softmax(K, layer):
    act, pe, dve = K.act, K.pe, K.dve
    n = f"softmax{layer}_"
    s = K.relay(n + "steps")
    L, M, pen, cols, R, Z = K.RL[:, 0:TC], K.RF[:, 0:TC], K.penalty, K.cols, K.rowbuf, K.rowbuf2

    def chain(col_in, z, mirrored, col_out):
        rows_of(K, s, [(col_in, 0, mirrored)])
        flat = lambda r: r.rearrange("a h c -> a (h c)")
        s.step(dve, lambda: dve.tensor_tensor_scan(out=flat(R[0:1, 1, :, :]), data0=flat(Z[0:1, z, :, :]),
                                                   data1=flat(R[0:1, 0, :, :]), initial=-BIG, op0=ALU.add, op1=ALU.max))
        s.step(dve, lambda: dve.memset(R[0:1, 2, :, :], -BIG))
        s.step(dve, lambda: dve.tensor_tensor(R[0:1, 2, :, 1:CH], R[0:1, 1, :, 0:CH - 1], Z[0:1, z + 1, :, 1:CH], ALU.add))
        columns_of(K, s, [(2, col_out, mirrored)])

    def scan(out, data, back, initial):
        if not back:
            return dve.tensor_tensor_scan(out=out, data0=pen, data1=data, initial=initial, op0=ALU.add, op1=ALU.max)
        return dve.tensor_tensor_scan(out=out[:, TC - 2::-1], data0=pen[:, TC - 1:0:-1], data1=data[:, TC - 2::-1],
                                      initial=initial, op0=ALU.add, op1=ALU.max)

    s.step(dve, lambda: scan(M, L, False, -BIG))
    s.step(dve, lambda: dve.tensor_copy(cols[:, 4:5], M[:, TC - 1:TC]))
    chain(4, 0, False, 5)
    s.step(dve, lambda: scan(M, L, False, cols[:, 5:6]))
    s.step(dve, lambda: dve.tensor_copy(cols[:, 6:7], M[:, TC - 1:TC]))
    s.step(dve, lambda: scan(M, M, True, cols[:, 6:7]))
    s.step(dve, lambda: dve.tensor_copy(cols[:, 4:5], M[:, 0:1]))
    chain(4, 2, True, 5)
    s.step(dve, lambda: dve.tensor_tensor(cols[:, 6:7], M[:, TC - 1:TC], cols[:, 5:6], ALU.max))
    s.step(dve, lambda: dve.tensor_copy(M[:, TC - 1:TC], cols[:, 6:7]))
    s.step(dve, lambda: scan(M, M, True, cols[:, 6:7]))
    s.step(dve, lambda: dve.tensor_tensor(L, L, M, ALU.subtract))
    s.step(act, lambda: act.activation(L, L, ACT.Exp))
    s.step(dve, lambda: dve.scalar_tensor_tensor(M[:, 1:TC], pen[:, 1:TC], 0.0, M[:, 1:TC], ALU.is_lt, ALU.mult))
    s.step(dve, lambda: dve.tensor_scalar(cols[:, 7:8], cols[:, 3:4], -1.0, 1.0, ALU.mult, ALU.add))
    s.step(dve, lambda: dve.tensor_tensor(M[:, 0:1], M[:, 0:1], cols[:, 7:8], ALU.mult))
    K.barrier()
    for what, source, out in (("weights", L, chunked(K.RA, H)), ("maxima", M, chunked(K.RL, H))):
        tr, ev = K.relay(n + what + "_transposed"), K.relay(n + what + "_out")
        for z, k0 in enumerate(range(0, KC, 4)):
            ks = range(k0, min(k0 + 4, KC))
            if z >= 4:
                pe.wait_ge(ev.sem, z - 3)
            for k in ks:
                last = pe.transpose(K.ps[:, z % 4, (k - k0) * P:(k - k0 + 1) * P], source[:, k * P:(k + 1) * P], K.ident[:, :])
            tr.done(last)
            dve.wait_ge(tr.sem, z + 1)
            ev.done(dve.tensor_copy(out[:, k0:k0 + len(ks), :, :],
                                    K.ps[:, z % 4, 0:len(ks) * P].rearrange("p (k c h) -> p k c h", c=CH, h=H)))
        K.barrier()


def add_visit(K, i, u, scattered, added, count, acc, width, psB, blocks):
    dve = K.dve
    K.loop_wait(dve, scattered, i + 2)
    for j in range(G):
        K.loop_wait(dve, added, count + j)
        row = acc[:, bass.ds(blocks[j], 1), 0:width].rearrange("p b w -> p (b w)")
        last = dve.tensor_tensor(row, row, psB[:, j, 0:width], ALU.add)
        last.then_inc(added, 1)


def weighted_sum(K, layer):
    nc, pool, act, pe, dve, sp = K.nc, K.pool, K.act, K.pe, K.dve, K.sp
    K.acc = table(K.RF, AW)
    at = NB * AW
    def take(n, w):
        nonlocal at
        v = K.RF[:, at:at + n * U * G].rearrange("p (u g w) -> p u g w", u=U, g=G)
        at += n * U * G
        return v
    xs, onehot, rhs = take(F, F), take(P, P), take(AW, AW)
    assert at <= REGION
    weight = K.RA[:, 0:SLOTS * H].rearrange("p (s h) -> p s h", h=H)
    top = K.RL[:, 0:SLOTS * H].rearrange("p (s h) -> p s h", h=H)
    psB = [K.ps[:, 2 * u:2 * u + 2, :].rearrange("p k (a w) -> p (k a) w", a=2) for u in range(U)]
    n = f"sum{layer}_"
    loaded, made, copied, weighted, scattered = ([K.sem(f"{n}{x}{u}") for u in range(U)] for x in
                                                 ("xs_loaded", "onehot_made", "columns_copied", "weighted", "scattered"))
    added, init = K.sem(n + "added"), K.relay(n + "init")
    init.done(dve.memset(K.acc, 0.0))
    init.done(dve.memset(rhs[:, :, :, AW - 1:AW], 1.0))
    dve.sem_inc(added, 1 + G)
    for u in range(U):
        dve.sem_inc(scattered[u], 1)
        dve.sem_inc(weighted[u], 1)
    K.barrier()
    with nc.Fori(0, SLOTS // (G * U), engines=ENGINES) as i:
        for u in range(U):
            slot = i * (G * U) + u * G
            K.loop_wait(sp, weighted[u], i + 1)
            sp.dma_start(xs[:, u, :, :].rearrange("p g w -> p (g w)"),
                         K.spill[bass.ds(i * U + u, 1), :, :].rearrange("a p w -> (a p) w")).then_inc(loaded[u], 16)
            K.loop_wait(dve, scattered[u], i + 1)
            dve.tensor_tensor(onehot[:, u, :, :], K.iota[:, :].unsqueeze(1).broadcast_to([P, G, P]),
                              K.DL[:, bass.ds(slot, G)].unsqueeze(2).broadcast_to([P, G, P]),
                              ALU.is_equal).then_inc(made[u], 1)
            K.loop_wait(act, scattered[u], i + 1)
            act.activation(rhs[:, u, :, F:F + H], weight[:, bass.ds(slot, G), :], ACT.Copy)
            act.activation(rhs[:, u, :, F + H:F + 2 * H], top[:, bass.ds(slot, G), :], ACT.Copy).then_inc(copied[u], 1)
            K.loop_wait(pool, scattered[u], i + 1)
            K.loop_wait(pool, loaded[u], i * 16 + 16)
            pool.tensor_tensor(rhs[:, u, :, 0:F].rearrange("p g (h c) -> p g h c", c=C),
                               xs[:, u, :, :].rearrange("p g (h c) -> p g h c", c=C),
                               weight[:, bass.ds(slot, G), :].unsqueeze(3).broadcast_to([P, G, H, C]),
                               ALU.mult).then_inc(weighted[u], 1)
            K.loop_wait(pe, made[u], i + 1)
            K.loop_wait(pe, copied[u], i + 1)
            K.loop_wait(pe, weighted[u], i + 2)
            K.loop_wait(pe, added, i * (U * G) + (u + 1) * G - (U - 1) * G + 1)
            for j in range(G):
                last = pe.matmul(psB[u][:, j, 0:AW], onehot[:, u, j, :], rhs[:, u, j, :], start=True, stop=True)
            last.then_inc(scattered[u], 1)
        for u in range(U):
            slot = i * (G * U) + u * G
            blocks = slot_blocks(K, dve, ET.DVE, slot)
            add_visit(K, i, u, scattered[u], added, i * (U * G) + u * G + G + 1, K.acc, AW, psB[u], blocks)
    K.barrier()


class Sheet:

    def __init__(self, K, name):
        self.K, self.s = K, K.relay(name)

    def tt(self, out, a, b, op):
        self.s.step(self.K.dve, lambda: self.K.dve.tensor_tensor(out, a, b, op))

    def ts(self, out, a, x, y, op0, op1=None):
        self.s.step(self.K.dve, lambda: self.K.dve.tensor_scalar(out, a, x, y, op0, op1) if op1 is not None
                    else self.K.dve.tensor_scalar(out, a, x, None, op0))

    def stt(self, out, a, x, b, op0, op1):
        self.s.step(self.K.dve, lambda: self.K.dve.scalar_tensor_tensor(out, a, x, b, op0, op1))

    def sum(self, out, a):
        self.s.step(self.K.dve, lambda: self.K.dve.tensor_reduce(out, a, AX.X, ALU.add))

    def copy(self, out, a):
        self.s.step(self.K.dve, lambda: self.K.dve.tensor_copy(out, a))

    def act(self, out, a, func, **kw):
        self.s.step(self.K.act, lambda: self.K.act.activation(out, a, func, **kw))

    def reciprocal(self, out, a):
        self.s.step(self.K.dve, lambda: self.K.dve.reciprocal(out, a))

    def center(self, x, small):
        self.sum(small, x)
        self.ts(small, small, 1.0 / F, None, ALU.mult)
        self.tt(x, x, wide(small), ALU.subtract)

    def layernorm(self, x, tmp, small, g=None, b=None):
        self.center(x, small)
        self.tt(tmp, x, x, ALU.mult)
        self.sum(small, tmp)
        self.ts(small, small, 1.0 / F, EPS, ALU.mult, ALU.add)
        self.act(small, small, ACT.Sqrt)
        self.reciprocal(small, small)
        self.tt(x, x, wide(small), ALU.mult)
        if g is not None:
            self.tt(x, x, by_column(g), ALU.mult)
            self.tt(x, x, by_column(b), ALU.add)


def wide(small):
    return small.unsqueeze(2).broadcast_to([P, NB, F])


def by_column(vector):
    return vector.unsqueeze(1).broadcast_to([P, NB, F])


def heads(x):
    return x.unsqueeze(3).broadcast_to([P, NB, H, C])


def attention_out(K, layer):
    dve, act, sp, pe, pool = K.dve, K.act, K.sp, K.pe, K.pool
    S, d = Sheet(K, f"attend{layer}"), K.dmas(f"attend{layer}_dma")
    acc = K.acc
    xs, out = table(K.RA, F), table(K.RL, F)
    res, tmp = table(K.RA, F, NB * F), table(K.RL, F, NB * F)
    small = K.RF[:, NB * AW:NB * AW + 6 * NB * H].rearrange("p (k b h) -> p k b h", k=6, h=H)
    self_logit, m_edge, m_all, w_edge, w_self, den = (small[:, k, :, :] for k in range(6))
    row = K.node_small[:, 0, :]
    if layer == 1:
        d.done(sp.dma_start(xs, rows(K.rows1)[:, :, F:2 * F]))
        d.done(sp.dma_start(res, rows(K.h0)))
        hs = K.hidden_total
        S.s.step(dve, lambda: dve.tensor_reduce(hs[:, 0:2], K.hidden_sums[:, :, :], AX.X, ALU.add))
        S.act(hs[:, 2:3], K.b1rep[:, 0:1], ACT.Relu)
        S.ts(hs[:, 2:3], hs[:, 2:3], -float(SLOTS * P - E) / CH, None, ALU.mult)
        S.ts(hs[:, 3:4], hs[:, 0:1], hs[:, 1:2], None, ALU.add)
        S.ts(hs[:, 3:4], hs[:, 3:4], hs[:, 2:3], hs[:, 2:3], ALU.add, ALU.add)
        S.ts(hs[:, 3:4], hs[:, 3:4], 1.0 / E, None, ALU.mult)
        S.copy(K.hidden_mean[:, :], hs[:, 3:4].broadcast_to([P, P]))
        S.s.step(pe, lambda: pe.matmul(K.ps[:, 0, 0:2 * H], K.hidden_mean[:, :],
                                       K.Vrep[:, :, :].rearrange("p l h -> p (l h)"), start=True, stop=True))
        S.tt(K.loop_edge[:, :, :], K.ps[:, 0, 0:2 * H].rearrange("p (l h) -> p l h", h=H), K.crow[:, :, :], ALU.add)
        S.copy(K.count[:, :], acc[:, :, AW - 1])
    else:
        d.done(sp.dma_start(xs, rows(K.rows2)[:, :, 0:F]))
        d.done(sp.dma_start(res, rows(K.h1)))
    S.tt(self_logit, K.a_node[:, :, 0:H], K.a_node[:, :, H:2 * H], ALU.add)
    S.tt(self_logit, self_logit, K.loop_edge[:, layer - 1, :].unsqueeze(1).broadcast_to([P, NB, H]), ALU.add)
    S.stt(self_logit, self_logit, SLOPE, self_logit, ALU.mult, ALU.max)
    none = K.node_small[:, 1, :]
    S.ts(none, K.count[:, :], 0.5, -BIG, ALU.is_lt, ALU.mult)
    S.tt(m_edge, acc[:, :, F + H:F + 2 * H], none.unsqueeze(2).broadcast_to([P, NB, H]), ALU.add)
    S.tt(m_all, m_edge, self_logit, ALU.max)
    S.tt(w_edge, m_edge, m_all, ALU.subtract)
    S.act(w_edge, w_edge, ACT.Exp)
    S.tt(w_self, self_logit, m_all, ALU.subtract)
    S.act(w_self, w_self, ACT.Exp)
    S.tt(den, acc[:, :, F:F + H], w_edge, ALU.mult)
    S.tt(den, den, w_self, ALU.add)
    S.ts(den, den, 1e-16, None, ALU.add)
    S.reciprocal(den, den)
    S.tt(w_edge, w_edge, den, ALU.mult)
    S.tt(w_self, w_self, den, ALU.mult)
    by_head = lambda t: t.rearrange("p b (h c) -> p b h c", c=C)
    S.tt(by_head(out), by_head(acc[:, :, 0:F]), heads(w_edge), ALU.mult)
    d.after(dve)
    S.tt(by_head(xs), by_head(xs), heads(w_self), ALU.mult)
    S.tt(out, out, xs, ALU.add)
    S.tt(out, out, by_column(K.vec[f"L0_gnn_bias{layer}"]), ALU.add)
    S.ts(tmp, out, 0.0, None, ALU.min)
    S.act(tmp, tmp, ACT.Exp)
    S.ts(out, out, 0.0, None, ALU.max)
    S.stt(out, tmp, -1.0, out, ALU.add, ALU.add)
    S.tt(out, out, res, ALU.add)
    S.layernorm(out, tmp, row, K.vec[f"L0_gnn_g{layer}"], K.vec[f"L0_gnn_bn{layer}"])
    K.barrier()
    d.done(sp.dma_start(rows(K.h1 if layer == 1 else K.h2), out))
    if layer == 1:
        stage = table(K.RF, ROW2)

        def evacuate(b, ps):
            dve.tensor_copy(stage[:, b, :], ps[:, 0:ROW2])
            return dve.tensor_copy(K.a_node[:, b, :], ps[:, F:F + 2 * H])

        project(K, "second", [(out, K.W2[:, :])], F + 2 * H, evacuate)
        K.barrier()
        d.done(sp.dma_start(rows(K.rows2), stage))
        d.after(sp, pool)
        K.barrier()
        K.by_dst = table(K.RL, H)
        S.copy(K.by_dst, K.a_node[:, :, H:2 * H])
    d.after(sp)
    K.barrier()


def jump(K, D):
    dve, sp, pe, act = K.dve, K.sp, K.pe, K.act
    K.x1, K.prow = K.dram("x1", [NPAD, F]), K.dram("msg_rows", [NPAD, F])
    h0, h1 = table(K.RA, F), table(K.RA, F, NB * F)
    h2, x1 = table(K.RL, F), table(K.RL, F, NB * F)
    xin, tmp = table(K.RF, F), table(K.RF, F, NB * F)
    row = K.node_small[:, 0, :]
    S, d = Sheet(K, "jump"), K.dmas("jump_dma")
    S.s.step(K.pool, lambda: K.pool.memset(xin[:, NB - 1, :], 0.0))
    S.s.after(sp)
    for t, source in ((h0, K.h0), (h1, K.h1), (h2, K.h2)):
        d.done(sp.dma_start(t, rows(source)))
    load_x(K, D, xin, d)
    d.after(pe, dve)
    project(K, "jk", [(h0, K.JK[:, 0, :]), (h1, K.JK[:, 1, :]), (h2, K.JK[:, 2, :])], F,
            lambda b, ps: dve.tensor_tensor(x1[:, b, :], ps, xin[:, b, :], ALU.add))
    K.barrier()
    S.tt(x1, x1, by_column(K.vec["L0_gnn_jk_b"]), ALU.add)
    S.layernorm(x1, tmp, row)
    K.barrier()
    d.done(sp.dma_start(rows(K.x1), x1))
    pt, qt = table(K.RA, F), table(K.RL, F)

    def evacuate(b, ps):
        dve.tensor_copy(pt[:, b, :], ps[:, 0:F])
        return dve.tensor_tensor(qt[:, b, :], ps[:, F:2 * F], K.vec["L1_gnn_msg_b"], ALU.add)

    project(K, "msg", [(x1, K.WM[:, 0:2, :].rearrange("p s o -> p (s o)"))], 2 * F, evacuate)
    K.barrier()
    S.center(pt, row)
    S.center(qt, row)
    S.s.after(sp)
    d.done(sp.dma_start(rows(K.prow), pt))
    d.after(sp)
    K.by_dst = qt
    K.barrier()


def message_pass(K):
    nc, pool, act, pe, dve = K.nc, K.pool, K.act, K.pe, K.dve
    MW = F + 1
    K.acc = table(K.RF, MW)
    at = {"A": 0}
    def take(n):
        v = K.RA[:, at["A"]:at["A"] + n * U * G].rearrange("p (u g w) -> p u g w", u=U, g=G)
        at["A"] += n * U * G
        return v
    rowbuf, onehot, onehotW, onehotT, rhs, junk = take(F), take(P), take(P), take(P), take(MW), take(F)
    stat = K.RA[:, at["A"]:at["A"] + 2 * U * G].rearrange("p (k u g) -> p k u g", k=2, u=U)
    at["A"] += 2 * U * G
    minus_beta = K.RA[:, at["A"]:at["A"] + F]
    psT = [K.ps[:, u, :].rearrange("p (g e) -> p g e", g=G) for u in range(U)]
    psH = [K.ps[:, 2 + u, :].rearrange("p (g e) -> p g e", g=G) for u in range(U)]
    psB = [K.ps[:, 4 + 2 * u:6 + 2 * u, :].rearrange("p k (a w) -> p (k a) w", a=2) for u in range(U)]
    gather = Gather(K, "message", K.prow, F, rowbuf)
    (made, transposed, transpose_out, summed, squared, shifted, rooted, inverted, scaled, ready, scattered) = (
        [K.sem(f"message_{x}{u}") for u in range(U)] for x in
        ("onehot_made", "transposed", "transpose_out", "summed", "squared", "shifted", "rooted", "inverted",
         "scaled", "ready", "scattered"))
    added, init = K.sem("message_added"), K.relay("message_init")
    init.done(dve.memset(K.acc, 0.0))
    init.done(dve.memset(rhs[:, :, :, F:MW], 1.0))
    init.done(dve.tensor_scalar(minus_beta, K.vec["L1_gnn_msg_beta"], -1.0, None, ALU.mult))
    dve.sem_inc(added, 1 + G)
    for u in range(U):
        for sem in (transposed[u], transpose_out[u], summed[u], scaled[u], scattered[u]):
            dve.sem_inc(sem, 1)
    K.barrier()
    with nc.Fori(0, SLOTS // (G * U), engines=ENGINES) as i:
        for u in range(U):
            slot = i * (G * U) + u * G
            K.loop_wait(pool, summed[u], i + 1)
            gather.emit(i, u, slot)
            K.loop_wait(dve, transposed[u], i + 1)
            K.loop_wait(dve, scattered[u], i + 1)
            dve.tensor_tensor(onehot[:, u, :, :], K.iota[:, :].unsqueeze(1).broadcast_to([P, G, P]),
                              K.DL[:, bass.ds(slot, G)].unsqueeze(2).broadcast_to([P, G, P]),
                              ALU.is_equal).then_inc(made[u], 1)
            K.loop_wait(dve, made[u], i * 2 + 1)
            dve.tensor_tensor(onehotW[:, u, :, :], onehot[:, u, :, :],
                              K.WT[:, bass.ds(slot, G)].unsqueeze(2).broadcast_to([P, G, P]),
                              ALU.mult).then_inc(made[u], 1)
            K.loop_wait(pe, made[u], i * 2 + 2)
            K.loop_wait(pe, transpose_out[u], i + 1)
            for j in range(G):
                last = pe.transpose(psT[u][:, j, :], onehot[:, u, j, :], K.ident[:, :])
            last.then_inc(transposed[u], 1)
            K.loop_wait(act, transposed[u], i + 2)
            K.loop_wait(act, summed[u], i + 1)
            act.activation(onehotT[:, u, :, :], psT[u], ACT.Copy).then_inc(transpose_out[u], 1)
        for u in range(U):
            slot = i * (G * U) + u * G
            blocks = slot_blocks(K, pe, ET.PE, slot)
            K.loop_wait(pe, transpose_out[u], i + 2)
            K.loop_wait(pe, scaled[u], i + 1)
            gather.wait(pe, i, u)
            for j in range(G):
                pe.matmul(psH[u][:, j, :], onehotT[:, u, j, :],
                          K.by_dst[:, bass.ds(blocks[j], 1), :].rearrange("p b w -> p (b w)"), start=True, stop=False)
                last = pe.matmul(psH[u][:, j, :], K.ident[:, :], rowbuf[:, u, j, :], start=False, stop=True)
            last.then_inc(summed[u], 1)
            K.loop_wait(act, summed[u], i + 2)
            for j in range(G):
                last = act.activation(junk[:, u, j, :], psH[u][:, j, :], ACT.Square, accum_out=stat[:, 0, u, j:j + 1])
            last.then_inc(squared[u], 1)
            K.loop_wait(dve, squared[u], i + 1)
            dve.tensor_scalar(stat[:, 0, u, :], stat[:, 0, u, :], 1.0 / F, EPS, ALU.mult, ALU.add).then_inc(shifted[u], 1)
            K.loop_wait(act, shifted[u], i + 1)
            act.activation(stat[:, 1, u, :], stat[:, 0, u, :], ACT.Sqrt).then_inc(rooted[u], 1)
        for u in range(U):
            slot = i * (G * U) + u * G
            K.loop_wait(dve, rooted[u], i + 1)
            dve.reciprocal(stat[:, 1, u, :], stat[:, 1, u, :]).then_inc(inverted[u], 1)
            K.loop_wait(dve, inverted[u], i + 1)
            for j in range(G):
                last = dve.scalar_tensor_tensor(rhs[:, u, j, 0:F], psH[u][:, j, :], stat[:, 1, u, j:j + 1],
                                                K.vec["L1_gnn_msg_g"], ALU.mult, ALU.mult)
            last.then_inc(scaled[u], 1)
            K.loop_wait(dve, scaled[u], i + 2)
            dve.tensor_tensor(rhs[:, u, :, 0:F], rhs[:, u, :, 0:F], minus_beta.unsqueeze(1).broadcast_to([P, G, F]),
                              ALU.max).then_inc(ready[u], 1)
            K.loop_wait(pe, ready[u], i + 1)
            K.loop_wait(pe, added, i * (U * G) + (u + 1) * G - (U - 1) * G + 1)
            for j in range(G):
                last = pe.matmul(psB[u][:, j, 0:MW], onehotW[:, u, j, :], rhs[:, u, j, :], start=True, stop=True)
            last.then_inc(scattered[u], 1)
        for u in range(U):
            slot = i * (G * U) + u * G
            blocks = slot_blocks(K, dve, ET.DVE, slot)
            add_visit(K, i, u, scattered[u], added, i * (U * G) + u * G + G + 1, K.acc, MW, psB[u], blocks)
    K.barrier()


def update(K, D, out):
    dve, sp, pe, act = K.dve, K.sp, K.pe, K.act
    acc = K.acc
    x1, msg = table(K.RA, F), table(K.RA, F, NB * F)
    new, tmp = table(K.RL, F), table(K.RL, F, NB * F)
    S, d = Sheet(K, "update"), K.dmas("update_dma")
    row, gate = K.node_small[:, 0, :], K.node_small[:, 1, :]
    d.done(sp.dma_start(x1, rows(K.x1)))
    S.tt(msg, by_column(K.vec["L1_gnn_msg_beta"]), wide(acc[:, :, F]), ALU.mult)
    S.tt(msg, msg, acc[:, :, 0:F], ALU.add)
    S.ts(row, K.count[:, :], 1e-8, None, ALU.add)
    S.reciprocal(row, row)
    S.ts(gate, K.count[:, :], 0.0, None, ALU.is_gt)
    S.tt(row, row, gate, ALU.mult)
    S.tt(msg, msg, wide(row), ALU.mult)
    d.after(dve, pe)
    S.s.after(pe)
    project(K, "upd", [(x1, K.WM[:, 2, :]), (msg, K.WM[:, 3, :])], F,
            lambda b, ps: dve.tensor_tensor(new[:, b, :], ps, K.vec["L1_gnn_upd_b"], ALU.add))
    K.barrier()
    S.layernorm(new, tmp, row, K.vec["L1_gnn_upd_g"], K.vec["L1_gnn_upd_beta"])
    S.ts(new, new, 0.0, None, ALU.max)
    S.tt(tmp, x1, by_column(K.vec["gate_w_row"]), ALU.mult)
    S.sum(gate, tmp)
    S.act(gate, gate, ACT.Sigmoid, bias=K.gate_b[:, 0:1])
    S.tt(new, new, wide(gate), ALU.mult)
    S.ts(gate, gate, -1.0, 1.0, ALU.mult, ALU.add)
    S.tt(tmp, x1, wide(gate), ALU.mult)
    S.tt(new, new, tmp, ALU.add)
    S.tt(new, new, x1, ALU.add)
    S.layernorm(new, tmp, row)
    S.s.after(sp)
    cut = (NB - 1) * P
    d.done(sp.dma_start(out[0:cut, :].rearrange("(b p) w -> p b w", p=P), new[:, 0:NB - 1, :]))
    d.done(sp.dma_start(out[cut:N, :], new[0:LAST, NB - 1, :]))
    d.after(sp)


def graph_layers(nc, D, out, probe=None):
    with ExitStack() as ctx:
        K = Build(nc, ctx)
        K.RA, K.RL, K.RF = (K.sb("region_" + n, [P, REGION]) for n in "ALF")
        K.ps = ctx.enter_context(nc.psum_tensor("psum", [P, 8, 512], fp32))
        K.xT = K.sb("block_transposed", [P, 2, P])
        K.slot_index = K.sb("slot_index", [P, U, G], i32)
        K.node_small = K.sb("node_small", [P, 2, NB])
        K.count = K.sb("edge_count", [P, NB])
        K.hidden_sums = K.sb("hidden_sums", [P, 2, -(-KC // 4)])
        K.hidden_total = K.sb("hidden_total", [P, 4])
        K.hidden_mean = K.sb("hidden_mean", [P, P])
        K.loop_edge = K.sb("loop_edge", [P, 2, H])
        K.cols = K.sb("chunk_columns", [P, 8])
        K.rowbuf = K.RA[0:1, 10240:10240 + 7 * P].rearrange("a (k h c) -> a k h c", h=H, c=CH)
        K.rowbuf2 = K.RA[0:1, 11264:11264 + 4 * P].rearrange("a (k h c) -> a k h c", h=H, c=CH)
        K.rowflat = K.RA[0:1, 12288:12288 + P]
        K.penalty = K.RA[:, 0:-(-TC // 2)].bitcast(bf16)[:, 0:TC]
        K.spill = K.dram("xs_by_slot", [SLOTS // G, P, G * F])
        K.edge2 = K.dram("edge_alpha2", [P, TC])
        K.credit = K.dram("credit", [U, P])
        def run(stage, *args):
            with K.phase():
                stage(K, *args)

        run(load_weights, D)
        run(place_edges, D)
        run(nodes_in, D)
        for layer in (1, 2):
            run(logits_pass, layer)
            if layer == 1:
                run(edge_features)
            run(logits, layer)
            run(breaks, layer)
            run(segment_softmax, layer)
            run(weighted_sum, layer)
            run(attention_out, layer)
        run(jump, D)
        run(message_pass)
        run(update, D, out)


def kernel(**inputs):
    import numpy as _np
    import concourse.bacc as _bacc
    from concourse import mybir as _mybir
    from concourse.bass_utils import run_bass_kernel_spmd as _run

    given = {k: _np.asarray(v) for k, v in inputs.items()}
    for k in ("L0_gnn_lin_w1", "L0_gnn_lin_w2", "L0_gnn_in_w", "L0_gnn_jk_w", "L0_gnn_enc_w1"):
        given[k + "_T"] = given[k].T
    given["gate_w_row"] = given["L1_gnn_gate_w"].reshape(-1)
    unused = ("L0_gnn_in_w", "L0_gnn_jk_w", "L0_gnn_enc_w1", "L1_gnn_gate_w")
    nc = _bacc.Bacc("TRN2", target_bir_lowering=False, num_devices=1)
    arrays, D = {}, {}
    for name, a in given.items():
        if name in unused:
            continue
        a = _np.ascontiguousarray(a)
        arrays["in_" + name] = a
        D[name] = nc.dram_tensor("in_" + name, a.shape, _mybir.dt.from_np(a.dtype), kind="ExternalInput").ap()
    out = nc.dram_tensor("out_0", (N, F), _mybir.dt.float32, kind="ExternalOutput").ap()
    graph_layers(nc, D, out)
    r = _run(nc, [arrays], core_ids=[0])
    return r.results[0]["out_0"]
```

```python
import concourse.bass as bass
from concourse import mybir
from contextlib import ExitStack, contextmanager

P = 128
N, E, F = 6250, 200000, 128
H, C = 8, 16
HID = 16
NB = -(-N // P)
NPAD = NB * P
LAST = N - (NB - 1) * P
TILES = -(-E // P)
G = 4
U = 4
AHEAD = 3
CH = P // H
SLOTS = -(-(TILES + NB - 1) // (CH * 1)) * CH
while SLOTS % (G * U):
    SLOTS += CH
TURNS = SLOTS // (G * U)
SPARE = AHEAD * G
KC = SLOTS // CH
TC = KC * P
SC = -(-SLOTS // P)
EROWS = SLOTS - (NB - 1)
BIG = 1e30
EPS = 1e-5
SLOPE = 0.2
ROW1 = F + F + H + 1
ROW2 = F + H
DCOL1 = F + H + 1
AW = F + H + H + 1
RF_ = max(NB * ROW1, (SLOTS + SPARE) * H)
REGION = -(-RF_ // 64) * 64

fp32, bf16, i32, i16 = mybir.dt.float32, mybir.dt.bfloat16, mybir.dt.int32, mybir.dt.int16
ALU = mybir.AluOpType
ACT = mybir.ActivationFunctionType
AX = mybir.AxisListType
ET = mybir.EngineType
ENGINES = [ET.Pool, ET.Activation, ET.PE, ET.DVE, ET.SP]


class Relay:

    def __init__(self, sem, by=1):
        self.sem, self.by, self.n = sem, by, 0

    def after(self, *engines):
        for e in engines:
            if self.n:
                e.wait_ge(self.sem, self.n)

    def done(self, instruction):
        instruction.then_inc(self.sem, self.by)
        self.n += self.by

    def step(self, engine, emit):
        self.after(engine)
        self.done(emit())


class Build:

    def __init__(self, nc, ctx):
        self.nc, self.ctx, self.sems, self.used = nc, ctx, ctx, []
        self.pool, self.act, self.pe, self.dve, self.sp = nc.gpsimd, nc.scalar, nc.tensor, nc.vector, nc.sync
        self.tick = {e: self.sem("tick_" + n) for n, e in
                     (("pool", self.pool), ("act", self.act), ("pe", self.pe), ("dve", self.dve), ("sp", self.sp))}

        self.arrived = [self.sem(f"rows_arrived{u}") for u in range(U)]
        self.arrived_before = [0] * U

    def sb(self, name, shape, dt=fp32):
        return self.ctx.enter_context(self.nc.sbuf_tensor(name, shape, dt))

    def dram(self, name, shape, dt=fp32):
        return self.nc.dram_tensor(name, shape, dt, kind="Internal").ap()

    @contextmanager
    def phase(self):
        self.used = []
        with ExitStack() as self.sems:
            yield
            self.barrier()
            for s in self.used:
                self.pool.sem_clear(s)
        self.barrier()

    def sem(self, name):
        s = self.sems.enter_context(self.nc.semaphore(name))
        self.used.append(s)
        return s

    def relay(self, name):
        return Relay(self.sem(name))

    def dmas(self, name):
        return Relay(self.sem(name), 16)

    def loop_wait(self, engine, sem, i, per, plus):
        if isinstance(i, int):
            engine.wait_ge(sem, i * per + plus)
        else:
            key = (engine, per, plus)
            if key not in self.turn_values:
                self.turn_values[key] = engine.snap(i * per + plus)
            engine.wait_ge(sem, self.turn_values[key])
        engine.sem_inc(self.tick[engine], 1)

    @contextmanager
    def turns(self):
        with self.nc.Fori(0, TURNS, engines=ENGINES) as i:
            self.turn_values = {}
            yield i

    def barrier(self):
        self.nc.all_engine_barrier()


def table(region, width, at=0):
    return region[:, at:at + NB * width].rearrange("p (b w) -> p b w", w=width)


def rows(dram):
    return dram.rearrange("(b p) w -> p b w", p=P)


def load_weights(K, D):
    nc, pool, pe, dve, sp, act = K.nc, K.pool, K.pe, K.dve, K.sp, K.act
    K.ident = K.sb("ident", [P, P])
    K.iota = K.sb("iota", [P, P])
    K.ones = K.sb("ones", [P, P])
    K.ident_bf = K.sb("ident_bf", [P, P], bf16)
    K.W1 = K.sb("W_node1", [P, F + 2 * H + F])
    K.W2 = K.sb("W_node2", [P, F + 2 * H])
    K.JK = K.sb("W_jk", [P, 3, F])
    K.WM = K.sb("W_msg_upd", [P, 4, F])
    names = ["L0_gnn_bias1", "L0_gnn_g1", "L0_gnn_bn1", "L0_gnn_in_b", "L0_gnn_bias2", "L0_gnn_g2", "L0_gnn_bn2",
             "L0_gnn_jk_b", "L1_gnn_msg_b", "L1_gnn_msg_g", "L1_gnn_msg_beta", "L1_gnn_upd_b", "L1_gnn_upd_g",
             "L1_gnn_upd_beta", "gate_w_row"]
    K.vecs = K.sb("vectors", [P, len(names), F])
    K.vec = {n: K.vecs[:, k, :] for k, n in enumerate(names)}
    K.gate_b = K.sb("gate_b", [P, 1])
    K.Wbd = K.sb("enc_w1_diag", [4 * CH, 2, P])
    K.b1rep = K.sb("enc_b1_rep", [P, 1])
    K.Vbd = K.sb("edge_alpha_diag", [P, 2, 2, P])
    K.Vrep = K.sb("edge_alpha_rep", [P, 2, H])
    K.ccol = K.sb("edge_alpha_const_col", [P, 2])
    K.crow = K.sb("edge_alpha_const_row", [P, 2, H])
    R = K.RA
    att = R[:, 0:6 * H].rearrange("p (m h) -> p m h", h=H)
    lin = R[:, 64:64 + 2 * F].rearrange("p (m f) -> p m f", f=F)
    edge = R[:, 320:320 + 2 * H].rearrange("p (m f) -> p m f", f=H)
    encw2 = R[0:H, 340:340 + HID]
    encb2 = R[0:H, 360:361]
    We = R[0:H, 368:368 + 2 * H].rearrange("p (m f) -> p m f", f=H)
    WeR = R[0:H, 400:400 + 2 * P].rearrange("p (m f) -> p m f", f=P)
    b2R = R[0:H, 660:660 + P]
    V = R[0:HID, 800:800 + 2 * H].rearrange("p (m f) -> p m f", f=H)

    made, loads, folded = K.relay("const_made"), K.dmas("weights_in"), K.relay("folded")
    made.done(pool.memset(K.ident[:, :], 0.0))
    made.done(pool.memset(K.ones[:, :], 1.0))
    made.done(pool.iota(K.iota[:, :], [[1, P]], base=0, channel_multiplier=0, allow_small_or_imprecise_dtypes=True))
    made.step(pool, lambda: pool.affine_select(out=K.ident[:, :], in_=K.ident[:, :], compare_op=ALU.not_equal,
                                               fill=1.0, base=0, pattern=[[-1, P]], channel_multiplier=1))
    zeroed = K.relay("diagonals_zeroed")
    zeroed.done(dve.memset(att, 0.0))
    zeroed.done(dve.memset(K.Wbd[:, :, :], 0.0))
    zeroed.done(dve.memset(K.Vbd[:, :, :, :], 0.0))
    zeroed.after(sp, act)

    queue = [sp, act]

    def load(dst, src):
        queue.reverse()
        loads.done(queue[0].dma_start(dst, src))

    for l in (1, 2):
        lw = f"L0_gnn_lin_w{l}"
        load((K.W1 if l == 1 else K.W2)[:, 0:F], D[lw + "_T"])
        load(lin[:, l - 1, :], D[lw])
        load(edge[:, l - 1, :], D[f"L0_gnn_lin_edge_w{l}"])
        for k, what in enumerate(("src", "dst", "edge")):
            for h in range(H):
                load(att[C * h:C * h + C, 3 * (l - 1) + k, h:h + 1],
                     D[f"L0_gnn_att_{what}{l}"][h:h + 1, :].rearrange("a c -> c a"))
    load(K.W1[:, F + 2 * H:], D["L0_gnn_in_w_T"])
    load(K.JK[:, :, :], D["L0_gnn_jk_w_T"].rearrange("(s f) o -> f s o", s=3))
    load(K.WM[:, 0:2, :], D["L1_gnn_msg_w"].rearrange("(s f) o -> f s o", s=2))
    load(K.WM[:, 2:4, :], D["L1_gnn_upd_w"].rearrange("(s f) o -> f s o", s=2))
    for n in names:
        load(K.vec[n], D[n].rearrange("(a f) -> a f", a=1).broadcast_to([P, F]))
    load(K.gate_b[:, :], D["L1_gnn_gate_b"].rearrange("(a f) -> a f", a=1).broadcast_to([P, 1]))
    load(encw2, D["L0_gnn_enc_w2"])
    load(encb2, D["L0_gnn_enc_b2"].rearrange("(a f) -> a f", f=1))
    for c in range(CH):
        q, d = divmod(c, CH // 2)
        load(K.Wbd[4 * c:4 * c + 4, q, HID * d:HID * d + HID], D["L0_gnn_enc_w1_T"])
    for d in range(CH // 2):
        load(K.b1rep[HID * d:HID * d + HID, :], D["L0_gnn_enc_b1"].rearrange("(a f) -> a f", f=1))
    loads.after(pe, dve)
    made.after(pe, dve)
    folded.done(dve.tensor_copy(K.ident_bf[:, :], K.ident[:, :]))
    ps = K.ps
    for l in (0, 1):
        W = (K.W1, K.W2)[l]
        folded.step(pe, lambda: pe.matmul(ps[:, 0, 0:H], lin[:, l, :], att[:, 3 * l, :], start=True, stop=True))
        folded.step(pe, lambda: pe.matmul(ps[:, 1, 0:H], lin[:, l, :], att[:, 3 * l + 1, :], start=True, stop=True))
        folded.step(pe, lambda: pe.matmul(ps[0:H, 2, 0:H], edge[:, l, :], att[:, 3 * l + 2, :], start=True, stop=True))
        folded.step(dve, lambda: dve.tensor_copy(W[:, F:F + 2 * H].rearrange("p (m h) -> p m h", h=H), ps[:, 0:2, 0:H]))
        folded.step(dve, lambda: dve.tensor_copy(We[:, l, :], ps[0:H, 2, 0:H]))
        folded.step(dve, lambda: dve.tensor_copy(
            WeR[:, l, :].rearrange("p (c h) -> p c h", h=H), We[:, l, :].unsqueeze(1).broadcast_to([H, CH, H])))
        folded.step(dve, lambda: dve.tensor_copy(b2R, encb2.broadcast_to([H, P])))
        folded.step(pe, lambda: pe.matmul(ps[0:HID, 3, 0:H], encw2, We[:, l, :], start=True, stop=True))
        folded.step(pe, lambda: pe.matmul(ps[:, 4, 0:1], WeR[:, l, :], encb2, start=True, stop=True))
        folded.step(pe, lambda: pe.matmul(ps[:, 5, 0:H], b2R, We[:, l, :], start=True, stop=True))
        folded.step(dve, lambda: dve.tensor_copy(V[:, l, :], ps[0:HID, 3, 0:H]))
        folded.step(dve, lambda: dve.tensor_copy(K.ccol[:, l:l + 1], ps[:, 4, 0:1]))
        folded.step(dve, lambda: dve.tensor_copy(K.crow[:, l, :], ps[:, 5, 0:H]))
    folded.after(sp, act)
    for l in (0, 1):
        for c in range(CH):
            q, d = divmod(c, CH // 2)
            load(K.Vbd[HID * d:HID * d + HID, l, q, H * c:H * c + H], V[:, l, :])
        for d in range(CH // 2):
            load(K.Vrep[HID * d:HID * d + HID, l, :], V[:, l, :])
    for v in range(AHEAD):
        load(K.spill[SLOTS // G + v, :, :], K.vecs[:, 0:G, :].rearrange("p g f -> p (g f)"))
    loads.after(sp)


def place_edges(K, D):
    nc, pool, pe, dve, sp, act = K.nc, K.pool, K.pe, K.dve, K.sp, K.act
    K.SRC = K.sb("slot_src", [P, SLOTS + SPARE], i32)
    K.DL = K.sb("slot_local_dst", [P, SLOTS + SPARE])
    K.KEY = K.sb("slot_key", [P, SLOTS])
    K.WT = K.sb("slot_weight", [P, SLOTS + SPARE])
    K.BLK = K.sb("slot_block", [1, SLOTS + SPARE], i16)
    edge_rows = K.dram("edge_rows", [EROWS, 3, P], i32)
    blk_dram = K.dram("slot_block_dram", [SC * P], i16)

    pad = K.RL[0:EROWS - TILES + 1, 0:3 * P].bitcast(i32).rearrange("p (a e) -> p a e", a=3)
    lasts_i = K.RL[:, 512:512 + SC].bitcast(i32)
    lasts = K.RL[:, 544:544 + SC]
    limits = K.RL[:, 576:576 + NB - 1]
    whole = K.RL[:, 1024:1024 + (NB - 1) * SC].rearrange("p (b c) -> p b c", c=SC)
    below = K.RL[:, 4000:4000 + NB - 1]
    thresh = K.RL[:, 4200:4200 + NB - 1]
    sidx = K.RL[:, 4300:4300 + SC]
    blk = K.RL[:, 4320:4320 + SC]
    blk_i = K.RL[:, 4340:4340 + SC].bitcast(i16)[:, 0:SC]
    tile_f = K.RL[:, 4360:4360 + SC]
    tile_i = K.RL[:, 4380:4380 + SC].bitcast(i32)
    blk128 = K.RL[:, 4400:4400 + SC]
    junk = K.RL[:, 4500:4500 + NB - 1]
    erow = K.RF[:, 0:SC * 3 * P].rearrange("p (c a e) -> p c a e", a=3, e=P)
    erow_flat = K.RF[:, 0:SC * 3 * P].rearrange("p (c w) -> p c w", w=3 * P).bitcast(i32)
    SW = SC * P
    srcf = K.RA[:, 0:SW].rearrange("p (c e) -> p c e", e=P)
    dstf = K.RA[:, SW:2 * SW].rearrange("p (c e) -> p c e", e=P)
    local = K.RA[:, 2 * SW:3 * SW].rearrange("p (c e) -> p c e", e=P)
    valid = K.RA[:, 3 * SW:4 * SW].rearrange("p (c e) -> p c e", e=P)

    m, d, g = K.relay("place_steps"), K.dmas("place_dmas"), Relay(K.arrived[0], 16)
    filled = K.relay("pad_filled")
    FT = E // P
    filled.done(pool.memset(lasts_i[:, FT // P:SC], 1 << 23))
    filled.done(pool.memset(K.SRC[:, SLOTS:], 0))
    filled.done(pool.memset(K.DL[:, SLOTS:], -1.0))
    filled.done(pool.memset(K.WT[:, SLOTS:], 0.0))
    filled.done(pool.memset(K.BLK[:, SLOTS:], 0))
    filled.done(pool.memset(pad[:, 0, :], 0))
    filled.done(pool.memset(pad[:, 1, :], -1))
    filled.done(pool.memset(pad[:, 2, :], 0))
    full = (TILES - 1) * P
    for a, name in enumerate(("src", "dst", "edge_weight")):
        flat = D[name] if name != "edge_weight" else D[name].bitcast(i32)
        d.done(sp.dma_start(edge_rows[0:TILES - 1, a, :], flat[0:full].rearrange("(t e) -> t e", e=P)))
        d.done(act.dma_start(edge_rows[TILES - 1:TILES, a, 0:E - full], flat[full:E].rearrange("(t e) -> t e", t=1)))
    last_dst = D["dst"][0:FT * P].rearrange("(t e) -> t e", e=P)[:, P - 1:P]
    filled.after(sp, act)
    with nc.allow_non_contiguous_dma("one destination of every tile"):
        d.done(sp.dma_start(lasts_i[:, 0:FT // P], last_dst[0:FT // P * P, :].rearrange("(c p) a -> p (c a)", p=P)))
        d.done(sp.dma_start(lasts_i[0:FT % P, FT // P:SC], last_dst[FT // P * P:FT, :]))
    if E - full < P:
        d.done(act.dma_start(edge_rows[TILES - 1:TILES, :, E - full:P], pad[0:1, :, E - full:P]))
    d.done(act.dma_start(edge_rows[TILES:EROWS, :, :], pad[1:EROWS - TILES + 1, :, :]))
    filled.done(pool.iota(sidx, [[P, SC]], base=0, channel_multiplier=1, allow_small_or_imprecise_dtypes=True))
    d.after(dve)
    filled.after(dve)
    m.step(dve, lambda: dve.tensor_copy(lasts, lasts_i))
    m.step(dve, lambda: dve.tensor_scalar(limits, K.iota[:, 1:NB], float(P), None, ALU.mult))
    m.step(dve, lambda: dve.tensor_tensor(whole, lasts.unsqueeze(1).broadcast_to([P, NB - 1, SC]),
                                          limits.unsqueeze(2).broadcast_to([P, NB - 1, SC]), ALU.is_lt))
    m.step(dve, lambda: dve.tensor_reduce(below, whole, AX.X, ALU.add))
    m.step(pe, lambda: pe.matmul(K.ps[:, 0, 0:NB - 1], K.ones[:, :], below, start=True, stop=True))
    m.step(dve, lambda: dve.tensor_tensor(thresh, K.ps[:, 0, 0:NB - 1], K.iota[:, 1:NB], ALU.add))
    for c in range(SC):
        m.step(dve, lambda: dve.tensor_scalar(junk, thresh, sidx[:, c:c + 1], 0.0, ALU.is_le, ALU.add,
                                              accum_out=blk[:, c:c + 1]))
    m.step(dve, lambda: dve.tensor_tensor(tile_f, sidx, blk, ALU.subtract))
    m.step(dve, lambda: dve.tensor_scalar(tile_f, tile_f, float(EROWS - 1), None, ALU.min))
    m.step(dve, lambda: dve.tensor_copy(tile_i, tile_f))
    m.step(dve, lambda: dve.tensor_copy(blk_i, blk))
    m.step(dve, lambda: dve.tensor_scalar(blk128, blk, float(P), None, ALU.mult))
    m.after(pool, sp)
    with nc.allow_non_contiguous_dma("block of each slot, once"):
        d.done(sp.dma_start(blk_dram.rearrange("(c p) -> p c", p=P), blk_i))
    d.after(pool, sp)
    d.done(sp.dma_start(K.BLK[:, 0:SLOTS], blk_dram[0:SLOTS].rearrange("(a s) -> a s", a=1)))
    for c in range(SC):
        g.done(pool.indirect_dma_start(out=erow_flat[:, c, :], out_offset=None,
                                       in_=edge_rows.rearrange("t a e -> t (a e)"),
                                       in_offset=bass.IndirectOffsetOnAxis(ap=tile_i[:, c:c + 1], axis=0)))
    g.after(dve, act, pe)
    K.arrived_before[0] += g.n
    m.step(act, lambda: act.activation(srcf, erow[:, :, 0, :].bitcast(i32), ACT.Copy))
    m.step(dve, lambda: dve.tensor_copy(dstf, erow[:, :, 1, :].bitcast(i32)))
    m.step(dve, lambda: dve.tensor_tensor(local, dstf, blk128.unsqueeze(2).broadcast_to([P, SC, P]), ALU.subtract))
    m.step(dve, lambda: dve.tensor_scalar(valid, local, 0.0, None, ALU.is_ge))
    m.step(dve, lambda: dve.scalar_tensor_tensor(valid, local, float(P), valid, ALU.is_lt, ALU.mult))
    m.step(dve, lambda: dve.scalar_tensor_tensor(local, local, 1.0, valid, ALU.add, ALU.mult))
    m.step(dve, lambda: dve.tensor_scalar(local, local, -1.0, None, ALU.add))
    m.step(dve, lambda: dve.scalar_tensor_tensor(dstf, dstf, 1.0, valid, ALU.add, ALU.mult))
    m.step(dve, lambda: dve.tensor_scalar(dstf, dstf, -1.0, None, ALU.add))
    n = 0
    for out, source in ((K.SRC, srcf), (K.DL, local), (K.KEY, dstf), (K.WT, erow[:, :, 2, :])):
        for c0 in range(0, SC, 4):
            cs = range(c0, min(c0 + 4, SC))
            w = min(SLOTS, (cs[-1] + 1) * P) - c0 * P
            m.after(pe)
            for c in cs:
                last = pe.transpose(K.ps[:, n % 8, (c - c0) * P:(c - c0 + 1) * P], source[:, c, :], K.ident[:, :])
            m.done(last)
            m.step(dve, lambda: dve.tensor_copy(out[:, c0 * P:c0 * P + w], K.ps[:, n % 8, 0:w]))
            n += 1
    d.after(sp)
    K.barrier()


def project(K, name, sources, width, evacuate):
    pe, act, dve = K.pe, K.act, K.dve
    transposed, copied = K.relay(name + "_transposed"), K.relay(name + "_copied")
    multiplied, evacuated = K.relay(name + "_multiplied"), K.relay(name + "_evacuated")
    units = [(b, k) for b in range(NB) for k in range(len(sources))]

    def transpose(q):
        b, k = units[q]
        if q >= 2:
            pe.wait_ge(copied.sem, q - 1)
        transposed.done(pe.transpose(K.ps[:, q % 2, 0:P], sources[k][0][:, b, :], K.ident[:, :]))
        act.wait_ge(transposed.sem, q + 1)
        if q >= 2:
            act.wait_ge(multiplied.sem, q - 1)
        copied.done(act.activation(K.xT[:, q % 2, :], K.ps[:, q % 2, 0:P], ACT.Copy))

    transpose(0)
    for q, (b, k) in enumerate(units):
        if q + 1 < len(units):
            transpose(q + 1)
        pe.wait_ge(copied.sem, q + 1)
        if k == 0 and b >= 2:
            pe.wait_ge(evacuated.sem, b - 1)
        multiplied.done(pe.matmul(K.ps[:, 2 + b % 2, 0:width], K.xT[:, q % 2, :], sources[k][1],
                                  start=k == 0, stop=k == len(sources) - 1))
        if k == len(sources) - 1:
            dve.wait_ge(multiplied.sem, q + 1)
            evacuated.done(evacuate(b, K.ps[:, 2 + b % 2, 0:width]))


def nodes_in(K, D):
    dve, sp, act, pool = K.dve, K.sp, K.act, K.pool
    K.rows1, K.h0, K.h1 = K.dram("rows1", [NPAD, ROW1]), K.dram("h0", [NPAD, F]), K.dram("h1", [NPAD, F])
    K.rows2, K.h2 = K.dram("rows2", [NPAD, ROW2]), K.dram("h2", [NPAD, F])
    K.a_node = K.sb("a_src_a_dst", [P, NB, 2 * H])
    K.by_dst = table(K.RL, DCOL1)
    stage, h0 = table(K.RA, ROW1), table(K.RF, F)
    square = table(K.RF, F)
    s, d = K.relay("nodes_in_steps"), K.dmas("nodes_in_dmas")
    s.done(pool.memset(K.by_dst[:, NB - 1, :], 0.0))
    s.after(sp)
    load_x(K, D, K.by_dst[:, :, 0:F], d)
    d.after(K.pe, dve)

    def evacuate(b, ps):
        dve.tensor_copy(stage[:, b, F:2 * F + H], ps[:, 0:F + H])
        dve.tensor_copy(K.a_node[:, b, :], ps[:, F:F + 2 * H])
        return dve.tensor_tensor(h0[:, b, :], ps[:, F + 2 * H:], K.vec["L0_gnn_in_b"], ALU.add)

    project(K, "in", [(K.by_dst[:, :, 0:F], K.W1[:, :])], F + 2 * H + F, evacuate)
    K.barrier()
    d.done(sp.dma_start(rows(K.h0), h0))
    s.step(dve, lambda: dve.tensor_copy(stage[:, :, 0:F], K.by_dst[:, :, 0:F]))
    s.step(dve, lambda: dve.tensor_copy(K.by_dst[:, :, F:F + H], K.a_node[:, :, H:2 * H]))
    d.after(dve)
    s.step(dve, lambda: dve.tensor_tensor(square, K.by_dst[:, :, 0:F], K.by_dst[:, :, 0:F], ALU.mult))
    s.step(dve, lambda: dve.tensor_reduce(stage[:, :, ROW1 - 1], square, AX.X, ALU.add))
    s.step(dve, lambda: dve.tensor_copy(K.by_dst[:, :, DCOL1 - 1], stage[:, :, ROW1 - 1]))
    s.after(sp)
    d.done(sp.dma_start(rows(K.rows1), stage))
    d.after(sp)
    K.barrier()


def load_x(K, D, out, relay):
    cut = (NB - 1) * P
    relay.done(K.sp.dma_start(out[:, 0:NB - 1, :], D["x"][0:cut, :].rearrange("(b p) w -> p b w", p=P)))
    relay.done(K.sp.dma_start(out[0:LAST, NB - 1, :], D["x"][cut:N, :]))


class Event:

    def __init__(self, K, name):
        self.K, self.sems = K, [K.sem(f"{name}{u}") for u in range(U)]
        for sem in self.sems:
            K.dve.sem_inc(sem, 1)

    def at(self, v):
        return self.sems[v % U]

    def wait(self, engine, i, v):
        self.K.loop_wait(engine, self.at(v), i, 1, v // U + 2)


class DmaEvent:

    def __init__(self, K, sems, each, before):
        self.K, self.sems, self.each, self.before = K, sems, 16 * each, before

    def at(self, v):
        return self.sems[v % U]

    def wait(self, engine, i, v):
        self.K.loop_wait(engine, self.at(v), i, self.each, (v // U + 1) * self.each + self.before[v % U])


def slots_of(i, v):
    return bass.ds(i * (G * U) + v * G, G)


def slot_of(i, v, j):
    return bass.ds(i * (G * U) + (v * G + j), 1)


def fresh_dma_event(K, name, each):
    sems = [K.sem(f"{name}{u}") for u in range(U)]
    for u in range(U):
        for _ in range(each):
            K.sp.dma_start(K.credit[u:u + 1, :], K.ident[0:1, 0:P]).then_inc(sems[u], 16)
            K.sp.wait_ge(sems[u], 16)
    return DmaEvent(K, sems, each, [16 * each] * U)


class Gather:

    def __init__(self, K, name, source, buffer, freed, extra):
        self.K, self.source, self.buffer, self.freed = K, source, buffer, freed
        self.picked, self.picking = Event(K, name + "_indices_picked"), freed[0]
        self.arrived = DmaEvent(K, K.arrived, G, list(K.arrived_before))
        for u in range(U):
            K.arrived_before[u] += 16 * G * (TURNS + (1 if u < extra else 0))

    def pick(self, i, v, first=False):
        if not first:
            self.picking.wait(self.K.pool, i, v - U)
        self.K.pool.tensor_copy(self.K.slot_index[:, v % U, :], self.K.SRC[:, slots_of(i, v)]
                                ).then_inc(self.picked.at(v), 1)

    def emit(self, i, v):
        K, pool = self.K, self.K.pool
        for event in self.freed:
            event.wait(pool, i, v - U)
        self.picked.wait(pool, i, v)
        for j in range(G):
            pool.indirect_dma_start(out=self.buffer[:, v % U, j, :], out_offset=None, in_=self.source,
                                    in_offset=bass.IndirectOffsetOnAxis(ap=K.slot_index[:, v % U, j:j + 1], axis=0)
                                    ).then_inc(self.arrived.at(v), 16)
        self.pick(i, v + 1)


class OneHots:

    def __init__(self, K, name, onehot, onehotT, psT, used, weighted=None, scattered=None):
        self.K, self.onehot, self.onehotT, self.psT = K, onehot, onehotT, psT
        self.used, self.weighted, self.scattered = used, weighted, scattered
        self.made, self.transposed, self.out = (Event(K, f"{name}_onehot_{x}") for x in ("made", "transposed", "transposed_out"))
        self.weights_in = Event(K, name + "_onehot_weighted") if weighted is not None else None

    def make(self, i, v):
        K, dve, act = self.K, self.K.dve, self.K.act
        self.transposed.wait(dve, i, v - U)
        if self.weighted is not None:
            self.weights_in.wait(dve, i, v - U)
        dve.tensor_tensor(self.onehot[:, v % U, :, :], K.iota[:, :].unsqueeze(1).broadcast_to([P, G, P]),
                          K.DL[:, slots_of(i, v)].unsqueeze(2).broadcast_to([P, G, P]),
                          ALU.is_equal).then_inc(self.made.at(v), 1)

    def weight(self, i, v):
        K, act = self.K, self.K.act
        self.scattered.wait(act, i, v - U)
        self.made.wait(act, i, v)
        for j in range(G):
            last = act.activation(self.weighted[:, v % U, j, :], self.onehot[:, v % U, j, :], ACT.Copy,
                                  scale=K.WT[:, slot_of(i, v, j)])
        last.then_inc(self.weights_in.at(v), 1)

    def transpose(self, i, v):
        K, pe, act = self.K, self.K.pe, self.K.act
        self.made.wait(pe, i, v)
        self.out.wait(pe, i, v - 2)
        for j in range(G):
            last = pe.transpose(self.psT[v % 2][:, j, :], self.onehot[:, v % U, j, :], K.ident_bf[:, :])
        last.then_inc(self.transposed.at(v), 1)
        self.transposed.wait(act, i, v)
        self.used.wait(act, i, v - U)
        act.activation(self.onehotT[:, v % U, :, :], self.psT[v % 2], ACT.Copy).then_inc(self.out.at(v), 1)


def pieces(region, at, *specs):
    out = []
    for w, dtype in specs:
        cols = U * G * w // (2 if dtype is bf16 else 1)
        v = region[:, at:at + cols]
        v = v.bitcast(bf16) if dtype is bf16 else v
        out.append(v.rearrange("p (u g w) -> p u g w", u=U, g=G))
        at += cols
    assert at <= REGION
    return out


def turn_values(K, kind, entries, most, i, per, visits=U):
    where = slice(0, per * visits) if isinstance(i, int) else bass.ds(i * (per * U), per * visits)
    _, values = K.nc.values_load_multi_w_load_instructions(
        entries[0:1, where], engines=[kind], min_val=0, max_val=most,
        skip_runtime_bounds_check_because="a slot's block counts the 48 block starts passed, one more at most in each slot")
    return lambda v, j: values[v * per + j]


def turn_blocks(K, kind, i, visits=U):
    return turn_values(K, kind, K.BLK, NB - 1, i, G, visits)


def logits_pass(K, layer):
    pe, dve, sp = K.pe, K.dve, K.sp
    first = layer == 1
    row, dcol = (ROW1, DCOL1) if first else (ROW2, H)
    xs0, as0 = (F, 2 * F) if first else (0, F)
    d0 = F if first else 0
    onehot, onehotT = pieces(K.RL, NB * DCOL1, (P, bf16), (P, None))
    rowbuf, junk = pieces(K.RF, SLOTS * 4, (row, None), (F, bf16))
    dots = K.dots
    asum = K.RA[:, 0:SLOTS * H].rearrange("p (s h) -> p s h", h=H)
    feat = K.RF[:, 0:SLOTS * 4].rearrange("p (s f) -> p s f", f=4)
    psT = [K.ps[:, b, 0:G * P // 2].bitcast(bf16).rearrange("p (g e) -> p g e", g=G) for b in range(2)]
    psX = [K.ps[:, 2 + 2 * b:4 + 2 * b, :].rearrange("p k (a w) -> p (k a) w", a=2) for b in range(2)]
    n = f"logits{layer}"
    selected, dotted, consumed = (Event(K, f"{n}_{x}") for x in ("selected", "dotted", "consumed"))
    spilled = fresh_dma_event(K, n + "_spilled", 1)
    gather = Gather(K, n, K.rows1 if first else K.rows2, rowbuf, [consumed, spilled], 0)
    ones = OneHots(K, n, onehot, onehotT, psT, selected)
    K.barrier()
    gather.pick(0, 0, True)
    for v in range(AHEAD):
        ones.make(0, v)
        ones.transpose(0, v)
    with K.turns() as i:
        blocks = turn_blocks(K, ET.PE, i)
        for v in range(U):
            gather.emit(i, v)
            gather.arrived.wait(sp, i, v)
            sp.dma_start(K.spill[bass.ds(i * U + v, 1), :, :].rearrange("a p (g w) -> (a p) g w", g=G),
                         rowbuf[:, v, :, xs0:xs0 + F]).then_inc(spilled.at(v), 16)
            ones.out.wait(pe, i, v)
            consumed.wait(pe, i, v - 2)
            for j in range(G):
                last = pe.matmul(psX[v % 2][:, j, 0:dcol], onehotT[:, v, j, :],
                                 K.by_dst[:, bass.ds(blocks(v, j), 1), 0:dcol].rearrange("p b w -> p (b w)"),
                                 start=True, stop=True)
            last.then_inc(selected.at(v), 1)
            ones.make(i, v + AHEAD)
            ones.transpose(i, v + AHEAD)
            selected.wait(dve, i, v)
            gather.arrived.wait(dve, i, v)
            X = psX[v % 2]
            if first:
                for j in range(G):
                    last = dve.tensor_tensor_reduce(out=junk[:, v, j, :], in0=rowbuf[:, v, j, 0:F], in1=X[:, j, 0:F],
                                                    scale=1.0, scalar=0.0, op0=ALU.mult, op1=ALU.add,
                                                    accum_out=dots[:, v, j:j + 1])
                last.then_inc(dotted.at(v), 1)
                dve.tensor_copy(feat[:, slots_of(i, v), 2:3], rowbuf[:, v, :, ROW1 - 1:ROW1])
                dve.tensor_copy(feat[:, slots_of(i, v), 3:4], X[:, :, DCOL1 - 1:DCOL1])
                dotted.wait(dve, i, v)
                dve.tensor_copy(feat[:, slots_of(i, v), 0:1], dots[:, v, :].unsqueeze(2))
            dve.tensor_tensor(asum[:, slots_of(i, v), :], rowbuf[:, v, :, as0:as0 + H], X[:, :, d0:d0 + H],
                              ALU.add).then_inc(consumed.at(v), 1)
    for v in range(U):
        sp.wait_ge(spilled.at(v), 16 + 16 * TURNS)


def chunked(region, width):
    return region[:, 0:SLOTS * width].rearrange("p (c k w) -> p k c w", k=KC, w=width)


def edge_features(K):
    dve = K.dve
    feat = K.RF[:, 0:SLOTS * 4].rearrange("p (s f) -> p s f", f=4)
    valid = K.RF[:, SLOTS * 4:SLOTS * 5]
    s = K.relay("features")
    s.step(dve, lambda: dve.tensor_scalar(valid, K.DL[:, 0:SLOTS], 0.0, None, ALU.is_ge))
    s.step(dve, lambda: dve.tensor_tensor(feat[:, :, 1], feat[:, :, 2], feat[:, :, 3], ALU.add))
    s.step(dve, lambda: dve.scalar_tensor_tensor(feat[:, :, 1], feat[:, :, 0], -2.0, feat[:, :, 1], ALU.mult, ALU.add))
    s.step(dve, lambda: dve.tensor_tensor(feat, feat, valid.unsqueeze(2).broadcast_to([P, SLOTS, 4]), ALU.mult))
    K.barrier()


def logits(K, layer):
    act, pe, dve, sp, pool = K.act, K.pe, K.dve, K.sp, K.pool
    L = K.RL
    first = layer == 1
    feat, asum = chunked(K.RF, 4), chunked(K.RA, H)
    at = SLOTS * 4
    def take(n):
        nonlocal at
        at += n
        return K.RF[:, at - n:at]
    W = 4 * P
    featT, hidden, raw, edge2 = take(2 * W), take(4 * W), take(2 * W), take(2 * W)
    sum_packed = take(8 * P).rearrange("p (z k w) -> p z k w", z=2, w=P)
    feat_packed = K.xT[:, :, :].rearrange("p u (k w) -> p (u k) w", w=4 * CH)
    assert at <= REGION
    n = f"softmax_in{layer}_"
    packed = K.relay(n + "packed")
    ftr, fcp, hid_mm, hid_out = (K.relay(n + x) for x in ("features_transposed", "features_out", "hidden_product", "hidden_out"))
    lg_mm, e2_mm, biased, done, e2_out = (K.relay(n + x) for x in ("logit_product", "edge2_product", "biased", "done", "edge2_out"))
    io = [K.dmas(n + f"edge2_dma{z}") for z in range(2)]
    for z, k0 in enumerate(range(0, KC, 4)):
        ks = range(k0, min(k0 + 4, KC))
        w = len(ks) * P
        half = (z % 2) * W
        if z >= 2:
            pool.wait_ge(lg_mm.sem, z - 1)
        split = lambda t, w: t.rearrange("p k (c w) -> p k c w", w=w)
        if first:
            if z >= 1:
                pool.wait_ge(ftr.sem, z)
            pool.tensor_copy(split(feat_packed[:, 0:len(ks), :], 4), feat[:, k0:k0 + len(ks), :, :])
        packed.done(pool.tensor_copy(split(sum_packed[:, z % 2, 0:len(ks), :], H), asum[:, k0:k0 + len(ks), :, :]))
        pe.wait_ge(packed.sem, z + 1)
        if first:
            if z >= 1:
                pe.wait_ge(fcp.sem, z)
            for k in ks:
                last = pe.transpose(K.ps[0:4 * CH, 0, (k - k0) * P:(k - k0 + 1) * P], feat_packed[:, k - k0, :], K.ident[:, :])
            ftr.done(last)
            act.wait_ge(ftr.sem, z + 1)
            if z >= 2:
                act.wait_ge(hid_mm.sem, 2 * (z - 1))
            fcp.done(act.activation(featT[0:4 * CH, half:half + w], K.ps[0:4 * CH, 0, 0:w], ACT.Copy))
            for q in (0, 1):
                pe.wait_ge(fcp.sem, z + 1)
                if z >= 1:
                    pe.wait_ge(hid_out.sem, 2 * (z - 1) + q + 1)
                hid_mm.done(pe.matmul(K.ps[:, 1 + q, 0:w], K.Wbd[:, q, :], featT[0:4 * CH, half:half + w], start=True, stop=True))
                act.wait_ge(hid_mm.sem, 2 * z + q + 1)
                if z >= 2:
                    act.wait_ge(e2_mm.sem, z - 1)
                hid_out.done(act.activation(hidden[:, 2 * half + q * W:2 * half + q * W + w], K.ps[:, 1 + q, 0:w], ACT.Relu,
                                            bias=K.b1rep[:, 0:1], accum_out=K.hidden_sums[:, q, z:z + 1]))
            pe.wait_ge(hid_out.sem, 2 * z + 2)
        if z >= 2:
            pe.wait_ge(biased.sem, z - 1)
        bank = 3 + z % 2
        if first:
            for q in (0, 1):
                pe.matmul(K.ps[:, bank, 0:w], K.Vbd[:, 0, q, :], hidden[:, 2 * half + q * W:2 * half + q * W + w],
                          start=q == 0, stop=False, skip_group_check=True)
        for k in ks:
            last = pe.matmul(K.ps[:, bank, (k - k0) * P:(k - k0 + 1) * P], sum_packed[:, z % 2, k - k0, :], K.ident[:, :],
                             start=not first, stop=True, skip_group_check=True)
        lg_mm.done(last)
        if first:
            if z >= 2:
                pe.wait_ge(e2_out.sem, z - 1)
            for q in (0, 1):
                last = pe.matmul(K.ps[:, 5 + z % 2, 0:w], K.Vbd[:, 1, q, :], hidden[:, 2 * half + q * W:2 * half + q * W + w],
                                 start=q == 0, stop=q == 1)
            e2_mm.done(last)
        dve.wait_ge(lg_mm.sem, z + 1)
        if first:
            biased.done(dve.tensor_scalar(raw[:, half:half + w], K.ps[:, bank, 0:w], K.ccol[:, 0:1], None, ALU.add))
            act.wait_ge(e2_mm.sem, z + 1)
            if z >= 2:
                io[z % 2].after(act)
            e2_out.done(act.activation(edge2[:, half:half + w], K.ps[:, 5 + z % 2, 0:w], ACT.Identity, bias=K.ccol[:, 1:2]))
            sp.wait_ge(e2_out.sem, z + 1)
            io[z % 2].done(sp.dma_start(K.edge2[:, k0 * P:k0 * P + w], edge2[:, half:half + w]))
        else:
            if z >= 2:
                sp.wait_ge(biased.sem, z - 1)
            io[z % 2].done(sp.dma_start(edge2[:, half:half + w], K.edge2[:, k0 * P:k0 * P + w]))
            io[z % 2].after(dve)
            biased.done(dve.tensor_tensor(raw[:, half:half + w], K.ps[:, bank, 0:w], edge2[:, half:half + w], ALU.add))
        dve.wait_ge(biased.sem, z + 1)
        done.done(dve.scalar_tensor_tensor(L[:, k0 * P:k0 * P + w], raw[:, half:half + w], SLOPE, raw[:, half:half + w],
                                           ALU.mult, ALU.max))
    for r in io:
        r.after(sp)
    K.barrier()


def breaks(K, layer):
    act, pe, dve = K.act, K.pe, K.dve
    n = f"breaks{layer}_"
    tr, cp, s = K.relay(n + "transposed"), K.relay(n + "copied"), K.relay(n + "steps")
    keys = K.RF[:, 0:TC]
    pen = K.penalty
    rep = K.RA[:, 8192:8192 + 2 * 4 * P].rearrange("p (z c h) -> p z c h", z=8, h=H)
    kview = chunked(K.KEY, 1)
    for k in range(KC):
        if k >= 8:
            dve.wait_ge(tr.sem, k - 7)
        s.done(dve.tensor_copy(rep[:, k % 8, :, :], kview[:, k, :, :].broadcast_to([P, CH, H])))
        pe.wait_ge(s.sem, k + 1)
        if k >= 8:
            pe.wait_ge(cp.sem, k - 7)
        tr.done(pe.transpose(K.ps[:, k % 8, 0:P], rep[:, k % 8, :, :].rearrange("p c h -> p (c h)"), K.ident[:, :]))
        act.wait_ge(tr.sem, k + 1)
        cp.done(act.activation(keys[:, k * P:(k + 1) * P], K.ps[:, k % 8, 0:P], ACT.Copy))
    K.barrier()
    s.step(dve, lambda: dve.memset(pen[:, 0:1], 0.0))
    s.step(dve, lambda: dve.tensor_tensor(pen[:, 1:TC], keys[:, 1:TC], keys[:, 0:TC - 1], ALU.not_equal))
    s.step(dve, lambda: dve.tensor_scalar(pen[:, 1:TC], pen[:, 1:TC], -BIG, None, ALU.mult))
    cols, R = K.cols, K.rowbuf
    s.step(dve, lambda: dve.tensor_reduce(cols[:, 0:1], pen, AX.X, ALU.min))
    s.step(dve, lambda: dve.tensor_scalar(cols[:, 0:1], cols[:, 0:1], 0.0, None, ALU.is_ge))
    s.step(dve, lambda: dve.tensor_copy(cols[:, 1:2], keys[:, 0:1]))
    s.step(dve, lambda: dve.tensor_copy(cols[:, 2:3], keys[:, TC - 1:TC]))
    rows_of(K, s, [(0, 0, False), (1, 1, False), (2, 2, False)])
    whole, first, last = (R[0:1, k, :, :] for k in range(3))
    goes = R[0:1, 3, :, :]
    s.step(dve, lambda: dve.memset(R[0:1, 3:7, :, :], 0.0))
    s.step(dve, lambda: dve.tensor_tensor(goes[:, :, 1:CH], first[:, :, 1:CH], last[:, :, 0:CH - 1], ALU.is_equal))
    M = K.rowbuf2
    s.step(dve, lambda: dve.tensor_tensor(M[0:1, 0, :, :], whole, goes, ALU.mult))
    s.step(dve, lambda: dve.tensor_copy(M[0:1, 1, :, :], goes))
    s.step(dve, lambda: dve.memset(M[0:1, 2:4, :, :], 0.0))
    s.step(dve, lambda: dve.tensor_copy(M[0:1, 3, :, 1:CH], goes[:, :, CH - 1:0:-1]))
    s.step(dve, lambda: dve.tensor_tensor(M[0:1, 2, :, 1:CH], M[0:1, 3, :, 1:CH], whole[:, :, CH - 2::-1], ALU.mult))
    s.step(dve, lambda: dve.tensor_scalar(M[0:1, :, :, :], M[0:1, :, :, :], BIG, -BIG, ALU.mult, ALU.add))
    s.step(dve, lambda: dve.tensor_copy(R[0:1, 4, :, :], goes))
    columns_of(K, s, [(4, 3, False)])
    K.barrier()


def rows_of(K, s, moves):
    for col, row, mirrored in moves:
        s.step(K.pe, lambda: K.pe.matmul(K.ps[0:1, 0, 0:P], K.cols[:, col:col + 1], K.ident[:, :], start=True, stop=True))
        source = K.ps[0:1, 0, 0:P].rearrange("a (c h) -> a h c", h=H)
        s.step(K.dve, lambda: K.dve.tensor_copy(K.rowbuf[0:1, row, :, :], source[:, :, ::-1] if mirrored else source))


def columns_of(K, s, moves):
    flat = K.rowflat
    for row, col, mirrored in moves:
        source = K.rowbuf[0:1, row, :, :]
        s.step(K.dve, lambda: K.dve.tensor_copy(flat[0:1, :].rearrange("a (c h) -> a h c", h=H),
                                                source[:, :, ::-1] if mirrored else source))
        s.step(K.pe, lambda: K.pe.matmul(K.ps[:, 1, 0:1], flat[0:1, :], K.ones[0:1, 0:1], start=True, stop=True))
        s.step(K.dve, lambda: K.dve.tensor_copy(K.cols[:, col:col + 1], K.ps[:, 1, 0:1]))


def segment_softmax(K, layer):
    act, pe, dve = K.act, K.pe, K.dve
    n = f"softmax{layer}_"
    s = K.relay(n + "steps")
    L, M, pen, cols, R, Z = K.RL[:, 0:TC], K.RF[:, 0:TC], K.penalty, K.cols, K.rowbuf, K.rowbuf2

    def chain(col_in, z, mirrored, col_out):
        rows_of(K, s, [(col_in, 0, mirrored)])
        flat = lambda r: r.rearrange("a h c -> a (h c)")
        s.step(dve, lambda: dve.tensor_tensor_scan(out=flat(R[0:1, 1, :, :]), data0=flat(Z[0:1, z, :, :]),
                                                   data1=flat(R[0:1, 0, :, :]), initial=-BIG, op0=ALU.add, op1=ALU.max))
        s.step(dve, lambda: dve.memset(R[0:1, 2, :, :], -BIG))
        s.step(dve, lambda: dve.tensor_tensor(R[0:1, 2, :, 1:CH], R[0:1, 1, :, 0:CH - 1], Z[0:1, z + 1, :, 1:CH], ALU.add))
        columns_of(K, s, [(2, col_out, mirrored)])

    def scan(out, data, back, initial):
        if not back:
            return dve.tensor_tensor_scan(out=out, data0=pen, data1=data, initial=initial, op0=ALU.add, op1=ALU.max)
        return dve.tensor_tensor_scan(out=out[:, TC - 2::-1], data0=pen[:, TC - 1:0:-1], data1=data[:, TC - 2::-1],
                                      initial=initial, op0=ALU.add, op1=ALU.max)

    s.step(dve, lambda: scan(M, L, False, -BIG))
    s.step(dve, lambda: dve.tensor_copy(cols[:, 4:5], M[:, TC - 1:TC]))
    chain(4, 0, False, 5)
    s.step(dve, lambda: scan(M, L, False, cols[:, 5:6]))
    s.step(dve, lambda: dve.tensor_copy(cols[:, 6:7], M[:, TC - 1:TC]))
    s.step(dve, lambda: scan(M, M, True, cols[:, 6:7]))
    s.step(dve, lambda: dve.tensor_copy(cols[:, 4:5], M[:, 0:1]))
    chain(4, 2, True, 5)
    s.step(dve, lambda: dve.tensor_tensor(cols[:, 6:7], M[:, TC - 1:TC], cols[:, 5:6], ALU.max))
    s.step(dve, lambda: dve.tensor_copy(M[:, TC - 1:TC], cols[:, 6:7]))
    s.step(dve, lambda: scan(M, M, True, cols[:, 6:7]))
    s.step(dve, lambda: dve.tensor_tensor(L, L, M, ALU.subtract))
    s.step(act, lambda: act.activation(L, L, ACT.Exp))
    s.step(dve, lambda: dve.scalar_tensor_tensor(M[:, 1:TC], pen[:, 1:TC], 0.0, M[:, 1:TC], ALU.is_lt, ALU.mult))
    s.step(dve, lambda: dve.tensor_scalar(cols[:, 7:8], cols[:, 3:4], -1.0, 1.0, ALU.mult, ALU.add))
    s.step(dve, lambda: dve.tensor_tensor(M[:, 0:1], M[:, 0:1], cols[:, 7:8], ALU.mult))
    K.barrier()
    for what, source, out in (("weights", L, chunked(K.RA, H)), ("maxima", M, chunked(K.RL, H))):
        tr, ev = K.relay(n + what + "_transposed"), K.relay(n + what + "_out")
        for z, k0 in enumerate(range(0, KC, 4)):
            ks = range(k0, min(k0 + 4, KC))
            if z >= 4:
                pe.wait_ge(ev.sem, z - 3)
            for k in ks:
                last = pe.transpose(K.ps[:, z % 4, (k - k0) * P:(k - k0 + 1) * P], source[:, k * P:(k + 1) * P], K.ident[:, :])
            tr.done(last)
            dve.wait_ge(tr.sem, z + 1)
            ev.done(dve.tensor_copy(out[:, k0:k0 + len(ks), :, :],
                                    K.ps[:, z % 4, 0:len(ks) * P].rearrange("p (k c h) -> p k c h", c=CH, h=H)))
        K.barrier()


class Adder:

    def __init__(self, K, name, acc, psum, scattered, parts, span=1):
        self.K, self.acc, self.psum, self.scattered, self.parts, self.span = K, acc, psum, scattered, parts, span
        self.added = [Event(K, f"{name}_added{j}_") for j in range(parts)]

    def emit(self, i, v, j, block):
        K, dve = self.K, self.K.dve
        if j == 0:
            self.scattered.wait(dve, i, v)
        self.added[j - 1].wait(dve, i, v if j else v - 1)
        row = self.acc[:, bass.ds(block, self.span), :].rearrange("p b w -> p (b w)")
        dve.tensor_tensor(row, row, self.psum(v, j), ALU.add).then_inc(self.added[j].at(v), 1)


def weighted_sum(K, layer):
    pool, act, pe, dve, sp = K.pool, K.act, K.pe, K.dve, K.sp
    acc = K.RF[:, 0:(NB + 1) * AW].rearrange("p (b w) -> p b w", w=AW)
    K.acc = acc[:, 0:NB, :]
    onehot, rhs = pieces(K.RF, (NB + 1) * AW, (P, None), (AW, None))
    zero = K.RF[0:1, REGION - P:REGION].bitcast(bf16)
    pair_block, pair_step = (K.RF[0:1, REGION - P - (k + 1) * SLOTS // 4:REGION - P - k * SLOTS // 4].bitcast(i16) for k in (0, 1))
    assert (NB + 1) * AW + U * G * (P + AW) <= REGION - P - SLOTS // 2
    weight, top = (R[:, 0:(SLOTS + SPARE) * H].rearrange("p (s h) -> p s h", h=H) for R in (K.RA, K.RL))
    PAIRS = G // 2
    psB = lambda v, k: K.ps[:, (v % 2) * PAIRS + k, 0:2 * AW]
    n = f"sum{layer}_"
    made, copied, weighted, scattered = (Event(K, n + x) for x in ("onehot_made", "columns_copied", "weighted", "scattered"))
    loaded = DmaEvent(K, [K.sem(f"{n}xs_loaded{u}") for u in range(U)], 1, [0] * U)
    adder = Adder(K, n, acc, psB, scattered, PAIRS, 2)
    init = K.relay(n + "init")
    init.done(dve.memset(acc, 0.0))
    init.done(dve.memset(zero, 0.0))
    pairs = K.BLK[:, 0:SLOTS].rearrange("a (k two) -> a k two", two=2)
    init.done(dve.tensor_copy(pair_block, pairs[:, :, 0]))
    init.step(dve, lambda: dve.tensor_tensor(pair_step, pairs[:, :, 1], pairs[:, :, 0], ALU.subtract))
    init.step(dve, lambda: dve.tensor_scalar(pair_step, pair_step, float(AW), None, ALU.mult))
    init.done(dve.memset(rhs[:, :, :, AW - 1:AW], 1.0))
    init.done(dve.memset(weight[:, SLOTS:, :], 0.0))
    init.done(dve.memset(top[:, SLOTS:, :], 0.0))
    K.barrier()

    def one_hots(i, v, js):
        if js[0] == 0:
            scattered.wait(dve, i, v - U)
        first = i * (G * U) + (v * G + js[0])
        last = dve.tensor_tensor(onehot[:, v % U, js[0]:js[-1] + 1, :],
                                 K.iota[:, :].unsqueeze(1).broadcast_to([P, len(js), P]),
                                 K.DL[:, bass.ds(first, len(js))].unsqueeze(2).broadcast_to([P, len(js), P]), ALU.is_equal)
        if js[-1] == G - 1:
            last.then_inc(made.at(v), 1)

    def prepare(i, v):
        b = v % U
        at = bass.ds(i * U + v, 1) if not isinstance(i, int) else slice(v, v + 1)
        scattered.wait(sp, i, v - U)
        sp.dma_start(rhs[:, b, :, 0:F], K.spill[at, :, :].rearrange("a p (g w) -> (a p) g w", g=G)
                     ).then_inc(loaded.at(v), 16)
        scattered.wait(act, i, v - U)
        act.activation(rhs[:, b, :, F:F + H], weight[:, slots_of(i, v), :], ACT.Copy)
        act.activation(rhs[:, b, :, F + H:F + 2 * H], top[:, slots_of(i, v), :], ACT.Copy).then_inc(copied.at(v), 1)
        loaded.wait(pool, i, v)
        rows_ = rhs[:, b, :, 0:F].rearrange("p g (h c) -> p g h c", c=C)
        pool.tensor_tensor(rows_, rows_, weight[:, slots_of(i, v), :].unsqueeze(3).broadcast_to([P, G, H, C]),
                           ALU.mult).then_inc(weighted.at(v), 1)

    for v in range(AHEAD):
        one_hots(0, v, range(G))
        prepare(0, v)
    with K.turns() as i:
        blocks = turn_values(K, ET.DVE, pair_block, NB - 1, i, PAIRS)
        steps = turn_values(K, ET.PE, pair_step, AW, i, PAIRS)
        for v in range(U):
            for event in (made, copied, weighted):
                event.wait(pe, i, v)
            adder.added[-1].wait(pe, i, v - 2)
            for k in range(PAIRS):
                sums = psB(v, k)
                pe.matmul(sums[:, AW:2 * AW], zero[:, 0:P], zero[:, 0:AW], start=True, stop=False, skip_group_check=True)
                pe.matmul(sums[:, 0:AW], onehot[:, v, 2 * k, :], rhs[:, v, 2 * k, :], start=True, stop=False,
                          skip_group_check=True)
                last = pe.matmul(K.ps[:, (v % 2) * PAIRS + k, bass.ds(steps(v, k), AW)], onehot[:, v, 2 * k + 1, :],
                                 rhs[:, v, 2 * k + 1, :], start=False, stop=True, skip_group_check=True)
            last.then_inc(scattered.at(v), 1)
            prepare(i, v + AHEAD)
            for k in range(PAIRS):
                one_hots(i, v + AHEAD, [2 * k, 2 * k + 1])
                adder.emit(i, v, k, blocks(v, k))
    for v in range(AHEAD):
        sp.wait_ge(loaded.at(v), 16 * (TURNS + 1))


class Sheet:

    def __init__(self, K, name):
        self.K, self.s = K, K.relay(name)

    def tt(self, out, a, b, op):
        self.s.step(self.K.dve, lambda: self.K.dve.tensor_tensor(out, a, b, op))

    def ts(self, out, a, x, y, op0, op1=None):
        self.s.step(self.K.dve, lambda: self.K.dve.tensor_scalar(out, a, x, y, op0, op1) if op1 is not None
                    else self.K.dve.tensor_scalar(out, a, x, None, op0))

    def stt(self, out, a, x, b, op0, op1):
        self.s.step(self.K.dve, lambda: self.K.dve.scalar_tensor_tensor(out, a, x, b, op0, op1))

    def sum(self, out, a):
        self.s.step(self.K.dve, lambda: self.K.dve.tensor_reduce(out, a, AX.X, ALU.add))

    def copy(self, out, a):
        self.s.step(self.K.dve, lambda: self.K.dve.tensor_copy(out, a))

    def act(self, out, a, func, **kw):
        self.s.step(self.K.act, lambda: self.K.act.activation(out, a, func, **kw))

    def reciprocal(self, out, a):
        self.s.step(self.K.dve, lambda: self.K.dve.reciprocal(out, a))

    def center(self, x, small):
        self.sum(small, x)
        self.ts(small, small, 1.0 / F, None, ALU.mult)
        self.tt(x, x, wide(small), ALU.subtract)

    def layernorm(self, x, tmp, small, g=None, b=None):
        self.center(x, small)
        self.tt(tmp, x, x, ALU.mult)
        self.sum(small, tmp)
        self.ts(small, small, 1.0 / F, EPS, ALU.mult, ALU.add)
        self.act(small, small, ACT.Sqrt)
        self.reciprocal(small, small)
        self.tt(x, x, wide(small), ALU.mult)
        if g is not None:
            self.tt(x, x, by_column(g), ALU.mult)
            self.tt(x, x, by_column(b), ALU.add)


def wide(small):
    return small.unsqueeze(2).broadcast_to([P, NB, F])


def by_column(vector):
    return vector.unsqueeze(1).broadcast_to([P, NB, F])


def heads(x):
    return x.unsqueeze(3).broadcast_to([P, NB, H, C])


def attention_out(K, layer):
    dve, act, sp, pe, pool = K.dve, K.act, K.sp, K.pe, K.pool
    S, d = Sheet(K, f"attend{layer}"), K.dmas(f"attend{layer}_dma")
    acc = K.acc
    xs, out = table(K.RA, F), table(K.RL, F)
    res, tmp = table(K.RA, F, NB * F), table(K.RL, F, NB * F)
    small = K.RF[:, NB * AW:NB * AW + 6 * NB * H].rearrange("p (k b h) -> p k b h", k=6, h=H)
    self_logit, m_edge, m_all, w_edge, w_self, den = (small[:, k, :, :] for k in range(6))
    row = K.node_small[:, 0, :]
    if layer == 1:
        d.done(sp.dma_start(xs, rows(K.rows1)[:, :, F:2 * F]))
        d.done(sp.dma_start(res, rows(K.h0)))
        hs = K.hidden_total
        S.s.step(dve, lambda: dve.tensor_reduce(hs[:, 0:2], K.hidden_sums[:, :, :], AX.X, ALU.add))
        S.act(hs[:, 2:3], K.b1rep[:, 0:1], ACT.Relu)
        S.ts(hs[:, 2:3], hs[:, 2:3], -float(SLOTS * P - E) / CH, None, ALU.mult)
        S.ts(hs[:, 3:4], hs[:, 0:1], hs[:, 1:2], None, ALU.add)
        S.ts(hs[:, 3:4], hs[:, 3:4], hs[:, 2:3], hs[:, 2:3], ALU.add, ALU.add)
        S.ts(hs[:, 3:4], hs[:, 3:4], 1.0 / E, None, ALU.mult)
        S.copy(K.hidden_mean[:, :], hs[:, 3:4].broadcast_to([P, P]))
        S.s.step(pe, lambda: pe.matmul(K.ps[:, 0, 0:2 * H], K.hidden_mean[:, :],
                                       K.Vrep[:, :, :].rearrange("p l h -> p (l h)"), start=True, stop=True))
        S.tt(K.loop_edge[:, :, :], K.ps[:, 0, 0:2 * H].rearrange("p (l h) -> p l h", h=H), K.crow[:, :, :], ALU.add)
        S.copy(K.count[:, :], acc[:, :, AW - 1])
    else:
        d.done(sp.dma_start(xs, rows(K.rows2)[:, :, 0:F]))
        d.done(sp.dma_start(res, rows(K.h1)))
    S.tt(self_logit, K.a_node[:, :, 0:H], K.a_node[:, :, H:2 * H], ALU.add)
    S.tt(self_logit, self_logit, K.loop_edge[:, layer - 1, :].unsqueeze(1).broadcast_to([P, NB, H]), ALU.add)
    S.stt(self_logit, self_logit, SLOPE, self_logit, ALU.mult, ALU.max)
    none = K.node_small[:, 1, :]
    S.ts(none, K.count[:, :], 0.5, -BIG, ALU.is_lt, ALU.mult)
    S.tt(m_edge, acc[:, :, F + H:F + 2 * H], none.unsqueeze(2).broadcast_to([P, NB, H]), ALU.add)
    S.tt(m_all, m_edge, self_logit, ALU.max)
    S.tt(w_edge, m_edge, m_all, ALU.subtract)
    S.act(w_edge, w_edge, ACT.Exp)
    S.tt(w_self, self_logit, m_all, ALU.subtract)
    S.act(w_self, w_self, ACT.Exp)
    S.tt(den, acc[:, :, F:F + H], w_edge, ALU.mult)
    S.tt(den, den, w_self, ALU.add)
    S.ts(den, den, 1e-16, None, ALU.add)
    S.reciprocal(den, den)
    S.tt(w_edge, w_edge, den, ALU.mult)
    S.tt(w_self, w_self, den, ALU.mult)
    by_head = lambda t: t.rearrange("p b (h c) -> p b h c", c=C)
    S.tt(by_head(out), by_head(acc[:, :, 0:F]), heads(w_edge), ALU.mult)
    d.after(dve)
    S.tt(by_head(xs), by_head(xs), heads(w_self), ALU.mult)
    S.tt(out, out, xs, ALU.add)
    S.tt(out, out, by_column(K.vec[f"L0_gnn_bias{layer}"]), ALU.add)
    S.ts(tmp, out, 0.0, None, ALU.min)
    S.act(tmp, tmp, ACT.Exp)
    S.ts(out, out, 0.0, None, ALU.max)
    S.stt(out, tmp, -1.0, out, ALU.add, ALU.add)
    S.tt(out, out, res, ALU.add)
    S.layernorm(out, tmp, row, K.vec[f"L0_gnn_g{layer}"], K.vec[f"L0_gnn_bn{layer}"])
    K.barrier()
    d.done(sp.dma_start(rows(K.h1 if layer == 1 else K.h2), out))
    if layer == 1:
        stage = table(K.RF, ROW2)

        def evacuate(b, ps):
            dve.tensor_copy(stage[:, b, :], ps[:, 0:ROW2])
            return dve.tensor_copy(K.a_node[:, b, :], ps[:, F:F + 2 * H])

        project(K, "second", [(out, K.W2[:, :])], F + 2 * H, evacuate)
        K.barrier()
        d.done(sp.dma_start(rows(K.rows2), stage))
        d.after(sp, pool)
        K.barrier()
        K.by_dst = table(K.RL, H)
        S.copy(K.by_dst, K.a_node[:, :, H:2 * H])
    d.after(sp)
    K.barrier()


def jump(K, D):
    dve, sp, pe, act = K.dve, K.sp, K.pe, K.act
    K.x1, K.prow = K.dram("x1", [NPAD, F]), K.dram("msg_rows", [NPAD, 3 * F], bf16)
    h0, h1 = table(K.RA, F), table(K.RA, F, NB * F)
    h2, x1 = table(K.RL, F), table(K.RL, F, NB * F)
    xin, tmp = table(K.RF, F), table(K.RF, F, NB * F)
    row = K.node_small[:, 0, :]
    S, d = Sheet(K, "jump"), K.dmas("jump_dma")
    S.s.step(K.pool, lambda: K.pool.memset(xin[:, NB - 1, :], 0.0))
    S.s.after(sp)
    for t, source in ((h0, K.h0), (h1, K.h1), (h2, K.h2)):
        d.done(sp.dma_start(t, rows(source)))
    load_x(K, D, xin, d)
    d.after(pe, dve)
    project(K, "jk", [(h0, K.JK[:, 0, :]), (h1, K.JK[:, 1, :]), (h2, K.JK[:, 2, :])], F,
            lambda b, ps: dve.tensor_tensor(x1[:, b, :], ps, xin[:, b, :], ALU.add))
    K.barrier()
    S.tt(x1, x1, by_column(K.vec["L0_gnn_jk_b"]), ALU.add)
    S.layernorm(x1, tmp, row)
    K.barrier()
    d.done(sp.dma_start(rows(K.x1), x1))
    pt, qt = table(K.RA, F), table(K.RL, F)

    def evacuate(b, ps):
        dve.tensor_copy(pt[:, b, :], ps[:, 0:F])
        return dve.tensor_tensor(qt[:, b, :], ps[:, F:2 * F], K.vec["L1_gnn_msg_b"], ALU.add)

    project(K, "msg", [(x1, K.WM[:, 0:2, :].rearrange("p s o -> p (s o)"))], 2 * F, evacuate)
    K.barrier()
    S.center(pt, row)
    S.center(qt, row)
    parts = K.RF[:, 0:NB * 3 * F // 2].bitcast(bf16).rearrange("p (b k f) -> p b k f", k=3, f=F)
    for part in range(3):
        S.copy(parts[:, :, part, :], pt)
        if part < 2:
            S.tt(pt, pt, parts[:, :, part, :], ALU.subtract)
    S.s.after(sp)
    d.done(sp.dma_start(rows(K.prow), parts.rearrange("p b k f -> p b (k f)")))
    d.after(sp)
    K.by_dst = qt
    K.barrier()


def message_pass(K):
    pool, act, pe, dve = K.pool, K.act, K.pe, K.dve
    MW = F + 1
    K.acc = table(K.RF, MW)
    rowbuf, onehot, onehotW, onehotT, rhs = pieces(K.RA, 0, (3 * F, bf16), (P, bf16), (P, None), (P, None), (MW, None))
    (junk,) = pieces(K.RL, NB * F, (F, bf16))
    minus_beta, eps = K.RL[:, 9000:9000 + F], K.RL[:, 9200:9201]
    squares = K.RL[:, 9300:9300 + U * G].rearrange("p (u g) -> p u g", u=U)
    rstd = K.RL[:, 9400:9400 + U * G].rearrange("p (u g) -> p u g", u=U)
    psT = [K.ps[:, b, 0:G * P // 2].bitcast(bf16).rearrange("p (g e) -> p g e", g=G) for b in range(2)]
    psH = [K.ps[:, 2 + b, :].rearrange("p (g e) -> p g e", g=G) for b in range(2)]
    psB = [K.ps[:, 4 + 2 * b:6 + 2 * b, :].rearrange("p k (a w) -> p (k a) w", a=2) for b in range(2)]
    summed, squared, rooted, inverted, scaled, ready, scattered = (
        Event(K, "message_" + x) for x in ("summed", "squared", "rooted", "inverted", "scaled", "ready", "scattered"))
    gather = Gather(K, "message", K.prow, rowbuf, [summed], 2)
    ones = OneHots(K, "message", onehot, onehotT, psT, summed, onehotW, scattered)
    adder = Adder(K, "message", K.acc, lambda v, j: psB[v % 2][:, j, 0:MW], scattered, G)
    init = K.relay("message_init")
    init.done(dve.memset(K.acc, 0.0))
    init.done(dve.memset(rhs[:, :, :, F:MW], 1.0))
    init.done(dve.memset(eps, EPS))
    init.done(dve.tensor_scalar(minus_beta, K.vec["L1_gnn_msg_beta"], -1.0, None, ALU.mult))
    K.barrier()

    def sums(i, v, blocks):
        b = v % U
        gather.emit(i, v)
        ones.out.wait(pe, i, v)
        scaled.wait(pe, i, v - 2)
        gather.arrived.wait(pe, i, v)
        for j in range(G):
            pe.matmul(psH[v % 2][:, j, :], onehotT[:, b, j, :],
                      K.by_dst[:, bass.ds(blocks(v, j), 1), :].rearrange("p b w -> p (b w)"), start=True, stop=False)
            for part in range(3):
                last = pe.matmul(psH[v % 2][:, j, :], K.ident_bf[:, :], rowbuf[:, b, j, part * F:(part + 1) * F],
                                 start=False, stop=part == 2)
        last.then_inc(summed.at(v), 1)
        summed.wait(act, i, v)
        scaled.wait(act, i, v - U)
        for j in range(G):
            last = act.activation(junk[:, b, j, :], psH[v % 2][:, j, :], ACT.Square, accum_out=squares[:, b, j:j + 1])
        last.then_inc(squared.at(v), 1)
        squared.wait(act, i, v)
        act.activation(rstd[:, b, :], squares[:, b, :], ACT.Sqrt, bias=eps, scale=1.0 / F).then_inc(rooted.at(v), 1)

    def scales(i, v, between):
        b = v % U
        rooted.wait(dve, i, v)
        dve.reciprocal(rstd[:, b, :], rstd[:, b, :]).then_inc(inverted.at(v), 1)
        scattered.wait(dve, i, v - U)
        inverted.wait(dve, i, v)
        for j in range(G):
            last = dve.scalar_tensor_tensor(rhs[:, b, j, 0:F], psH[v % 2][:, j, :], rstd[:, b, j:j + 1],
                                            K.vec["L1_gnn_msg_g"], ALU.mult, ALU.mult)
            if j == G - 1:
                last.then_inc(scaled.at(v), 1)
            between(j)
        scaled.wait(dve, i, v)
        dve.tensor_tensor(rhs[:, b, :, 0:F], rhs[:, b, :, 0:F], minus_beta.unsqueeze(1).broadcast_to([P, G, F]),
                          ALU.max).then_inc(ready.at(v), 1)

    gather.pick(0, 0, True)
    for v in range(AHEAD):
        ones.make(0, v)
        ones.transpose(0, v)
        ones.weight(0, v)
    blocks_pe = turn_blocks(K, ET.PE, 0, 2)
    for v in (0, 1):
        sums(0, v, blocks_pe)
    scales(0, 0, lambda j: None)
    with K.turns() as i:
        blocks_pe, blocks_dve = turn_blocks(K, ET.PE, i, U + 2), turn_blocks(K, ET.DVE, i)
        for v in range(U):
            ready.wait(pe, i, v)
            ones.weights_in.wait(pe, i, v)
            adder.added[-1].wait(pe, i, v - 2)
            for j in range(G):
                last = pe.matmul(psB[v % 2][:, j, 0:MW], onehotW[:, v, j, :], rhs[:, v, j, :], start=True, stop=True)
            last.then_inc(scattered.at(v), 1)
            ones.make(i, v + AHEAD)
            ones.transpose(i, v + AHEAD)
            sums(i, v + 2, blocks_pe)
            ones.weight(i, v + AHEAD)
            scales(i, v + 1, lambda j: adder.emit(i, v, j, blocks_dve(v, j)))
    for v in range(2):
        pool.wait_ge(gather.arrived.at(v), K.arrived_before[v])


def update(K, D, out):
    dve, sp, pe, act = K.dve, K.sp, K.pe, K.act
    acc = K.acc
    x1, msg = table(K.RA, F), table(K.RA, F, NB * F)
    new, tmp = table(K.RL, F), table(K.RL, F, NB * F)
    S, d = Sheet(K, "update"), K.dmas("update_dma")
    row, gate = K.node_small[:, 0, :], K.node_small[:, 1, :]
    d.done(sp.dma_start(x1, rows(K.x1)))
    S.tt(msg, by_column(K.vec["L1_gnn_msg_beta"]), wide(acc[:, :, F]), ALU.mult)
    S.tt(msg, msg, acc[:, :, 0:F], ALU.add)
    S.ts(row, K.count[:, :], 1e-8, None, ALU.add)
    S.reciprocal(row, row)
    S.ts(gate, K.count[:, :], 0.0, None, ALU.is_gt)
    S.tt(row, row, gate, ALU.mult)
    S.tt(msg, msg, wide(row), ALU.mult)
    d.after(dve, pe)
    S.s.after(pe)
    project(K, "upd", [(x1, K.WM[:, 2, :]), (msg, K.WM[:, 3, :])], F,
            lambda b, ps: dve.tensor_tensor(new[:, b, :], ps, K.vec["L1_gnn_upd_b"], ALU.add))
    K.barrier()
    S.layernorm(new, tmp, row, K.vec["L1_gnn_upd_g"], K.vec["L1_gnn_upd_beta"])
    S.ts(new, new, 0.0, None, ALU.max)
    S.tt(tmp, x1, by_column(K.vec["gate_w_row"]), ALU.mult)
    S.sum(gate, tmp)
    S.act(gate, gate, ACT.Sigmoid, bias=K.gate_b[:, 0:1])
    S.tt(new, new, wide(gate), ALU.mult)
    S.ts(gate, gate, -1.0, 1.0, ALU.mult, ALU.add)
    S.tt(tmp, x1, wide(gate), ALU.mult)
    S.tt(new, new, tmp, ALU.add)
    S.tt(new, new, x1, ALU.add)
    S.layernorm(new, tmp, row)
    S.s.after(sp)
    cut = (NB - 1) * P
    d.done(sp.dma_start(out[0:cut, :].rearrange("(b p) w -> p b w", p=P), new[:, 0:NB - 1, :]))
    d.done(sp.dma_start(out[cut:N, :], new[0:LAST, NB - 1, :]))
    d.after(sp)


def graph_layers(nc, D, out, probe=None):
    with ExitStack() as ctx:
        K = Build(nc, ctx)
        K.RA, K.RL, K.RF = (K.sb("region_" + n, [P, REGION]) for n in "ALF")
        K.ps = ctx.enter_context(nc.psum_tensor("psum", [P, 8, 512], fp32))
        K.xT = K.sb("block_transposed", [P, 2, P])
        K.slot_index = K.sb("slot_index", [P, U, G], i32)
        K.dots = K.sb("dots", [P, U, G])
        K.node_small = K.sb("node_small", [P, 2, NB])
        K.count = K.sb("edge_count", [P, NB])
        K.hidden_sums = K.sb("hidden_sums", [P, 2, -(-KC // 4)])
        K.hidden_total = K.sb("hidden_total", [P, 4])
        K.hidden_mean = K.sb("hidden_mean", [P, P])
        K.loop_edge = K.sb("loop_edge", [P, 2, H])
        K.cols = K.sb("chunk_columns", [P, 8])
        K.rowbuf = K.RA[0:1, 10240:10240 + 7 * P].rearrange("a (k h c) -> a k h c", h=H, c=CH)
        K.rowbuf2 = K.RA[0:1, 11264:11264 + 4 * P].rearrange("a (k h c) -> a k h c", h=H, c=CH)
        K.rowflat = K.RA[0:1, 12288:12288 + P]
        K.penalty = K.RA[:, 0:-(-TC // 2)].bitcast(bf16)[:, 0:TC]
        K.spill = K.dram("xs_by_slot", [SLOTS // G + AHEAD, P, G * F])
        K.edge2 = K.dram("edge_alpha2", [P, TC])
        K.credit = K.dram("credit", [U, P])
        def run(stage, *args):
            with K.phase():
                stage(K, *args)

        run(load_weights, D)
        run(place_edges, D)
        run(nodes_in, D)
        for layer in (1, 2):
            run(logits_pass, layer)
            if layer == 1:
                run(edge_features)
            run(logits, layer)
            run(breaks, layer)
            run(segment_softmax, layer)
            run(weighted_sum, layer)
            run(attention_out, layer)
        run(jump, D)
        run(message_pass)
        run(update, D, out)


def kernel(**inputs):
    import numpy as _np
    import concourse.bacc as _bacc
    from concourse import mybir as _mybir
    from concourse.bass_utils import run_bass_kernel_spmd as _run

    given = {k: _np.asarray(v) for k, v in inputs.items()}
    for k in ("L0_gnn_lin_w1", "L0_gnn_lin_w2", "L0_gnn_in_w", "L0_gnn_jk_w", "L0_gnn_enc_w1"):
        given[k + "_T"] = given[k].T
    given["gate_w_row"] = given["L1_gnn_gate_w"].reshape(-1)
    unused = ("L0_gnn_in_w", "L0_gnn_jk_w", "L0_gnn_enc_w1", "L1_gnn_gate_w")
    nc = _bacc.Bacc("TRN2", target_bir_lowering=False, num_devices=1)
    arrays, D = {}, {}
    for name, a in given.items():
        if name in unused:
            continue
        a = _np.ascontiguousarray(a)
        arrays["in_" + name] = a
        D[name] = nc.dram_tensor("in_" + name, a.shape, _mybir.dt.from_np(a.dtype), kind="ExternalInput").ap()
    out = nc.dram_tensor("out_0", (N, F), _mybir.dt.float32, kind="ExternalOutput").ap()
    graph_layers(nc, D, out)
    r = _run(nc, [arrays], core_ids=[0])
    return r.results[0]["out_0"]
```

```python
import concourse.bass as bass
from concourse import mybir
from contextlib import ExitStack, contextmanager

P = 128
N, E, F = 6250, 200000, 128
H, C = 8, 16
HID = 16
NB = -(-N // P)
NPAD = NB * P
LAST = N - (NB - 1) * P
TILES = -(-E // P)
G = 4
U = 4
AHEAD = 3
CH = P // H
assert CH == G * U
SLOTS = -(-(TILES + NB - 1) // CH) * CH
TURNS = SLOTS // (G * U)
SPARE = AHEAD * G
SRC_SPARE = (U + 1) * G
KC = SLOTS // CH
TC = KC * P
SC = -(-SLOTS // P)
EROWS = SLOTS - (NB - 1)
BIG = 1e30
EPS = 1e-5
SLOPE = 0.2
ROW1 = F + F + H + 1
ROW2 = F + H
DCOL1 = F + H + 1
AW = F + H + H + 1
REGION = -(-max(NB * ROW1, (SLOTS + SPARE) * H) // 64) * 64

fp32, bf16, i32, i16 = mybir.dt.float32, mybir.dt.bfloat16, mybir.dt.int32, mybir.dt.int16
ALU = mybir.AluOpType
ACT = mybir.ActivationFunctionType
AX = mybir.AxisListType
ET = mybir.EngineType
ENGINES = [ET.Pool, ET.Activation, ET.PE, ET.DVE, ET.SP]


class Relay:

    def __init__(self, sem, by=1):
        self.sem, self.by, self.n = sem, by, 0

    def after(self, *engines):
        for e in engines:
            if self.n:
                e.wait_ge(self.sem, self.n)

    def done(self, instruction):
        instruction.then_inc(self.sem, self.by)
        self.n += self.by

    def step(self, engine, emit):
        self.after(engine)
        self.done(emit())


class Build:

    def __init__(self, nc, ctx):
        self.nc, self.ctx, self.sems, self.used = nc, ctx, ctx, []
        self.pool, self.act, self.pe, self.dve, self.sp = nc.gpsimd, nc.scalar, nc.tensor, nc.vector, nc.sync
        self.tick = {e: self.sem("tick_" + n) for n, e in
                     (("pool", self.pool), ("act", self.act), ("pe", self.pe), ("dve", self.dve), ("sp", self.sp))}

        self.arrived = [self.sem(f"rows_arrived{u}") for u in range(U)]
        self.arrived_before = [0] * U

    def sb(self, name, shape, dt=fp32):
        return self.ctx.enter_context(self.nc.sbuf_tensor(name, shape, dt))

    def dram(self, name, shape, dt=fp32):
        return self.nc.dram_tensor(name, shape, dt, kind="Internal").ap()

    @contextmanager
    def phase(self):
        self.used = []
        with ExitStack() as self.sems:
            yield
            self.barrier()
            for s in self.used:
                self.pool.sem_clear(s)
        self.barrier()

    def sem(self, name):
        s = self.sems.enter_context(self.nc.semaphore(name))
        self.used.append(s)
        return s

    def relay(self, name):
        return Relay(self.sem(name))

    def dmas(self, name):
        return Relay(self.sem(name), 16)

    def loop_wait(self, engine, sem, i, per, plus):
        if isinstance(i, int):
            engine.wait_ge(sem, i * per + plus)
        else:
            key = (engine, per, plus)
            if key not in self.turn_values:
                self.turn_values[key] = engine.snap(i * per + plus)
            engine.wait_ge(sem, self.turn_values[key])
        engine.sem_inc(self.tick[engine], 1)

    @contextmanager
    def turns(self):
        with self.nc.Fori(0, TURNS, engines=ENGINES) as i:
            self.turn_values = {}
            yield i

    def barrier(self):
        self.nc.all_engine_barrier()


def table(region, width, at=0):
    return region[:, at:at + NB * width].rearrange("p (b w) -> p b w", w=width)


def rows(dram):
    return dram.rearrange("(b p) w -> p b w", p=P)


def load_weights(K, D):
    pool, pe, dve, sp, act = K.pool, K.pe, K.dve, K.sp, K.act
    K.ident = K.sb("ident", [P, P])
    K.iota = K.sb("iota", [P, P])
    K.ones = K.sb("ones", [P, P])
    K.ident_bf = K.sb("ident_bf", [P, P], bf16)
    K.W1 = K.sb("W_node1", [P, F + 2 * H + F])
    K.W2 = K.sb("W_node2", [P, F + 2 * H])
    K.JK = K.sb("W_jk", [P, 3, F])
    K.WM = K.sb("W_msg_upd", [P, 4, F])
    names = ["L0_gnn_bias1", "L0_gnn_g1", "L0_gnn_bn1", "L0_gnn_in_b", "L0_gnn_bias2", "L0_gnn_g2", "L0_gnn_bn2",
             "L0_gnn_jk_b", "L1_gnn_msg_b", "L1_gnn_msg_g", "L1_gnn_msg_beta", "L1_gnn_upd_b", "L1_gnn_upd_g",
             "L1_gnn_upd_beta", "gate_w_row"]
    K.vecs = K.sb("vectors", [P, len(names), F])
    K.vec = {n: K.vecs[:, k, :] for k, n in enumerate(names)}
    K.gate_b = K.sb("gate_b", [P, 1])
    K.Wbd = K.sb("enc_w1_diag", [4 * CH, 2, P])
    K.b1rep = K.sb("enc_b1_rep", [P, 1])
    K.Vbd = K.sb("edge_alpha_diag", [P, 2, 2, P])
    K.Vrep = K.sb("edge_alpha_rep", [P, 2, H])
    K.ccol = K.sb("edge_alpha_const_col", [P, 2])
    K.crow = K.sb("edge_alpha_const_row", [P, 2, H])
    R = K.RA
    att = R[:, 0:6 * H].rearrange("p (m h) -> p m h", h=H)
    lin = R[:, 64:64 + 2 * F].rearrange("p (m f) -> p m f", f=F)
    edge = R[:, 320:320 + 2 * H].rearrange("p (m f) -> p m f", f=H)
    encw2 = R[0:H, 340:340 + HID]
    encb2 = R[0:H, 360:361]
    We = R[0:H, 368:368 + 2 * H].rearrange("p (m f) -> p m f", f=H)
    WeR = R[0:H, 400:400 + 2 * P].rearrange("p (m f) -> p m f", f=P)
    b2R = R[0:H, 660:660 + P]
    V = R[0:HID, 800:800 + 2 * H]
    att_col = R[:, 820:826]
    w1_rep = R[0:4 * CH, 830:830 + HID]
    group, group4 = R[:, 850:850 + H], R[0:4 * CH, 860:860 + CH]
    spread = R[0:HID, 880:880 + P]

    made, loads, folded = K.relay("const_made"), K.dmas("weights_in"), K.relay("folded")
    made.done(pool.memset(K.ident[:, :], 0.0))
    made.done(pool.memset(K.ones[:, :], 1.0))
    made.done(pool.iota(K.iota[:, :], [[1, P]], base=0, channel_multiplier=0, allow_small_or_imprecise_dtypes=True))
    made.step(pool, lambda: pool.affine_select(out=K.ident[:, :], in_=K.ident[:, :], compare_op=ALU.not_equal,
                                               fill=1.0, base=0, pattern=[[-1, P]], channel_multiplier=1))

    queue = [sp, act]

    def load(dst, src):
        queue.reverse()
        loads.done(queue[0].dma_start(dst, src))

    for l in (1, 2):
        lw = f"L0_gnn_lin_w{l}"
        load((K.W1 if l == 1 else K.W2)[:, 0:F], D[lw + "_T"])
        load(lin[:, l - 1, :], D[lw])
        load(edge[:, l - 1, :], D[f"L0_gnn_lin_edge_w{l}"])
        for k, what in enumerate(("src", "dst", "edge")):
            load(att_col[:, 3 * (l - 1) + k:3 * (l - 1) + k + 1], D[f"L0_gnn_att_{what}{l}"].rearrange("h (c a) -> (h c) a", a=1))
    load(K.W1[:, F + 2 * H:], D["L0_gnn_in_w_T"])
    load(K.JK[:, :, :], D["L0_gnn_jk_w_T"].rearrange("(s f) o -> f s o", s=3))
    load(K.WM[:, 0:2, :], D["L1_gnn_msg_w"].rearrange("(s f) o -> f s o", s=2))
    load(K.WM[:, 2:4, :], D["L1_gnn_upd_w"].rearrange("(s f) o -> f s o", s=2))
    for n in names:
        load(K.vec[n], D[n].rearrange("(a f) -> a f", a=1).broadcast_to([P, F]))
    load(K.gate_b[:, :], D["L1_gnn_gate_b"].rearrange("(a f) -> a f", a=1).broadcast_to([P, 1]))
    load(encw2, D["L0_gnn_enc_w2"])
    load(encb2, D["L0_gnn_enc_b2"].rearrange("(a f) -> a f", f=1))
    for c in range(CH):
        load(w1_rep[4 * c:4 * c + 4, :], D["L0_gnn_enc_w1_T"])
    for d in range(CH // 2):
        load(K.b1rep[HID * d:HID * d + HID, :], D["L0_gnn_enc_b1"].rearrange("(a f) -> a f", f=1))
    loads.after(pe, dve)
    made.after(pe, dve)
    folded.done(dve.tensor_copy(K.ident_bf[:, :], K.ident[:, :]))
    eye = K.ident[:, :].rearrange("p (h c) -> p h c", c=C)
    folded.done(dve.tensor_reduce(group, eye, AX.X, ALU.add))
    folded.done(dve.tensor_reduce(group4, K.ident[0:4 * CH, 0:4 * CH].rearrange("p (c f) -> p c f", f=4), AX.X, ALU.add))
    folded.done(dve.tensor_copy(spread.rearrange("p (d k) -> p d k", k=HID),
                                K.ident[0:HID, 0:HID].unsqueeze(1).broadcast_to([HID, CH // 2, HID])))
    folded.done(dve.memset(K.Vbd[:, :, :, :], 0.0))
    folded.step(dve, lambda: dve.tensor_tensor(att, group.unsqueeze(1).broadcast_to([P, 6, H]),
                                               att_col.unsqueeze(2).broadcast_to([P, 6, H]), ALU.mult))
    folded.step(dve, lambda: dve.tensor_tensor(
        K.Wbd[:, :, :].rearrange("p q (d o) -> p (q d) o", o=HID), group4.unsqueeze(2).broadcast_to([4 * CH, CH, HID]),
        w1_rep.unsqueeze(1).broadcast_to([4 * CH, CH, HID]), ALU.mult))
    means = R[:, 700:706]
    folded.done(dve.tensor_reduce(means[:, 0:4], K.WM[:, :, :], AX.X, ALU.add))
    folded.done(dve.tensor_reduce(means[:, 4:5], K.vec["L1_gnn_msg_b"], AX.X, ALU.add))
    folded.done(dve.tensor_reduce(means[:, 5:6], K.vec["L1_gnn_upd_b"], AX.X, ALU.add))
    folded.step(dve, lambda: dve.tensor_scalar(means, means, 1.0 / F, None, ALU.mult))
    folded.step(dve, lambda: dve.tensor_tensor(K.WM[:, :, :], K.WM[:, :, :], means[:, 0:4].unsqueeze(2).broadcast_to([P, 4, F]),
                                               ALU.subtract))
    for k, name in ((4, "L1_gnn_msg_b"), (5, "L1_gnn_upd_b")):
        folded.step(dve, lambda: dve.tensor_tensor(K.vec[name], K.vec[name], means[:, k:k + 1].broadcast_to([P, F]),
                                                   ALU.subtract))
    ps = K.ps
    for l in (0, 1):
        W = (K.W1, K.W2)[l]
        folded.step(pe, lambda: pe.matmul(ps[:, 0, 0:H], lin[:, l, :], att[:, 3 * l, :], start=True, stop=True))
        folded.step(pe, lambda: pe.matmul(ps[:, 1, 0:H], lin[:, l, :], att[:, 3 * l + 1, :], start=True, stop=True))
        folded.step(pe, lambda: pe.matmul(ps[0:H, 2, 0:H], edge[:, l, :], att[:, 3 * l + 2, :], start=True, stop=True))
        folded.step(dve, lambda: dve.tensor_copy(W[:, F:F + 2 * H].rearrange("p (m h) -> p m h", h=H), ps[:, 0:2, 0:H]))
        folded.step(dve, lambda: dve.tensor_copy(We[:, l, :], ps[0:H, 2, 0:H]))
        folded.step(dve, lambda: dve.tensor_copy(
            WeR[:, l, :].rearrange("p (c h) -> p c h", h=H), We[:, l, :].unsqueeze(1).broadcast_to([H, CH, H])))
        folded.step(dve, lambda: dve.tensor_copy(b2R, encb2.broadcast_to([H, P])))
        folded.step(pe, lambda: pe.matmul(ps[0:HID, 3, 0:H], encw2, We[:, l, :], start=True, stop=True))
        folded.step(pe, lambda: pe.matmul(ps[:, 4, 0:1], WeR[:, l, :], encb2, start=True, stop=True))
        folded.step(pe, lambda: pe.matmul(ps[:, 5, 0:H], b2R, We[:, l, :], start=True, stop=True))
        folded.step(dve, lambda: dve.tensor_copy(V[:, l * H:l * H + H], ps[0:HID, 3, 0:H]))
        folded.step(dve, lambda: dve.tensor_copy(K.ccol[:, l:l + 1], ps[:, 4, 0:1]))
        folded.step(dve, lambda: dve.tensor_copy(K.crow[:, l, :], ps[:, 5, 0:H]))
    folded.step(pe, lambda: pe.matmul(ps[:, 6, 0:2 * H], spread, V, start=True, stop=True))
    folded.step(dve, lambda: dve.tensor_copy(K.Vrep[:, :, :], ps[:, 6, 0:2 * H].rearrange("p (l h) -> p l h", h=H)))
    for l in (0, 1):
        for q in (0, 1):
            half = K.Vbd[:, l, q, q * (P // 2):(q + 1) * (P // 2)].rearrange("p (d h) -> p d h", h=H)
            folded.step(dve, lambda: dve.tensor_tensor(half, group.unsqueeze(2).broadcast_to([P, CH // 2, H]),
                                                       K.Vrep[:, l, :].unsqueeze(1).broadcast_to([P, CH // 2, H]), ALU.mult))
    folded.after(sp, act)
    for v in range(AHEAD):
        load(K.spill[SLOTS // G + v, :, :], K.vecs[:, 0:G, :].rearrange("p g f -> p (g f)"))
    loads.after(sp)


def place_edges(K, D):
    nc, pool, pe, dve, sp, act = K.nc, K.pool, K.pe, K.dve, K.sp, K.act
    K.SRC = K.sb("slot_src", [P, SLOTS + SRC_SPARE], i32)
    K.DL = K.sb("slot_local_dst", [P, SLOTS + SRC_SPARE])
    K.KEY = K.sb("slot_key", [P, SLOTS])
    K.WT = K.sb("slot_weight", [P, SLOTS + SPARE])
    K.BLK = K.sb("slot_block", [1, SLOTS + SPARE], i16)
    edge_rows = K.dram("edge_rows", [EROWS, 3, P], i32)
    blk_dram = K.dram("slot_block_dram", [SC * P], i16)

    pad = K.RL[0:EROWS - TILES + 1, 0:3 * P].bitcast(i32).rearrange("p (a e) -> p a e", a=3)
    lasts_i = K.RL[:, 512:512 + SC].bitcast(i32)
    lasts = K.RL[:, 544:544 + SC]
    limits = K.RL[:, 576:576 + NB - 1]
    whole = K.RL[:, 1024:1024 + (NB - 1) * SC].rearrange("p (b c) -> p b c", c=SC)
    below = K.RL[:, 4000:4000 + NB - 1]
    thresh = K.RL[:, 4200:4200 + NB - 1]
    sidx = K.RL[:, 4300:4300 + SC]
    blk = K.RL[:, 4320:4320 + SC]
    blk_i = K.RL[:, 4340:4340 + SC].bitcast(i16)[:, 0:SC]
    tile_f = K.RL[:, 4360:4360 + SC]
    tile_i = K.RL[:, 4380:4380 + SC].bitcast(i32)
    blk128 = K.RL[:, 4400:4400 + SC]
    junk = K.RL[:, 4500:4500 + NB - 1]
    erow = K.RF[:, 0:SC * 3 * P].rearrange("p (c a e) -> p c a e", a=3, e=P)
    erow_flat = K.RF[:, 0:SC * 3 * P].rearrange("p (c w) -> p c w", w=3 * P).bitcast(i32)
    SW = SC * P
    srcf = K.RA[:, 0:SW].rearrange("p (c e) -> p c e", e=P)
    dstf = K.RA[:, SW:2 * SW].rearrange("p (c e) -> p c e", e=P)
    local = K.RA[:, 2 * SW:3 * SW].rearrange("p (c e) -> p c e", e=P)
    valid = K.RA[:, 3 * SW:4 * SW].rearrange("p (c e) -> p c e", e=P)

    m, d, g = K.relay("place_steps"), K.dmas("place_dmas"), Relay(K.arrived[0], 16)
    filled = K.relay("pad_filled")
    FT = E // P
    filled.done(pool.memset(lasts_i[:, FT // P:SC], 1 << 23))
    filled.done(pool.memset(K.SRC[:, SLOTS:], 0))
    filled.done(pool.memset(K.DL[:, SLOTS:], -1.0))
    filled.done(pool.memset(K.WT[:, SLOTS:], 0.0))
    filled.done(pool.memset(K.BLK[:, SLOTS:], 0))
    filled.done(pool.memset(pad[:, 0, :], 0))
    filled.done(pool.memset(pad[:, 1, :], -1))
    filled.done(pool.memset(pad[:, 2, :], 0))
    full = (TILES - 1) * P
    for a, name in enumerate(("src", "dst", "edge_weight")):
        flat = D[name] if name != "edge_weight" else D[name].bitcast(i32)
        d.done(sp.dma_start(edge_rows[0:TILES - 1, a, :], flat[0:full].rearrange("(t e) -> t e", e=P)))
        d.done(act.dma_start(edge_rows[TILES - 1:TILES, a, 0:E - full], flat[full:E].rearrange("(t e) -> t e", t=1)))
    last_dst = D["dst"][0:FT * P].rearrange("(t e) -> t e", e=P)[:, P - 1:P]
    filled.after(sp, act)
    with nc.allow_non_contiguous_dma("one destination of every tile"):
        d.done(sp.dma_start(lasts_i[:, 0:FT // P], last_dst[0:FT // P * P, :].rearrange("(c p) a -> p (c a)", p=P)))
        d.done(sp.dma_start(lasts_i[0:FT % P, FT // P:SC], last_dst[FT // P * P:FT, :]))
    if E - full < P:
        d.done(act.dma_start(edge_rows[TILES - 1:TILES, :, E - full:P], pad[0:1, :, E - full:P]))
    d.done(act.dma_start(edge_rows[TILES:EROWS, :, :], pad[1:EROWS - TILES + 1, :, :]))
    filled.done(pool.iota(sidx, [[P, SC]], base=0, channel_multiplier=1, allow_small_or_imprecise_dtypes=True))
    d.after(dve)
    filled.after(dve)
    m.step(dve, lambda: dve.tensor_copy(lasts, lasts_i))
    m.step(dve, lambda: dve.tensor_scalar(limits, K.iota[:, 1:NB], float(P), None, ALU.mult))
    m.step(dve, lambda: dve.tensor_tensor(whole, lasts.unsqueeze(1).broadcast_to([P, NB - 1, SC]),
                                          limits.unsqueeze(2).broadcast_to([P, NB - 1, SC]), ALU.is_lt))
    m.step(dve, lambda: dve.tensor_reduce(below, whole, AX.X, ALU.add))
    m.step(pe, lambda: pe.matmul(K.ps[:, 0, 0:NB - 1], K.ones[:, :], below, start=True, stop=True))
    m.step(dve, lambda: dve.tensor_tensor(thresh, K.ps[:, 0, 0:NB - 1], K.iota[:, 1:NB], ALU.add))
    for c in range(SC):
        m.step(dve, lambda: dve.tensor_scalar(junk, thresh, sidx[:, c:c + 1], 0.0, ALU.is_le, ALU.add,
                                              accum_out=blk[:, c:c + 1]))
    m.step(dve, lambda: dve.tensor_tensor(tile_f, sidx, blk, ALU.subtract))
    m.step(dve, lambda: dve.tensor_scalar(tile_f, tile_f, float(EROWS - 1), None, ALU.min))
    m.step(dve, lambda: dve.tensor_copy(tile_i, tile_f))
    m.step(dve, lambda: dve.tensor_copy(blk_i, blk))
    m.step(dve, lambda: dve.tensor_scalar(blk128, blk, float(P), None, ALU.mult))
    m.after(pool, sp)
    with nc.allow_non_contiguous_dma("block of each slot, once"):
        d.done(sp.dma_start(blk_dram.rearrange("(c p) -> p c", p=P), blk_i))
    d.after(pool, sp)
    d.done(sp.dma_start(K.BLK[:, 0:SLOTS], blk_dram[0:SLOTS].rearrange("(a s) -> a s", a=1)))
    for c in range(SC):
        g.done(pool.indirect_dma_start(out=erow_flat[:, c, :], out_offset=None,
                                       in_=edge_rows.rearrange("t a e -> t (a e)"),
                                       in_offset=bass.IndirectOffsetOnAxis(ap=tile_i[:, c:c + 1], axis=0)))
    g.after(dve, act, pe)
    K.arrived_before[0] += g.n
    m.step(act, lambda: act.activation(srcf, erow[:, :, 0, :].bitcast(i32), ACT.Copy))
    m.step(dve, lambda: dve.tensor_copy(dstf, erow[:, :, 1, :].bitcast(i32)))
    m.step(dve, lambda: dve.tensor_tensor(local, dstf, blk128.unsqueeze(2).broadcast_to([P, SC, P]), ALU.subtract))
    m.step(dve, lambda: dve.tensor_scalar(valid, local, 0.0, None, ALU.is_ge))
    m.step(dve, lambda: dve.scalar_tensor_tensor(valid, local, float(P), valid, ALU.is_lt, ALU.mult))
    m.step(dve, lambda: dve.scalar_tensor_tensor(local, local, 1.0, valid, ALU.add, ALU.mult))
    m.step(dve, lambda: dve.tensor_scalar(local, local, -1.0, None, ALU.add))
    m.step(dve, lambda: dve.scalar_tensor_tensor(dstf, dstf, 1.0, valid, ALU.add, ALU.mult))
    m.step(dve, lambda: dve.tensor_scalar(dstf, dstf, -1.0, None, ALU.add))
    n = 0
    for out, source in ((K.SRC, srcf), (K.DL, local), (K.KEY, dstf), (K.WT, erow[:, :, 2, :])):
        for c0 in range(0, SC, 4):
            cs = range(c0, min(c0 + 4, SC))
            w = min(SLOTS, (cs[-1] + 1) * P) - c0 * P
            m.after(pe)
            for c in cs:
                last = pe.transpose(K.ps[:, n % 8, (c - c0) * P:(c - c0 + 1) * P], source[:, c, :], K.ident[:, :])
            m.done(last)
            m.step(dve, lambda: dve.tensor_copy(out[:, c0 * P:c0 * P + w], K.ps[:, n % 8, 0:w]))
            n += 1
    d.after(sp)
    K.barrier()


def project(K, name, sources, width, evacuate):
    pe, act, dve = K.pe, K.act, K.dve
    transposed, copied = K.relay(name + "_transposed"), K.relay(name + "_copied")
    multiplied, evacuated = K.relay(name + "_multiplied"), K.relay(name + "_evacuated")
    units = [(b, k) for b in range(NB) for k in range(len(sources))]

    def transpose(q):
        b, k = units[q]
        if q >= 2:
            pe.wait_ge(copied.sem, q - 1)
        transposed.done(pe.transpose(K.ps[:, q % 2, 0:P], sources[k][0][:, b, :], K.ident[:, :]))
        act.wait_ge(transposed.sem, q + 1)
        if q >= 2:
            act.wait_ge(multiplied.sem, q - 1)
        copied.done(act.activation(K.xT[:, q % 2, :], K.ps[:, q % 2, 0:P], ACT.Copy))

    transpose(0)
    for q, (b, k) in enumerate(units):
        if q + 1 < len(units):
            transpose(q + 1)
        pe.wait_ge(copied.sem, q + 1)
        if k == 0 and b >= 2:
            pe.wait_ge(evacuated.sem, b - 1)
        multiplied.done(pe.matmul(K.ps[:, 2 + b % 2, 0:width], K.xT[:, q % 2, :], sources[k][1],
                                  start=k == 0, stop=k == len(sources) - 1))
        if k == len(sources) - 1:
            dve.wait_ge(multiplied.sem, q + 1)
            evacuated.done(evacuate(b, K.ps[:, 2 + b % 2, 0:width]))


def nodes_in(K, D):
    dve, sp, act, pool = K.dve, K.sp, K.act, K.pool
    K.rows1, K.h0, K.h1 = K.dram("rows1", [NPAD, ROW1]), K.dram("h0", [NPAD, F]), K.dram("h1", [NPAD, F])
    K.rows2 = K.dram("rows2", [NPAD, ROW2])
    K.a_node = K.sb("a_src_a_dst", [P, NB, 2 * H])
    K.by_dst = table(K.RL, DCOL1)
    stage, h0 = table(K.RA, ROW1), table(K.RF, F)
    squares = K.RF[:, NB * F:NB * F + P]
    s, d = K.relay("nodes_in_steps"), K.dmas("nodes_in_dmas")
    s.done(pool.memset(K.by_dst[:, NB - 1, :], 0.0))
    s.after(sp)
    load_x(K, D, K.by_dst[:, :, 0:F], d)
    d.after(K.pe, dve, act)
    squared = K.relay("nodes_squared")

    def evacuate(b, ps):
        act.activation(stage[:, b, 0:F], K.by_dst[:, b, 0:F], ACT.Copy)
        squared.step(act, lambda: act.activation(squares, K.by_dst[:, b, 0:F], ACT.Square,
                                                 accum_out=stage[:, b, ROW1 - 1:ROW1]))
        dve.tensor_copy(stage[:, b, F:2 * F + H], ps[:, 0:F + H])
        dve.tensor_copy(K.a_node[:, b, :], ps[:, F:F + 2 * H])
        return dve.tensor_tensor(h0[:, b, :], ps[:, F + 2 * H:], K.vec["L0_gnn_in_b"], ALU.add)

    project(K, "in", [(K.by_dst[:, :, 0:F], K.W1[:, :])], F + 2 * H + F, evacuate)
    K.barrier()
    d.done(sp.dma_start(rows(K.h0), h0))
    s.step(dve, lambda: dve.tensor_copy(K.by_dst[:, :, F:F + H], K.a_node[:, :, H:2 * H]))
    s.step(dve, lambda: dve.tensor_copy(K.by_dst[:, :, DCOL1 - 1], stage[:, :, ROW1 - 1]))
    d.done(act.dma_start(rows(K.rows1), stage))
    s.after(sp)
    d.after(sp)
    K.barrier()


def load_x(K, D, out, relay):
    cut = (NB - 1) * P
    relay.done(K.sp.dma_start(out[:, 0:NB - 1, :], D["x"][0:cut, :].rearrange("(b p) w -> p b w", p=P)))
    relay.done(K.sp.dma_start(out[0:LAST, NB - 1, :], D["x"][cut:N, :]))


class Event:

    def __init__(self, K, name):
        self.K, self.sems = K, [K.sem(f"{name}{u}") for u in range(U)]
        for sem in self.sems:
            K.dve.sem_inc(sem, 1)

    def at(self, v):
        return self.sems[v % U]

    def wait(self, engine, i, v):
        self.K.loop_wait(engine, self.at(v), i, 1, v // U + 2)


class DmaEvent:

    def __init__(self, K, sems, each, before):
        self.K, self.sems, self.each, self.before = K, sems, 16 * each, before

    def at(self, v):
        return self.sems[v % U]

    def wait(self, engine, i, v):
        self.K.loop_wait(engine, self.at(v), i, self.each, (v // U + 1) * self.each + self.before[v % U])


def slots_of(i, v):
    return bass.ds(i * (G * U) + v * G, G)


def slot_of(i, v, j):
    return bass.ds(i * (G * U) + (v * G + j), 1)


def fresh_dma_event(K, name, each):
    sems = [K.sem(f"{name}{u}") for u in range(U)]
    for u in range(U):
        for _ in range(each):
            K.sp.dma_start(K.credit[u:u + 1, :], K.ident[0:1, 0:P]).then_inc(sems[u], 16)
            K.sp.wait_ge(sems[u], 16)
    return DmaEvent(K, sems, each, [16 * each] * U)


class Gather:

    def __init__(self, K, name, source, buffer, freed, extra):
        self.K, self.source, self.buffer, self.freed = K, source, buffer, freed
        self.picked = Event(K, name + "_indices_picked")
        self.arrived = DmaEvent(K, K.arrived, G, list(K.arrived_before))
        for u in range(U):
            K.arrived_before[u] += 16 * G * (TURNS + (1 if u < extra else 0))

    def pick(self, i, v):
        self.K.dve.tensor_copy(self.K.slot_index[:, v % U, :], self.K.SRC[:, slots_of(i, v)]
                               ).then_inc(self.picked.at(v), 1)

    def emit(self, i, v):
        K, pool = self.K, self.K.pool
        for event in self.freed:
            event.wait(pool, i, v - U)
        self.picked.wait(pool, i, v)
        for j in range(G):
            pool.indirect_dma_start(out=self.buffer[:, v % U, j, :], out_offset=None, in_=self.source,
                                    in_offset=bass.IndirectOffsetOnAxis(ap=K.slot_index[:, v % U, j:j + 1], axis=0)
                                    ).then_inc(self.arrived.at(v), 16)


class OneHots:

    def __init__(self, K, name, onehot, onehotT, psT, used, weighted=None, scattered=None):
        self.K, self.onehot, self.onehotT, self.psT = K, onehot, onehotT, psT
        self.used, self.weighted, self.scattered = used, weighted, scattered
        self.made, self.transposed, self.out = (Event(K, f"{name}_onehot_{x}") for x in ("made", "transposed", "transposed_out"))
        self.weights_in = Event(K, name + "_onehot_weighted") if weighted is not None else None

    def make(self, i, v):
        K, dve = self.K, self.K.dve
        self.transposed.wait(dve, i, v - U)
        if self.weighted is not None:
            self.weights_in.wait(dve, i, v - U)
        dve.tensor_tensor(self.onehot[:, v % U, :, :], K.iota[:, :].unsqueeze(1).broadcast_to([P, G, P]),
                          K.DL[:, slots_of(i, v)].unsqueeze(2).broadcast_to([P, G, P]),
                          ALU.is_equal).then_inc(self.made.at(v), 1)

    def weight(self, i, v):
        K, act = self.K, self.K.act
        self.scattered.wait(act, i, v - U)
        self.made.wait(act, i, v)
        for j in range(G):
            last = act.activation(self.weighted[:, v % U, j, :], self.onehot[:, v % U, j, :], ACT.Copy,
                                  scale=K.WT[:, slot_of(i, v, j)])
        last.then_inc(self.weights_in.at(v), 1)

    def transpose(self, i, v):
        K, pe, act = self.K, self.K.pe, self.K.act
        self.made.wait(pe, i, v)
        self.out.wait(pe, i, v - 2)
        for j in range(G):
            last = pe.transpose(self.psT[v % 2][:, j, :], self.onehot[:, v % U, j, :], K.ident_bf[:, :])
        last.then_inc(self.transposed.at(v), 1)
        self.transposed.wait(act, i, v)
        self.used.wait(act, i, v - U)
        act.activation(self.onehotT[:, v % U, :, :], self.psT[v % 2], ACT.Copy).then_inc(self.out.at(v), 1)


def pieces(region, at, *specs):
    out = []
    for w, dtype in specs:
        cols = U * G * w // (2 if dtype is bf16 else 1)
        v = region[:, at:at + cols]
        v = v.bitcast(bf16) if dtype is bf16 else v
        out.append(v.rearrange("p (u g w) -> p u g w", u=U, g=G))
        at += cols
    assert at <= REGION
    return out


def turn_values(K, kind, entries, most, i, per, visits=U):
    where = slice(0, per * visits) if isinstance(i, int) else bass.ds(i * (per * U), per * visits)
    _, values = K.nc.values_load_multi_w_load_instructions(
        entries[0:1, where], engines=[kind], min_val=0, max_val=most,
        skip_runtime_bounds_check_because="a slot's block counts the 48 block starts passed, one more at most in each slot")
    return lambda v, j: values[v * per + j]


def turn_blocks(K, kind, i, visits=U):
    return turn_values(K, kind, K.BLK, NB - 1, i, G, visits)


def logits_pass(K, layer):
    pe, dve, sp = K.pe, K.dve, K.sp
    first = layer == 1
    row, dcol = (ROW1, DCOL1) if first else (ROW2, H)
    xs0, as0 = (F, 2 * F) if first else (0, F)
    d0 = F if first else 0
    onehot, onehotT = pieces(K.RL, NB * DCOL1, (P, bf16), (P, None))
    rowbuf, junk = pieces(K.RF, SLOTS * 4, (row, None), (F, bf16))
    dots = K.dots
    asum = K.RA[:, 0:SLOTS * H].rearrange("p (s h) -> p s h", h=H)
    feat = K.RF[:, 0:SLOTS * 4].rearrange("p (s f) -> p s f", f=4)
    psT = [K.ps[:, b, 0:G * P // 2].bitcast(bf16).rearrange("p (g e) -> p g e", g=G) for b in range(2)]
    psX = [K.ps[:, 2 + 2 * b:4 + 2 * b, :].rearrange("p k (a w) -> p (k a) w", a=2) for b in range(2)]
    n = f"logits{layer}"
    selected, dotted, consumed = (Event(K, f"{n}_{x}") for x in ("selected", "dotted", "consumed"))
    spilled = fresh_dma_event(K, n + "_spilled", 1)
    gather = Gather(K, n, K.rows1 if first else K.rows2, rowbuf, [consumed, spilled], 0)
    ones = OneHots(K, n, onehot, onehotT, psT, selected)
    K.barrier()
    for v in range(U):
        gather.pick(0, v)
    for v in range(AHEAD):
        ones.make(0, v)
        ones.transpose(0, v)
    with K.turns() as i:
        blocks = turn_blocks(K, ET.PE, i)
        for v in range(U):
            gather.emit(i, v)
            gather.arrived.wait(sp, i, v)
            sp.dma_start(K.spill[bass.ds(i * U + v, 1), :, :].rearrange("a p (g w) -> (a p) g w", g=G),
                         rowbuf[:, v, :, xs0:xs0 + F]).then_inc(spilled.at(v), 16)
            ones.out.wait(pe, i, v)
            consumed.wait(pe, i, v - 2)
            for j in range(G):
                last = pe.matmul(psX[v % 2][:, j, 0:dcol], onehotT[:, v, j, :],
                                 K.by_dst[:, bass.ds(blocks(v, j), 1), 0:dcol].rearrange("p b w -> p (b w)"),
                                 start=True, stop=True)
            last.then_inc(selected.at(v), 1)
            ones.make(i, v + AHEAD)
            ones.transpose(i, v + AHEAD)
            selected.wait(dve, i, v)
            gather.arrived.wait(dve, i, v)
            gather.pick(i, v + U)
            X = psX[v % 2]
            if first:
                for j in range(G):
                    last = dve.tensor_tensor_reduce(out=junk[:, v, j, :], in0=rowbuf[:, v, j, 0:F], in1=X[:, j, 0:F],
                                                    scale=1.0, scalar=0.0, op0=ALU.mult, op1=ALU.add,
                                                    accum_out=dots[:, v, j:j + 1])
                last.then_inc(dotted.at(v), 1)
                dve.tensor_copy(feat[:, slots_of(i, v), 2:3], rowbuf[:, v, :, ROW1 - 1:ROW1])
                dve.tensor_copy(feat[:, slots_of(i, v), 3:4], X[:, :, DCOL1 - 1:DCOL1])
                dotted.wait(dve, i, v)
                dve.tensor_copy(feat[:, slots_of(i, v), 0:1], dots[:, v, :].unsqueeze(2))
            dve.tensor_tensor(asum[:, slots_of(i, v), :], rowbuf[:, v, :, as0:as0 + H], X[:, :, d0:d0 + H],
                              ALU.add).then_inc(consumed.at(v), 1)
    for v in range(U):
        sp.wait_ge(spilled.at(v), 16 + 16 * TURNS)


def chunked(region, width):
    return region[:, 0:SLOTS * width].rearrange("p (c k w) -> p k c w", k=KC, w=width)


def edge_features(K):
    dve = K.dve
    feat = K.RF[:, 0:SLOTS * 4].rearrange("p (s f) -> p s f", f=4)
    valid = K.RF[:, SLOTS * 4:SLOTS * 5]
    s = K.relay("features")
    s.step(dve, lambda: dve.tensor_scalar(valid, K.DL[:, 0:SLOTS], 0.0, None, ALU.is_ge))
    s.step(dve, lambda: dve.tensor_tensor(feat[:, :, 1], feat[:, :, 2], feat[:, :, 3], ALU.add))
    s.step(dve, lambda: dve.scalar_tensor_tensor(feat[:, :, 1], feat[:, :, 0], -2.0, feat[:, :, 1], ALU.mult, ALU.add))
    s.step(dve, lambda: dve.tensor_tensor(feat, feat, valid.unsqueeze(2).broadcast_to([P, SLOTS, 4]), ALU.mult))
    K.barrier()


def logits(K, layer):
    act, pe, dve, sp, pool = K.act, K.pe, K.dve, K.sp, K.pool
    L = K.RL
    first = layer == 1
    feat, asum = chunked(K.RF, 4), chunked(K.RA, H)
    at = SLOTS * 4

    def take(n):
        nonlocal at
        at += n
        return K.RF[:, at - n:at]
    W = 4 * P
    featT, hidden, raw, edge2 = take(2 * W), take(4 * W), take(2 * W), take(2 * W)
    sum_packed = take(8 * P).rearrange("p (z k w) -> p z k w", z=2, w=P)
    feat_packed = K.xT[:, :, :].rearrange("p u (k w) -> p (u k) w", w=4 * CH)
    assert at <= REGION
    n = f"softmax_in{layer}_"
    feat_in, packed = K.relay(n + "features_packed"), K.relay(n + "packed")
    ftr, fcp, hid_mm, hid_out = (K.relay(n + x) for x in ("features_transposed", "features_out", "hidden_product", "hidden_out"))
    lg_mm, e2_mm, biased, done, e2_out = (K.relay(n + x) for x in ("logit_product", "edge2_product", "biased", "done", "edge2_out"))
    io = [K.dmas(n + f"edge2_dma{z}") for z in range(2)]
    starts = list(range(0, KC, 4))

    def prepare(z):
        k0 = starts[z]
        ks = range(k0, min(k0 + 4, KC))
        w = len(ks) * P
        half = (z % 2) * W
        split = lambda t, w: t.rearrange("p k (c w) -> p k c w", w=w)
        if first:
            if z >= 1:
                pool.wait_ge(ftr.sem, z)
            feat_in.done(pool.tensor_copy(split(feat_packed[:, 0:len(ks), :], 4), feat[:, k0:k0 + len(ks), :, :]))
        if z >= 2:
            pool.wait_ge(lg_mm.sem, z - 1)
        packed.done(pool.tensor_copy(split(sum_packed[:, z % 2, 0:len(ks), :], H), asum[:, k0:k0 + len(ks), :, :]))
        if first:
            bank = 7 * (z % 2)
            pe.wait_ge(feat_in.sem, z + 1)
            if z >= 2:
                pe.wait_ge(fcp.sem, z - 1)
            for k in ks:
                last = pe.transpose(K.ps[0:4 * CH, bank, (k - k0) * P:(k - k0 + 1) * P], feat_packed[:, k - k0, :], K.ident[:, :])
            ftr.done(last)
            act.wait_ge(ftr.sem, z + 1)
            if z >= 2:
                act.wait_ge(hid_mm.sem, 2 * (z - 1))
            fcp.done(act.activation(featT[0:4 * CH, half:half + w], K.ps[0:4 * CH, bank, 0:w], ACT.Copy))

    prepare(0)
    for z, k0 in enumerate(starts):
        ks = range(k0, min(k0 + 4, KC))
        w = len(ks) * P
        half = (z % 2) * W
        if z + 1 < len(starts):
            prepare(z + 1)
        if first:
            for q in (0, 1):
                pe.wait_ge(fcp.sem, z + 1)
                if z >= 1:
                    pe.wait_ge(hid_out.sem, 2 * (z - 1) + q + 1)
                hid_mm.done(pe.matmul(K.ps[:, 1 + q, 0:w], K.Wbd[:, q, :], featT[0:4 * CH, half:half + w], start=True, stop=True))
                act.wait_ge(hid_mm.sem, 2 * z + q + 1)
                if z >= 2:
                    act.wait_ge(e2_mm.sem, z - 1)
                hid_out.done(act.activation(hidden[:, 2 * half + q * W:2 * half + q * W + w], K.ps[:, 1 + q, 0:w], ACT.Relu,
                                            bias=K.b1rep[:, 0:1], accum_out=K.hidden_sums[:, q, z:z + 1]))
            pe.wait_ge(hid_out.sem, 2 * z + 2)
        if z >= 2:
            pe.wait_ge(biased.sem, z - 1)
        bank = 3 + z % 2
        if first:
            for q in (0, 1):
                pe.matmul(K.ps[:, bank, 0:w], K.Vbd[:, 0, q, :], hidden[:, 2 * half + q * W:2 * half + q * W + w],
                          start=q == 0, stop=False, skip_group_check=True)
        pe.wait_ge(packed.sem, z + 1)
        for k in ks:
            last = pe.matmul(K.ps[:, bank, (k - k0) * P:(k - k0 + 1) * P], sum_packed[:, z % 2, k - k0, :], K.ident[:, :],
                             start=not first, stop=True, skip_group_check=True)
        lg_mm.done(last)
        if first:
            if z >= 2:
                pe.wait_ge(e2_out.sem, z - 1)
            for q in (0, 1):
                last = pe.matmul(K.ps[:, 5 + z % 2, 0:w], K.Vbd[:, 1, q, :], hidden[:, 2 * half + q * W:2 * half + q * W + w],
                                 start=q == 0, stop=q == 1)
            e2_mm.done(last)
        dve.wait_ge(lg_mm.sem, z + 1)
        if first:
            biased.done(dve.tensor_scalar(raw[:, half:half + w], K.ps[:, bank, 0:w], K.ccol[:, 0:1], None, ALU.add))
            act.wait_ge(e2_mm.sem, z + 1)
            if z >= 2:
                io[z % 2].after(act)
            e2_out.done(act.activation(edge2[:, half:half + w], K.ps[:, 5 + z % 2, 0:w], ACT.Identity, bias=K.ccol[:, 1:2]))
            sp.wait_ge(e2_out.sem, z + 1)
            io[z % 2].done(sp.dma_start(K.edge2[:, k0 * P:k0 * P + w], edge2[:, half:half + w]))
        else:
            if z >= 2:
                sp.wait_ge(biased.sem, z - 1)
            io[z % 2].done(sp.dma_start(edge2[:, half:half + w], K.edge2[:, k0 * P:k0 * P + w]))
            io[z % 2].after(dve)
            biased.done(dve.tensor_tensor(raw[:, half:half + w], K.ps[:, bank, 0:w], edge2[:, half:half + w], ALU.add))
        dve.wait_ge(biased.sem, z + 1)
        done.done(dve.scalar_tensor_tensor(L[:, k0 * P:k0 * P + w], raw[:, half:half + w], SLOPE, raw[:, half:half + w],
                                           ALU.mult, ALU.max))
    for r in io:
        r.after(sp)
    K.barrier()


def breaks(K):
    act, pe, dve = K.act, K.pe, K.dve
    tr, cp, s = K.relay("breaks_transposed"), K.relay("breaks_copied"), K.relay("breaks_steps")
    keys = K.RF[:, 0:TC]
    pen = K.penalty
    rep = K.RA[:, 8192:8192 + 2 * 4 * P].rearrange("p (z c h) -> p z c h", z=8, h=H)
    kview = chunked(K.KEY, 1)
    for k in range(KC):
        if k >= 8:
            dve.wait_ge(tr.sem, k - 7)
        s.done(dve.tensor_copy(rep[:, k % 8, :, :], kview[:, k, :, :].broadcast_to([P, CH, H])))
        pe.wait_ge(s.sem, k + 1)
        if k >= 8:
            pe.wait_ge(cp.sem, k - 7)
        tr.done(pe.transpose(K.ps[:, k % 8, 0:P], rep[:, k % 8, :, :].rearrange("p c h -> p (c h)"), K.ident[:, :]))
        act.wait_ge(tr.sem, k + 1)
        cp.done(act.activation(keys[:, k * P:(k + 1) * P], K.ps[:, k % 8, 0:P], ACT.Copy))
    K.barrier()
    s.step(dve, lambda: dve.memset(pen[:, 0:1], 0.0))
    s.step(dve, lambda: dve.tensor_tensor(pen[:, 1:TC], keys[:, 1:TC], keys[:, 0:TC - 1], ALU.not_equal))
    s.step(dve, lambda: dve.tensor_scalar(pen[:, 1:TC], pen[:, 1:TC], -BIG, None, ALU.mult))
    cols, R = K.cols, K.rowbuf
    s.step(dve, lambda: dve.tensor_reduce(cols[:, 0:1], pen, AX.X, ALU.min))
    s.step(dve, lambda: dve.tensor_scalar(cols[:, 0:1], cols[:, 0:1], 0.0, None, ALU.is_ge))
    s.step(dve, lambda: dve.tensor_copy(cols[:, 1:2], keys[:, 0:1]))
    s.step(dve, lambda: dve.tensor_copy(cols[:, 2:3], keys[:, TC - 1:TC]))
    rows_of(K, s, [(0, 0, False), (1, 1, False), (2, 2, False)])
    whole, first, last = (R[0:1, k, :, :] for k in range(3))
    goes = R[0:1, 3, :, :]
    s.step(dve, lambda: dve.memset(R[0:1, 3:7, :, :], 0.0))
    s.step(dve, lambda: dve.tensor_tensor(goes[:, :, 1:CH], first[:, :, 1:CH], last[:, :, 0:CH - 1], ALU.is_equal))
    M = K.rowbuf2
    s.step(dve, lambda: dve.tensor_tensor(M[0:1, 0, :, :], whole, goes, ALU.mult))
    s.step(dve, lambda: dve.tensor_copy(M[0:1, 1, :, :], goes))
    s.step(dve, lambda: dve.memset(M[0:1, 2:4, :, :], 0.0))
    s.step(dve, lambda: dve.tensor_copy(M[0:1, 3, :, 1:CH], goes[:, :, CH - 1:0:-1]))
    s.step(dve, lambda: dve.tensor_tensor(M[0:1, 2, :, 1:CH], M[0:1, 3, :, 1:CH], whole[:, :, CH - 2::-1], ALU.mult))
    s.step(dve, lambda: dve.tensor_scalar(M[0:1, :, :, :], M[0:1, :, :, :], BIG, -BIG, ALU.mult, ALU.add))
    s.step(dve, lambda: dve.tensor_copy(R[0:1, 4, :, :], goes))
    columns_of(K, s, [(4, 3, False)])
    kept = K.dmas("breaks_kept")
    s.after(K.sp)
    kept.done(K.sp.dma_start(K.pen_dram, pen))
    kept.done(K.sp.dma_start(K.chain_dram, M[0:1, :, :, :].rearrange("a k h c -> a (k h c)")))
    kept.after(K.sp)
    K.barrier()


def breaks_again(K):
    back = K.dmas("breaks_back")
    cut = TC // 2
    back.done(K.sp.dma_start(K.penalty[:, 0:cut], K.pen_dram[:, 0:cut]))
    back.done(K.act.dma_start(K.penalty[:, cut:TC], K.pen_dram[:, cut:TC]))
    back.done(K.sp.dma_start(K.rowbuf2[0:1, :, :, :].rearrange("a k h c -> a (k h c)"), K.chain_dram))
    back.after(K.sp, K.act)


def rows_of(K, s, moves):
    for col, row, mirrored in moves:
        s.step(K.pe, lambda: K.pe.matmul(K.ps[0:1, 0, 0:P], K.cols[:, col:col + 1], K.ident[:, :], start=True, stop=True))
        source = K.ps[0:1, 0, 0:P].rearrange("a (c h) -> a h c", h=H)
        s.step(K.dve, lambda: K.dve.tensor_copy(K.rowbuf[0:1, row, :, :], source[:, :, ::-1] if mirrored else source))


def columns_of(K, s, moves):
    flat = K.rowflat
    for row, col, mirrored in moves:
        source = K.rowbuf[0:1, row, :, :]
        s.step(K.dve, lambda: K.dve.tensor_copy(flat[0:1, :].rearrange("a (c h) -> a h c", h=H),
                                                source[:, :, ::-1] if mirrored else source))
        s.step(K.pe, lambda: K.pe.matmul(K.ps[:, 1, 0:1], flat[0:1, :], K.ones[0:1, 0:1], start=True, stop=True))
        s.step(K.dve, lambda: K.dve.tensor_copy(K.cols[:, col:col + 1], K.ps[:, 1, 0:1]))


def segment_softmax(K, layer):
    act, pe, dve, pool = K.act, K.pe, K.dve, K.pool
    n = f"softmax{layer}_"
    s = K.relay(n + "steps")
    L, M, pen, cols, R, Z = K.RL[:, 0:TC], K.RF[:, 0:TC], K.penalty, K.cols, K.rowbuf, K.rowbuf2

    def chain(col_in, z, mirrored, col_out):
        rows_of(K, s, [(col_in, 0, mirrored)])
        flat = lambda r: r.rearrange("a h c -> a (h c)")
        s.step(dve, lambda: dve.tensor_tensor_scan(out=flat(R[0:1, 1, :, :]), data0=flat(Z[0:1, z, :, :]),
                                                   data1=flat(R[0:1, 0, :, :]), initial=-BIG, op0=ALU.add, op1=ALU.max))
        s.step(dve, lambda: dve.memset(R[0:1, 2, :, :], -BIG))
        s.step(dve, lambda: dve.tensor_tensor(R[0:1, 2, :, 1:CH], R[0:1, 1, :, 0:CH - 1], Z[0:1, z + 1, :, 1:CH], ALU.add))
        columns_of(K, s, [(2, col_out, mirrored)])

    def scan(out, data, back, initial):
        if not back:
            return dve.tensor_tensor_scan(out=out, data0=pen, data1=data, initial=initial, op0=ALU.add, op1=ALU.max)
        return dve.tensor_tensor_scan(out=out[:, TC - 2::-1], data0=pen[:, TC - 1:0:-1], data1=data[:, TC - 2::-1],
                                      initial=initial, op0=ALU.add, op1=ALU.max)

    s.step(dve, lambda: scan(M, L, False, -BIG))
    s.step(dve, lambda: dve.tensor_copy(cols[:, 4:5], M[:, TC - 1:TC]))
    chain(4, 0, False, 5)
    s.step(dve, lambda: scan(M, L, False, cols[:, 5:6]))
    s.step(dve, lambda: dve.tensor_copy(cols[:, 6:7], M[:, TC - 1:TC]))
    s.step(dve, lambda: scan(M, M, True, cols[:, 6:7]))
    s.step(dve, lambda: dve.tensor_copy(cols[:, 4:5], M[:, 0:1]))
    chain(4, 2, True, 5)
    s.step(dve, lambda: dve.tensor_tensor(cols[:, 6:7], M[:, TC - 1:TC], cols[:, 5:6], ALU.max))
    s.step(dve, lambda: dve.tensor_copy(M[:, TC - 1:TC], cols[:, 6:7]))
    s.step(dve, lambda: scan(M, M, True, cols[:, 6:7]))
    cuts = [TC * q // 4 for q in range(5)]
    less = [K.relay(n + f"less_maximum{q}") for q in range(4)]
    for q, (a, b) in enumerate(zip(cuts, cuts[1:])):
        engine = pool if q == 3 else dve
        s.after(engine)
        less[q].done(engine.tensor_tensor(L[:, a:b], L[:, a:b], M[:, a:b], ALU.subtract))
        less[q].after(act, dve)
        act.activation(L[:, a:b], L[:, a:b], ACT.Exp)
        a = max(a, 1)
        s.done(dve.scalar_tensor_tensor(M[:, a:b], pen[:, a:b], 0.0, M[:, a:b], ALU.is_lt, ALU.mult))
    s.step(dve, lambda: dve.tensor_scalar(cols[:, 7:8], cols[:, 3:4], -1.0, 1.0, ALU.mult, ALU.add))
    s.step(dve, lambda: dve.tensor_tensor(M[:, 0:1], M[:, 0:1], cols[:, 7:8], ALU.mult))
    K.barrier()
    for what, source, out in (("weights", L, chunked(K.RA, H)), ("maxima", M, chunked(K.RL, H))):
        tr = K.relay(n + what + "_transposed")
        ev = [K.relay(n + what + f"_out{e}") for e in range(2)]
        for z, k0 in enumerate(range(0, KC, 4)):
            ks = range(k0, min(k0 + 4, KC))
            if z >= 4:
                pe.wait_ge(ev[z % 2].sem, (z - 4) // 2 + 1)
            for k in ks:
                last = pe.transpose(K.ps[:, z % 4, (k - k0) * P:(k - k0 + 1) * P], source[:, k * P:(k + 1) * P], K.ident[:, :])
            tr.done(last)
            result = out[:, k0:k0 + len(ks), :, :]
            bank = K.ps[:, z % 4, 0:len(ks) * P].rearrange("p (k c h) -> p k c h", c=CH, h=H)
            (act if z % 2 else dve).wait_ge(tr.sem, z + 1)
            ev[z % 2].done(act.activation(result, bank, ACT.Copy) if z % 2 else dve.tensor_copy(result, bank))
        K.barrier()


class Adder:

    def __init__(self, K, name, acc, psum, scattered, parts, span=1):
        self.K, self.acc, self.psum, self.scattered, self.parts, self.span = K, acc, psum, scattered, parts, span
        self.added = [Event(K, f"{name}_added{j}_") for j in range(parts)]

    def emit(self, i, v, j, block):
        dve = self.K.dve
        if j == 0:
            self.scattered.wait(dve, i, v)
        self.added[j - 1].wait(dve, i, v if j else v - 1)
        row = self.acc[:, bass.ds(block, self.span), :].rearrange("p b w -> p (b w)")
        dve.tensor_tensor(row, row, self.psum(v, j), ALU.add).then_inc(self.added[j].at(v), 1)


def weighted_sum(K, layer):
    pool, act, pe, dve, sp = K.pool, K.act, K.pe, K.dve, K.sp
    acc = K.RF[:, 0:(NB + 1) * AW].rearrange("p (b w) -> p b w", w=AW)
    K.acc = acc[:, 0:NB, :]
    onehot, rhs = pieces(K.RF, (NB + 1) * AW, (P, None), (AW, None))
    zero = K.RF[0:1, REGION - P:REGION].bitcast(bf16)
    behind = [REGION - P - k * (SLOTS // 4) for k in range(3)]
    pair_block, pair_step = (K.RF[0:1, behind[k + 1]:behind[k]].bitcast(i16) for k in (0, 1))
    assert (NB + 1) * AW + U * G * (P + AW) <= REGION - P - SLOTS // 2
    weight, top = (R[:, 0:(SLOTS + SPARE) * H].rearrange("p (s h) -> p s h", h=H) for R in (K.RA, K.RL))
    PAIRS = G // 2
    psB = lambda v, k: K.ps[:, (v % 2) * PAIRS + k, 0:2 * AW]
    n = f"sum{layer}_"
    made, copied, weighted, scattered = (Event(K, n + x) for x in ("onehot_made", "columns_copied", "weighted", "scattered"))
    loaded = DmaEvent(K, [K.sem(f"{n}xs_loaded{u}") for u in range(U)], 1, [0] * U)
    adder = Adder(K, n, acc, psB, scattered, PAIRS, 2)
    init = K.relay(n + "init")
    init.done(dve.memset(acc, 0.0))
    init.done(dve.memset(zero, 0.0))
    pairs = K.BLK[:, 0:SLOTS].rearrange("a (k two) -> a k two", two=2)
    init.done(dve.tensor_copy(pair_block, pairs[:, :, 0]))
    init.step(dve, lambda: dve.tensor_tensor(pair_step, pairs[:, :, 1], pairs[:, :, 0], ALU.subtract))
    init.step(dve, lambda: dve.tensor_scalar(pair_step, pair_step, float(AW), None, ALU.mult))
    init.done(dve.memset(rhs[:, :, :, AW - 1:AW], 1.0))
    init.done(dve.memset(weight[:, SLOTS:, :], 0.0))
    init.done(dve.memset(top[:, SLOTS:, :], 0.0))
    K.barrier()

    def one_hots(i, v, js):
        if js[0] == 0:
            scattered.wait(dve, i, v - U)
        first = i * (G * U) + (v * G + js[0])
        last = dve.tensor_tensor(onehot[:, v % U, js[0]:js[-1] + 1, :],
                                 K.iota[:, :].unsqueeze(1).broadcast_to([P, len(js), P]),
                                 K.DL[:, bass.ds(first, len(js))].unsqueeze(2).broadcast_to([P, len(js), P]), ALU.is_equal)
        if js[-1] == G - 1:
            last.then_inc(made.at(v), 1)

    def prepare(i, v):
        b = v % U
        at = bass.ds(i * U + v, 1) if not isinstance(i, int) else slice(v, v + 1)
        scattered.wait(sp, i, v - U)
        sp.dma_start(rhs[:, b, :, 0:F], K.spill[at, :, :].rearrange("a p (g w) -> (a p) g w", g=G)
                     ).then_inc(loaded.at(v), 16)
        scattered.wait(act, i, v - U)
        act.activation(rhs[:, b, :, F:F + H], weight[:, slots_of(i, v), :], ACT.Copy)
        act.activation(rhs[:, b, :, F + H:F + 2 * H], top[:, slots_of(i, v), :], ACT.Copy).then_inc(copied.at(v), 1)
        loaded.wait(pool, i, v)
        rows_ = rhs[:, b, :, 0:F].rearrange("p g (h c) -> p g h c", c=C)
        pool.tensor_tensor(rows_, rows_, weight[:, slots_of(i, v), :].unsqueeze(3).broadcast_to([P, G, H, C]),
                           ALU.mult).then_inc(weighted.at(v), 1)

    for v in range(AHEAD):
        one_hots(0, v, range(G))
        prepare(0, v)
    with K.turns() as i:
        blocks = turn_values(K, ET.DVE, pair_block, NB - 1, i, PAIRS)
        steps = turn_values(K, ET.PE, pair_step, AW, i, PAIRS)
        for v in range(U):
            for event in (made, copied, weighted):
                event.wait(pe, i, v)
            adder.added[-1].wait(pe, i, v - 2)
            for k in range(PAIRS):
                sums = psB(v, k)
                pe.matmul(sums[:, AW:2 * AW], zero[:, 0:P], zero[:, 0:AW], start=True, stop=False, skip_group_check=True)
                pe.matmul(sums[:, 0:AW], onehot[:, v, 2 * k, :], rhs[:, v, 2 * k, :], start=True, stop=False,
                          skip_group_check=True)
                last = pe.matmul(K.ps[:, (v % 2) * PAIRS + k, bass.ds(steps(v, k), AW)], onehot[:, v, 2 * k + 1, :],
                                 rhs[:, v, 2 * k + 1, :], start=False, stop=True, skip_group_check=True)
            last.then_inc(scattered.at(v), 1)
            prepare(i, v + AHEAD)
            for k in range(PAIRS):
                one_hots(i, v + AHEAD, [2 * k, 2 * k + 1])
                adder.emit(i, v, k, blocks(v, k))
    for v in range(AHEAD):
        sp.wait_ge(loaded.at(v), 16 * (TURNS + 1))


class Sheet:

    CUTS = [(NB * c // 4, NB * (c + 1) // 4) for c in range(4)]

    def __init__(self, K, name):
        self.K, self.s = K, K.relay(name)
        self.runs = [K.relay(f"{name}_run{c}") for c in range(len(self.CUTS))]

    def after(self, *engines):
        for r in [self.s] + self.runs:
            r.after(*engines)

    def step(self, engine, emit):
        self.after(engine)
        self.s.done(emit())

    def each(self, engine, emit, *operands, last=None):
        for (a, b), run in zip(self.CUTS, self.runs):
            e = last if last is not None and run is self.runs[-1] else engine
            self.s.after(e)
            run.step(e, lambda: emit(e, *(o[:, a:b] for o in operands)))

    def tt(self, out, a, b, op):
        self.each(self.K.dve, lambda e, o, x, y: e.tensor_tensor(o, x, y, op), out, a, b,
                  last=self.K.pool if op in (ALU.add, ALU.subtract, ALU.mult) else None)

    def ts(self, out, a, x, y, op0, op1=None):
        self.each(self.K.dve, lambda e, o, i: e.tensor_scalar(o, i, x, y, op0, op1) if op1 is not None
                  else e.tensor_scalar(o, i, x, None, op0), out, a)

    def stt(self, out, a, x, b, op0, op1):
        self.each(self.K.dve, lambda e, o, i, y: e.scalar_tensor_tensor(o, i, x, y, op0, op1), out, a, b)

    def sum(self, out, a):
        self.each(self.K.dve, lambda e, o, i: e.tensor_reduce(o, i, AX.X, ALU.add), out, a)

    def copy(self, out, a):
        self.each(self.K.dve, lambda e, o, i: e.tensor_copy(o, i), out, a)

    def act(self, out, a, func, **kw):
        self.each(self.K.act, lambda e, o, i: e.activation(o, i, func, **kw), out, a)

    def reciprocal(self, out, a):
        self.each(self.K.dve, lambda e, o, i: e.reciprocal(o, i), out, a)

    def center(self, x, small):
        self.sum(small, x)
        self.ts(small, small, 1.0 / F, None, ALU.mult)
        self.tt(x, x, wide(small), ALU.subtract)

    def scale_rows(self, x, tmp, small, g=None, b=None):
        self.act(tmp, x, ACT.Square)
        self.sum(small, tmp)
        self.ts(small, small, 1.0 / F, EPS, ALU.mult, ALU.add)
        self.act(small, small, ACT.Sqrt)
        self.reciprocal(small, small)
        self.tt(x, x, wide(small), ALU.mult)
        if g is not None:
            self.tt(x, x, by_column(g), ALU.mult)
            self.tt(x, x, by_column(b), ALU.add)

    def layernorm(self, x, tmp, small, g=None, b=None):
        self.center(x, small)
        self.scale_rows(x, tmp, small, g, b)


def wide(small):
    return small.unsqueeze(2).broadcast_to([P, NB, F])


def by_column(vector):
    return vector.unsqueeze(1).broadcast_to([P, NB, F])


def heads(x):
    return x.unsqueeze(3).broadcast_to([P, NB, H, C])


def attention_out(K, layer, D):
    dve, act, sp, pe, pool = K.dve, K.act, K.sp, K.pe, K.pool
    S, d = Sheet(K, f"attend{layer}"), K.dmas(f"attend{layer}_dma")
    acc = K.acc
    xs, out = table(K.RA, F), table(K.RL, F)
    res, tmp = table(K.RA, F, NB * F), table(K.RL, F, NB * F)
    small = K.RF[:, NB * AW:NB * AW + 6 * NB * H].rearrange("p (k b h) -> p k b h", k=6, h=H)
    self_logit, m_edge, m_all, w_edge, w_self, den = (small[:, k, :, :] for k in range(6))
    row = K.node_small[:, 0, :]
    if layer == 1:
        d.done(sp.dma_start(xs, rows(K.rows1)[:, :, F:2 * F]))
        d.done(sp.dma_start(res, rows(K.h0)))
        hs = K.hidden_total
        S.step(dve, lambda: dve.tensor_reduce(hs[:, 0:2], K.hidden_sums[:, :, :], AX.X, ALU.add))
        S.step(act, lambda: act.activation(hs[:, 2:3], K.b1rep[:, 0:1], ACT.Relu))
        S.step(dve, lambda: dve.tensor_scalar(hs[:, 2:3], hs[:, 2:3], -float(SLOTS * P - E) / CH, None, ALU.mult))
        S.step(dve, lambda: dve.tensor_scalar(hs[:, 3:4], hs[:, 0:1], hs[:, 1:2], None, ALU.add))
        S.step(dve, lambda: dve.tensor_scalar(hs[:, 3:4], hs[:, 3:4], hs[:, 2:3], hs[:, 2:3], ALU.add, ALU.add))
        S.step(dve, lambda: dve.tensor_scalar(hs[:, 3:4], hs[:, 3:4], 1.0 / E, None, ALU.mult))
        S.step(dve, lambda: dve.tensor_copy(K.hidden_mean[:, :], hs[:, 3:4].broadcast_to([P, P])))
        S.step(pe, lambda: pe.matmul(K.ps[:, 0, 0:2 * H], K.hidden_mean[:, :],
                                     K.Vrep[:, :, :].rearrange("p l h -> p (l h)"), start=True, stop=True))
        S.step(dve, lambda: dve.tensor_tensor(K.loop_edge[:, :, :], K.ps[:, 0, 0:2 * H].rearrange("p (l h) -> p l h", h=H),
                                              K.crow[:, :, :], ALU.add))
        S.copy(K.count[:, :], acc[:, :, AW - 1])
    else:
        d.done(sp.dma_start(xs, rows(K.rows2)[:, :, 0:F]))
        d.done(sp.dma_start(res, rows(K.h1)))
    S.tt(self_logit, K.a_node[:, :, 0:H], K.a_node[:, :, H:2 * H], ALU.add)
    S.tt(self_logit, self_logit, K.loop_edge[:, layer - 1, :].unsqueeze(1).broadcast_to([P, NB, H]), ALU.add)
    S.stt(self_logit, self_logit, SLOPE, self_logit, ALU.mult, ALU.max)
    none = K.node_small[:, 1, :]
    S.ts(none, K.count[:, :], 0.5, -BIG, ALU.is_lt, ALU.mult)
    S.tt(m_edge, acc[:, :, F + H:F + 2 * H], none.unsqueeze(2).broadcast_to([P, NB, H]), ALU.add)
    S.tt(m_all, m_edge, self_logit, ALU.max)
    S.tt(w_edge, m_edge, m_all, ALU.subtract)
    S.act(w_edge, w_edge, ACT.Exp)
    S.tt(w_self, self_logit, m_all, ALU.subtract)
    S.act(w_self, w_self, ACT.Exp)
    S.tt(den, acc[:, :, F:F + H], w_edge, ALU.mult)
    S.tt(den, den, w_self, ALU.add)
    S.ts(den, den, 1e-16, None, ALU.add)
    S.reciprocal(den, den)
    S.tt(w_edge, w_edge, den, ALU.mult)
    S.tt(w_self, w_self, den, ALU.mult)
    by_head = lambda t: t.rearrange("p b (h c) -> p b h c", c=C)
    S.tt(by_head(out), by_head(acc[:, :, 0:F]), heads(w_edge), ALU.mult)
    d.after(dve, pool)
    S.tt(by_head(xs), by_head(xs), heads(w_self), ALU.mult)
    S.tt(out, out, xs, ALU.add)
    if layer == 2:
        x = table(K.RF, F)
        S.step(pool, lambda: pool.memset(x[:, NB - 1, :], 0.0))
        S.after(sp)
        d.done(sp.dma_start(xs, rows(K.h0)))
        load_x(K, D, x, d)
    S.tt(out, out, by_column(K.vec[f"L0_gnn_bias{layer}"]), ALU.add)
    S.act(tmp, out, ACT.Relu, scale=-1.0)
    S.act(tmp, tmp, ACT.Exp, scale=-1.0)
    S.act(out, out, ACT.Relu)
    S.stt(out, tmp, -1.0, out, ALU.add, ALU.add)
    S.tt(out, out, res, ALU.add)
    S.layernorm(out, tmp, row, K.vec[f"L0_gnn_g{layer}"], K.vec[f"L0_gnn_bn{layer}"])
    K.barrier()
    if layer == 1:
        d.done(sp.dma_start(rows(K.h1), out))
        stage = table(K.RF, ROW2)

        def evacuate(b, ps):
            dve.tensor_copy(stage[:, b, :], ps[:, 0:ROW2])
            return dve.tensor_copy(K.a_node[:, b, :], ps[:, F:F + 2 * H])

        project(K, "second", [(out, K.W2[:, :])], F + 2 * H, evacuate)
        K.barrier()
        d.done(sp.dma_start(rows(K.rows2), stage))
        d.after(sp, pool)
        K.barrier()
        K.by_dst = table(K.RL, H)
        S.copy(K.by_dst, K.a_node[:, :, H:2 * H])
    d.after(sp)
    K.barrier()


def jump(K):
    dve, sp = K.dve, K.sp
    K.x1, K.prow = K.dram("x1", [NPAD, F]), K.dram("msg_rows", [NPAD, 3 * F], bf16)
    h0, h1 = table(K.RA, F), table(K.RA, F, NB * F)
    h2, x1 = table(K.RL, F), table(K.RL, F, NB * F)
    xin, tmp = table(K.RF, F), table(K.RF, F, NB * F)
    row = K.node_small[:, 0, :]
    S, d = Sheet(K, "jump"), K.dmas("jump_dma")
    project(K, "jk", [(h0, K.JK[:, 0, :]), (h1, K.JK[:, 1, :]), (h2, K.JK[:, 2, :])], F,
            lambda b, ps: dve.tensor_tensor(x1[:, b, :], ps, xin[:, b, :], ALU.add))
    K.barrier()
    S.tt(x1, x1, by_column(K.vec["L0_gnn_jk_b"]), ALU.add)
    S.layernorm(x1, tmp, row)
    K.barrier()
    d.done(sp.dma_start(rows(K.x1), x1))
    pt, qt = table(K.RA, F), table(K.RL, F)

    def evacuate(b, ps):
        dve.tensor_copy(pt[:, b, :], ps[:, 0:F])
        return dve.tensor_tensor(qt[:, b, :], ps[:, F:2 * F], K.vec["L1_gnn_msg_b"], ALU.add)

    project(K, "msg", [(x1, K.WM[:, 0:2, :].rearrange("p s o -> p (s o)"))], 2 * F, evacuate)
    K.barrier()
    parts = K.RF[:, 0:NB * 3 * F // 2].bitcast(bf16).rearrange("p (b k f) -> p b k f", k=3, f=F)
    for part in range(3):
        S.copy(parts[:, :, part, :], pt)
        if part < 2:
            S.tt(pt, pt, parts[:, :, part, :], ALU.subtract)
    S.after(sp)
    d.done(sp.dma_start(rows(K.prow), parts.rearrange("p b k f -> p b (k f)")))
    d.after(sp)
    K.by_dst = qt
    K.barrier()


def message_pass(K):
    pool, act, pe, dve = K.pool, K.act, K.pe, K.dve
    MW = F + 1
    K.acc = table(K.RF, MW)
    rowbuf, onehot, onehotW, onehotT, rhs = pieces(K.RA, 0, (3 * F, bf16), (P, bf16), (P, None), (P, None), (MW, None))
    (junk,) = pieces(K.RL, NB * F, (F, bf16))
    minus_beta, eps = K.RL[:, 9000:9000 + F], K.RL[:, 9200:9201]
    squares = K.RL[:, 9300:9300 + U * G].rearrange("p (u g) -> p u g", u=U)
    rstd = K.RL[:, 9400:9400 + U * G].rearrange("p (u g) -> p u g", u=U)
    psT = [K.ps[:, b, 0:G * P // 2].bitcast(bf16).rearrange("p (g e) -> p g e", g=G) for b in range(2)]
    psB = K.ps[:, 2:4, :].rearrange("p k (a w) -> p (k a) w", a=2)
    psH = [K.ps[:, 4 + b, :].rearrange("p (g e) -> p g e", g=G) for b in range(U)]
    summed, squared, rooted, inverted, scaled, ready, scattered = (
        Event(K, "message_" + x) for x in ("summed", "squared", "rooted", "inverted", "scaled", "ready", "scattered"))
    gather = Gather(K, "message", K.prow, rowbuf, [summed], 2)
    ones = OneHots(K, "message", onehot, onehotT, psT, summed, onehotW, scattered)
    adder = Adder(K, "message", K.acc, lambda v, j: psB[:, j, 0:MW], scattered, G)
    init = K.relay("message_init")
    init.done(dve.memset(K.acc, 0.0))
    init.done(dve.memset(rhs[:, :, :, F:MW], 1.0))
    init.done(dve.memset(eps, EPS))
    init.done(dve.tensor_scalar(minus_beta, K.vec["L1_gnn_msg_beta"], -1.0, None, ALU.mult))
    K.barrier()

    def sums(i, v, blocks):
        b = v % U
        gather.emit(i, v)
        ones.out.wait(pe, i, v)
        scaled.wait(pe, i, v - U)
        gather.arrived.wait(pe, i, v)
        for j in range(G):
            pe.matmul(psH[b][:, j, :], onehotT[:, b, j, :],
                      K.by_dst[:, bass.ds(blocks(v, j), 1), :].rearrange("p b w -> p (b w)"), start=True, stop=False)
            for part in range(3):
                last = pe.matmul(psH[b][:, j, :], K.ident_bf[:, :], rowbuf[:, b, j, part * F:(part + 1) * F],
                                 start=False, stop=part == 2)
        last.then_inc(summed.at(v), 1)
        summed.wait(act, i, v)
        scaled.wait(act, i, v - U)
        for j in range(G):
            last = act.activation(junk[:, b, j, :], psH[b][:, j, :], ACT.Square, accum_out=squares[:, b, j:j + 1])
        last.then_inc(squared.at(v), 1)
        squared.wait(act, i, v)
        act.activation(rstd[:, b, :], squares[:, b, :], ACT.Sqrt, bias=eps, scale=1.0 / F).then_inc(rooted.at(v), 1)

    def scales(i, v, between):
        b = v % U
        rooted.wait(dve, i, v)
        gather.pick(i, v + U)
        dve.reciprocal(rstd[:, b, :], rstd[:, b, :]).then_inc(inverted.at(v), 1)
        scattered.wait(dve, i, v - U)
        inverted.wait(dve, i, v)
        for j in range(G):
            last = dve.scalar_tensor_tensor(rhs[:, b, j, 0:F], psH[b][:, j, :], rstd[:, b, j:j + 1],
                                            K.vec["L1_gnn_msg_g"], ALU.mult, ALU.mult)
            if j == G - 1:
                last.then_inc(scaled.at(v), 1)
            between(j)
        scaled.wait(dve, i, v)
        dve.tensor_tensor(rhs[:, b, :, 0:F], rhs[:, b, :, 0:F], minus_beta.unsqueeze(1).broadcast_to([P, G, F]),
                          ALU.max).then_inc(ready.at(v), 1)

    for v in range(U):
        gather.pick(0, v)
    for v in range(U):
        ones.make(0, v)
        if v < AHEAD:
            ones.transpose(0, v)
            ones.weight(0, v)
    blocks_pe = turn_blocks(K, ET.PE, 0, 2)
    for v in (0, 1):
        sums(0, v, blocks_pe)
    scales(0, 0, lambda j: None)
    with K.turns() as i:
        blocks_pe, blocks_dve = turn_blocks(K, ET.PE, i, U + 2), turn_blocks(K, ET.DVE, i)
        for v in range(U):
            ones.make(i, v + U)
            ones.transpose(i, v + AHEAD)
            sums(i, v + 2, blocks_pe)
            ready.wait(pe, i, v)
            ones.weights_in.wait(pe, i, v)
            adder.added[-1].wait(pe, i, v - 1)
            for j in range(G):
                last = pe.matmul(psB[:, j, 0:MW], onehotW[:, v, j, :], rhs[:, v, j, :], start=True, stop=True)
            last.then_inc(scattered.at(v), 1)
            ones.weight(i, v + AHEAD)
            scales(i, v + 1, lambda j: adder.emit(i, v, j, blocks_dve(v, j)))
    for v in range(2):
        pool.wait_ge(gather.arrived.at(v), K.arrived_before[v])


def update(K, D, out):
    dve, sp, pe, pool = K.dve, K.sp, K.pe, K.pool
    acc = K.acc
    x1, msg = table(K.RA, F), table(K.RA, F, NB * F)
    new, tmp = table(K.RL, F), table(K.RL, F, NB * F)
    S, d = Sheet(K, "update"), K.dmas("update_dma")
    row, gate = K.node_small[:, 0, :], K.node_small[:, 1, :]
    d.done(sp.dma_start(x1, rows(K.x1)))
    S.tt(msg, by_column(K.vec["L1_gnn_msg_beta"]), wide(acc[:, :, F]), ALU.mult)
    S.tt(msg, msg, acc[:, :, 0:F], ALU.add)
    S.ts(row, K.count[:, :], 1e-8, None, ALU.add)
    S.reciprocal(row, row)
    S.ts(gate, K.count[:, :], 0.0, None, ALU.is_gt)
    S.tt(row, row, gate, ALU.mult)
    S.tt(msg, msg, wide(row), ALU.mult)
    d.after(dve, pe, pool)
    S.after(pe)
    project(K, "upd", [(x1, K.WM[:, 2, :]), (msg, K.WM[:, 3, :])], F,
            lambda b, ps: dve.tensor_tensor(new[:, b, :], ps, K.vec["L1_gnn_upd_b"], ALU.add))
    K.barrier()
    S.scale_rows(new, tmp, row, K.vec["L1_gnn_upd_g"], K.vec["L1_gnn_upd_beta"])
    S.ts(new, new, 0.0, None, ALU.max)
    S.tt(tmp, x1, by_column(K.vec["gate_w_row"]), ALU.mult)
    S.sum(gate, tmp)
    S.act(gate, gate, ACT.Sigmoid, bias=K.gate_b[:, 0:1])
    S.tt(new, new, wide(gate), ALU.mult)
    S.ts(gate, gate, -1.0, 1.0, ALU.mult, ALU.add)
    S.tt(tmp, x1, wide(gate), ALU.mult)
    S.tt(new, new, tmp, ALU.add)
    S.tt(new, new, x1, ALU.add)
    S.layernorm(new, tmp, row)
    S.after(sp)
    cut = (NB - 1) * P
    d.done(sp.dma_start(out[0:cut, :].rearrange("(b p) w -> p b w", p=P), new[:, 0:NB - 1, :]))
    d.done(sp.dma_start(out[cut:N, :], new[0:LAST, NB - 1, :]))
    d.after(sp)


def graph_layers(nc, D, out):
    with ExitStack() as ctx:
        K = Build(nc, ctx)
        K.RA, K.RL, K.RF = (K.sb("region_" + n, [P, REGION]) for n in "ALF")
        K.ps = ctx.enter_context(nc.psum_tensor("psum", [P, 8, 512], fp32))
        K.xT = K.sb("block_transposed", [P, 2, P])
        K.slot_index = K.sb("slot_index", [P, U, G], i32)
        K.dots = K.sb("dots", [P, U, G])
        K.node_small = K.sb("node_small", [P, 2, NB])
        K.count = K.sb("edge_count", [P, NB])
        K.hidden_sums = K.sb("hidden_sums", [P, 2, -(-KC // 4)])
        K.hidden_total = K.sb("hidden_total", [P, 4])
        K.hidden_mean = K.sb("hidden_mean", [P, P])
        K.loop_edge = K.sb("loop_edge", [P, 2, H])
        K.cols = K.sb("chunk_columns", [P, 8])
        K.rowbuf = K.RA[0:1, 10240:10240 + 7 * P].rearrange("a (k h c) -> a k h c", h=H, c=CH)
        K.rowbuf2 = K.RA[0:1, 11264:11264 + 4 * P].rearrange("a (k h c) -> a k h c", h=H, c=CH)
        K.rowflat = K.RA[0:1, 12288:12288 + P]
        K.penalty = K.RA[:, 0:-(-TC // 2)].bitcast(bf16)[:, 0:TC]
        K.spill = K.dram("xs_by_slot", [SLOTS // G + AHEAD, P, G * F])
        K.edge2 = K.dram("edge_alpha2", [P, TC])
        K.pen_dram, K.chain_dram = K.dram("run_starts", [P, TC], bf16), K.dram("chain_penalties", [1, 4 * P])
        K.credit = K.dram("credit", [U, P])

        def run(stage, *args):
            with K.phase():
                stage(K, *args)

        run(load_weights, D)
        run(place_edges, D)
        run(nodes_in, D)
        for layer in (1, 2):
            run(logits_pass, layer)
            if layer == 1:
                run(edge_features)
            run(logits, layer)
            run(breaks if layer == 1 else breaks_again)
            run(segment_softmax, layer)
            run(weighted_sum, layer)
            run(attention_out, layer, D)
        run(jump)
        run(message_pass)
        run(update, D, out)


def kernel(**inputs):
    import numpy as _np
    import concourse.bacc as _bacc
    from concourse import mybir as _mybir
    from concourse.bass_utils import run_bass_kernel_spmd as _run

    given = {k: _np.asarray(v) for k, v in inputs.items()}
    for k in ("L0_gnn_lin_w1", "L0_gnn_lin_w2", "L0_gnn_in_w", "L0_gnn_jk_w", "L0_gnn_enc_w1"):
        given[k + "_T"] = given[k].T
    given["gate_w_row"] = given["L1_gnn_gate_w"].reshape(-1)
    unused = ("L0_gnn_in_w", "L0_gnn_jk_w", "L0_gnn_enc_w1", "L1_gnn_gate_w")
    nc = _bacc.Bacc("TRN2", target_bir_lowering=False, num_devices=1)
    arrays, D = {}, {}
    for name, a in given.items():
        if name in unused:
            continue
        a = _np.ascontiguousarray(a)
        arrays["in_" + name] = a
        D[name] = nc.dram_tensor("in_" + name, a.shape, _mybir.dt.from_np(a.dtype), kind="ExternalInput").ap()
    out = nc.dram_tensor("out_0", (N, F), _mybir.dt.float32, kind="ExternalOutput").ap()
    graph_layers(nc, D, out)
    r = _run(nc, [arrays], core_ids=[0])
    return r.results[0]["out_0"]
```
